# Optimizing a Trainium2 kernel written in Bass

```python
import numpy as np
import jax
import jax.numpy as jnp

def _softmax(x, axis=-1):
    return jax.nn.softmax(x, axis=axis)

def _gelu(x):
    return jax.nn.gelu(x, approximate=True)

def _silu(x):
    return jax.nn.silu(x)

def _sigmoid(x):
    return jax.nn.sigmoid(x)

def _layernorm(x, axis=-1, eps=1e-05):
    m = jnp.mean(x, axis=axis, keepdims=True)
    v = jnp.var(x, axis=axis, keepdims=True)
    return (x - m) / jnp.sqrt(v + eps)

def _scatter_add(tgt, idx, src, axis=0):
    return tgt.at[idx].add(src)

def _segment_sum(src, seg, n):
    return jax.ops.segment_sum(src, seg, n)
kernel_name = 'mk_decoder_preln_d1_seqx_r4_8a57bb'

def setup_inputs(seed: int=0):
    np.random.seed(seed)
    _w = jnp.asarray

    def _rec_inputs():
        import jax
        import jax.numpy as jnp
        _rk = jax.random.key(seed)
        x = -0.000125 + 0.9999 * jax.random.normal(jax.random.fold_in(_rk, 1), (8, 100, 512), jnp.float32)
        _lenS = 100 - jax.random.randint(jax.random.fold_in(_rk, 7), (8,), 0, max(1, 100 // 4) + 1, jnp.int32)
        _lenS2 = 361 - jax.random.randint(jax.random.fold_in(_rk, 8), (8,), 0, max(1, 361 // 4) + 1, jnp.int32)
        _ctx_2048P = jax.random.normal(jax.random.fold_in(_rk, 11), (8, 16, 512), jnp.float32)
        _ctx_2048c = jax.random.dirichlet(jax.random.fold_in(_rk, 511), 0.3 * jnp.ones((16,), jnp.float32), (8, 361))
        _ctx_2048t = jnp.einsum('bsk,bkd->bsd', _ctx_2048c, _ctx_2048P)
        _ctx_2048t = _ctx_2048t * jax.lax.rsqrt(jnp.mean(jnp.square(_ctx_2048t)) + 1e-12) * 0.953939
        ctx_2048 = 4.13588e-05 + 0.999923 * (_ctx_2048t + 0.3 * jax.random.normal(jax.random.fold_in(_rk, 611), (8, 361, 512), jnp.float32))
        return (x, ctx_2048)
    x, ctx_2048 = _rec_inputs()

    def _L0_attn_setup():
        import jax, jax.numpy as jnp
        import numpy as np
        import math
        D_MODEL = 512
        NUM_HEADS = 16
        HEAD_DIM = D_MODEL // NUM_HEADS
        key = jax.random.key(seed)
        k_x, k_wqkv, k_bqkv, k_wo, k_bo = jax.random.split(key, 5)
        B, S = (2, 512)
        scale = 1.0 / math.sqrt(D_MODEL)
        return {'x': jax.random.normal(k_x, (B, S, D_MODEL), dtype=jnp.float32), 'w_qkv': jax.random.normal(k_wqkv, (3 * D_MODEL, D_MODEL), dtype=jnp.float32) * scale, 'b_qkv': jax.random.normal(k_bqkv, (3 * D_MODEL,), dtype=jnp.float32) * 0.01, 'w_out': jax.random.normal(k_wo, (D_MODEL, D_MODEL), dtype=jnp.float32) * scale, 'b_out': jax.random.normal(k_bo, (D_MODEL,), dtype=jnp.float32) * 0.01}
    _L0_attn_all = _L0_attn_setup()
    _L0_attn_in = {k: v for k, v in _L0_attn_all.items() if k in ('w_qkv', 'b_qkv', 'w_out', 'b_out')}
    del _L0_attn_all

    def _L0_xattn_setup():
        import jax, jax.numpy as jnp
        import numpy as np
        D_MODEL = 512
        NUM_HEADS = 16
        HEAD_DIM = D_MODEL // NUM_HEADS
        key = jax.random.key(seed)
        ks = jax.random.split(key, 10)
        B, S, T = (4, 1024, 256)
        s = 1.0 / np.sqrt(D_MODEL)
        inp = {'query': jax.random.normal(ks[0], (B, S, D_MODEL), jnp.float32), 'key_value': jax.random.normal(ks[1], (B, T, D_MODEL), jnp.float32), 'Wq': jax.random.normal(ks[2], (D_MODEL, D_MODEL), jnp.float32) * s, 'bq': jnp.zeros((D_MODEL,), jnp.float32), 'Wk': jax.random.normal(ks[3], (D_MODEL, D_MODEL), jnp.float32) * s, 'bk': jnp.zeros((D_MODEL,), jnp.float32), 'Wv': jax.random.normal(ks[4], (D_MODEL, D_MODEL), jnp.float32) * s, 'bv': jnp.zeros((D_MODEL,), jnp.float32), 'Wo': jax.random.normal(ks[5], (D_MODEL, D_MODEL), jnp.float32) * s, 'bo': jnp.zeros((D_MODEL,), jnp.float32)}
        return inp
    _L0_xattn_all = _L0_xattn_setup()
    _L0_xattn_in = {k: v for k, v in _L0_xattn_all.items() if k in ('Wq', 'bq', 'Wk', 'bk', 'Wv', 'bv', 'Wo', 'bo')}
    del _L0_xattn_all

    def _L0_ffn_setup():
        import jax, jax.numpy as jnp
        import numpy as np
        TOPK = 2
        key = jax.random.key(seed)
        ks = jax.random.split(key, 10)
        B, S, D = (2, 512, 512)
        E, I = (8, 256)
        ISH = 1 * I
        std = 0.02
        x = jax.random.normal(ks[0], (B, S, D), jnp.float32)
        gate_w = jax.random.normal(ks[1], (E, D), jnp.float32) * std
        gate_b = jnp.zeros((E,), jnp.float32)
        W1 = jax.random.normal(ks[2], (E, I, D), jnp.float32) * std
        W2 = jax.random.normal(ks[3], (E, D, I), jnp.float32) * std
        W3 = jax.random.normal(ks[4], (E, I, D), jnp.float32) * std
        Ws1 = jax.random.normal(ks[5], (ISH, D), jnp.float32) * std
        Ws2 = jax.random.normal(ks[6], (D, ISH), jnp.float32) * std
        Ws3 = jax.random.normal(ks[7], (ISH, D), jnp.float32) * std
        return {'x': x, 'gate_w': gate_w, 'gate_b': gate_b, 'W1': W1, 'W2': W2, 'W3': W3, 'Ws1': Ws1, 'Ws2': Ws2, 'Ws3': Ws3}
    _L0_ffn_all = _L0_ffn_setup()
    _L0_ffn_in = {k: v for k, v in _L0_ffn_all.items() if k in ('gate_w', 'gate_b', 'W1', 'W2', 'W3', 'Ws1', 'Ws2', 'Ws3')}
    del _L0_ffn_all
    return {'x': x, 'ctx_2048': ctx_2048, 'L0_attn_w_qkv': _L0_attn_in['w_qkv'], 'L0_attn_b_qkv': _L0_attn_in['b_qkv'], 'L0_attn_w_out': _L0_attn_in['w_out'], 'L0_attn_b_out': _L0_attn_in['b_out'], 'L0_xattn_Wq': _L0_xattn_in['Wq'], 'L0_xattn_bq': _L0_xattn_in['bq'], 'L0_xattn_Wk': _L0_xattn_in['Wk'], 'L0_xattn_bk': _L0_xattn_in['bk'], 'L0_xattn_Wv': _L0_xattn_in['Wv'], 'L0_xattn_bv': _L0_xattn_in['bv'], 'L0_xattn_Wo': _L0_xattn_in['Wo'], 'L0_xattn_bo': _L0_xattn_in['bo'], 'L0_ffn_gate_w': _L0_ffn_in['gate_w'], 'L0_ffn_gate_b': _L0_ffn_in['gate_b'], 'L0_ffn_W1': _L0_ffn_in['W1'], 'L0_ffn_W2': _L0_ffn_in['W2'], 'L0_ffn_W3': _L0_ffn_in['W3'], 'L0_ffn_Ws1': _L0_ffn_in['Ws1'], 'L0_ffn_Ws2': _L0_ffn_in['Ws2'], 'L0_ffn_Ws3': _L0_ffn_in['Ws3']}

def reference(x, ctx_2048, L0_attn_w_qkv, L0_attn_b_qkv, L0_attn_w_out, L0_attn_b_out, L0_xattn_Wq, L0_xattn_bq, L0_xattn_Wk, L0_xattn_bk, L0_xattn_Wv, L0_xattn_bv, L0_xattn_Wo, L0_xattn_bo, L0_ffn_gate_w, L0_ffn_gate_b, L0_ffn_W1, L0_ffn_W2, L0_ffn_W3, L0_ffn_Ws1, L0_ffn_Ws2, L0_ffn_Ws3):
    import jax
    import jax.numpy as jnp

    def _L0_attn_ref(x, w_qkv, b_qkv, w_out, b_out):
        import jax, jax.numpy as jnp
        import numpy as np
        import math
        D_MODEL = 512
        NUM_HEADS = 16
        HEAD_DIM = D_MODEL // NUM_HEADS
        B, S, D = x.shape
        H, Hd = (NUM_HEADS, HEAD_DIM)
        qkv = jnp.einsum('bsd,ed->bse', x, w_qkv) + b_qkv
        qkv = qkv.reshape(B, S, 3, H, Hd)
        q = jnp.transpose(qkv[:, :, 0], (0, 2, 1, 3))
        k = jnp.transpose(qkv[:, :, 1], (0, 2, 1, 3))
        v = jnp.transpose(qkv[:, :, 2], (0, 2, 1, 3))
        scores = jnp.einsum('bhqd,bhkd->bhqk', q, k) / math.sqrt(Hd)
        causal = jnp.triu(jnp.full((S, S), -jnp.inf, dtype=scores.dtype), k=1)
        scores = scores + causal[None, None]
        attn = jax.nn.softmax(scores, axis=-1)
        out = jnp.einsum('bhqk,bhkd->bhqd', attn, v)
        out = jnp.transpose(out, (0, 2, 1, 3)).reshape(B, S, D)
        return jnp.einsum('bsd,ed->bse', out, w_out) + b_out

    def _L0_xattn_ref(query, key_value, Wq, bq, Wk, bk, Wv, bv, Wo, bo):
        import jax, jax.numpy as jnp
        import numpy as np
        D_MODEL = 512
        NUM_HEADS = 16
        HEAD_DIM = D_MODEL // NUM_HEADS
        B, S, _ = query.shape
        T = key_value.shape[1]
        Q = query @ Wq.T + bq
        K = key_value @ Wk.T + bk
        V = key_value @ Wv.T + bv
        Q = Q.reshape(B, S, NUM_HEADS, HEAD_DIM).transpose(0, 2, 1, 3)
        K = K.reshape(B, T, NUM_HEADS, HEAD_DIM).transpose(0, 2, 1, 3)
        V = V.reshape(B, T, NUM_HEADS, HEAD_DIM).transpose(0, 2, 1, 3)
        scale = 1.0 / np.sqrt(HEAD_DIM).astype(np.float32)
        scores = jnp.einsum('bhsd,bhtd->bhst', Q, K) * scale
        attn = jax.nn.softmax(scores, axis=-1)
        ctx = jnp.einsum('bhst,bhtd->bhsd', attn, V)
        ctx = ctx.transpose(0, 2, 1, 3).reshape(B, S, D_MODEL)
        return ctx @ Wo.T + bo

    def _L0_ffn_ref(x, gate_w, gate_b, W1, W2, W3, Ws1, Ws2, Ws3):
        import jax, jax.numpy as jnp
        import numpy as np
        TOPK = 2
        B, S, D = x.shape
        xt = x.reshape(-1, D)
        T = xt.shape[0]
        E = gate_w.shape[0]
        logits = xt @ gate_w.T
        scores = jax.nn.softmax(logits.astype(jnp.float32), axis=-1)
        biased = scores + gate_b
        _, idx = jax.lax.top_k(biased, TOPK)
        weights = jnp.take_along_axis(scores, idx, axis=1).astype(x.dtype)
        dw = jnp.zeros((T, E), x.dtype).at[jnp.arange(T)[:, None], idx].add(weights)
        h = jax.nn.silu(jnp.einsum('td,eid->tei', xt, W1)) * jnp.einsum('td,eid->tei', xt, W3)
        y = jnp.einsum('tei,edi,te->td', h, W2, dw)
        z = jax.nn.silu(xt @ Ws1.T) * (xt @ Ws3.T) @ Ws2.T
        return (y + z).reshape(B, S, D)
    x = x + _L0_attn_ref(_layernorm(x, axis=-1), L0_attn_w_qkv, L0_attn_b_qkv, L0_attn_w_out, L0_attn_b_out)
    x = x + _L0_xattn_ref(_layernorm(x, axis=-1), ctx_2048, L0_xattn_Wq, L0_xattn_bq, L0_xattn_Wk, L0_xattn_bk, L0_xattn_Wv, L0_xattn_bv, L0_xattn_Wo, L0_xattn_bo)
    x = x + _L0_ffn_ref(_layernorm(x, axis=-1), L0_ffn_gate_w, L0_ffn_gate_b, L0_ffn_W1, L0_ffn_W2, L0_ffn_W3, L0_ffn_Ws1, L0_ffn_Ws2, L0_ffn_Ws3)
    return x

_drawn_inputs = setup_inputs


def setup_inputs(seed=0):
    import zlib

    import numpy as np

    out = dict(_drawn_inputs(seed))
    spreads = {'L0_xattn_bq': (0.0, 0.461),
     'L0_xattn_bk': (0.0, 2.0),
     'L0_xattn_bv': (0.0, 0.1),
     'L0_xattn_bo': (0.0, 0.1),
     'L0_ffn_gate_b': (0.0, 0.8)}
    factors = {'L0_attn_b_qkv': 6.296,
     'L0_attn_b_out': 6.828,
     'L0_ffn_gate_w': 8.0,
     'L0_ffn_W1': 7.985,
     'L0_ffn_W2': 7.792,
     'L0_ffn_W3': 7.711,
     'L0_ffn_Ws1': 8.0,
     'L0_ffn_Ws2': 8.0,
     'L0_ffn_Ws3': 8.0}
    for name, (base, spread) in spreads.items():
        noise = np.random.default_rng([zlib.crc32(name.encode()), seed]).standard_normal(out[name].shape)
        drawn = base * np.exp(spread * noise) if base else spread * noise
        out[name] = jnp.asarray(drawn.astype(out[name].dtype))
    for name, factor in factors.items():
        out[name] = (out[name] * factor).astype(out[name].dtype)
    return out
```

```python
import concourse.bass as bass
from concourse import mybir
from contextlib import ExitStack


def decoder_layer(nc, x_d, ctx_d, wqk_d, wv_d, wout_d, bqk_d, bv_d, bout_d,
                  xwq_d, xwk_d, xwv_d, xwo_d, xbq_d, xbk_d, xbv_d, xbo_d,
                  gw_d, gb_d, iota_d, w13_d, w2_d, out_d):
    F32 = mybir.dt.float32
    F32R = mybir.dt.float32r
    U32 = mybir.dt.uint32
    ALU = mybir.AluOpType
    ACT = mybir.ActivationFunctionType
    AX = mybir.AxisListType

    B, T, D = 8, 100, 512
    S = 361
    SP = S + 1
    KD = D // 128
    NG = 4
    HD = 32
    NE = 8
    FI = 256
    NF = NE + 1
    SCALE = float(HD) ** -0.5
    MASKED = -1.0e30
    EPS = 1e-5
    KEYS = [128, 128, S - 256]
    NSELF = B * NG
    PASSES = ((0, 0), (1, 0), (0, 1))

    ctx = ExitStack()
    with ctx:
        cursor = [(nc.sbuf_base + 31) // 32 * 32]

        def at(name, shape, dt, offset):
            return nc.alloc_sbuf_tensor_at(name, shape, dt, offset=offset)

        def size(shape):
            n = 4
            for s in shape[1:]:
                n *= s
            return (n + 31) // 32 * 32

        def sb(name, shape, dt=F32):
            t = at(name, shape, dt, cursor[0])
            cursor[0] += size(shape)
            return t

        def sem(name):
            return ctx.enter_context(nc.semaphore(name))

        x = sb("x_res", [T, B, D])
        v = [sb(f"v_{h}", [128, 2, 3, D], F32R) for h in ("hi", "lo")]
        probs_at = cursor[0]
        P = sb("probs", [T, 4, SP])
        PT = [sb(f"probsT_{h}", [128, 3, 4 * T], F32R) for h in ("hi", "lo")]
        oT = sb("oT", [128, NG, T])
        oTs = [sb(f"oT_{h}", [128, NG, T], F32R) for h in ("hi", "lo")]
        nat = [sb(f"nat_{h}", [128, 8, 2 * T], F32R) for h in ("hi", "lo")]
        xnT = [sb(f"xnT_{h}", [128, KD, 2 * T], F32R) for h in ("hi", "lo")]
        g_end = cursor[0]
        xn = sb("xn", [T, 2, D])
        stage = sb("stage", [128, 2, 1024])
        bout = sb("bout_bc", [T, D])
        xbo = sb("xbo_bc", [T, D])
        ident = sb("ident", [128, 128])
        identr = sb("identr", [T, T], F32R)
        maskf = at("maskf", [T, 4, T], F32, probs_at)
        maskr = sb("maskr", [T, 4, T], F32R)
        bqk = sb("bqk", [128, 8])
        bv = sb("bv", [128, 4])
        xbq = sb("xbq", [128, 4])
        xbk = sb("xbk", [128, 4])
        xbv = sb("xbv", [128, 4])
        st = sb("bnst", [T, B, 6])
        mv = sb("meanvar", [T, B, 2])
        ve = sb("vareps", [T, B])
        sd = sb("sdev", [T, B])
        r0 = sb("rstd0", [T, B])
        t1 = sb("newt1", [T, B])
        t2 = sb("newt2", [T, B])
        t3 = sb("newt3", [T, B])
        rstd = sb("rstd", [T, B])
        mx = sb("rowmax", [T, 4])
        nb = sb("negmax", [T, 4])
        rs = sb("rowsum", [T, 2, 4])
        rr = sb("rowrec", [T, 4])
        common_end = cursor[0]

        wqk = [sb(f"wqk_{h}", [128, 8, KD, 128], F32R) for h in ("hi", "lo")]
        wv = [sb(f"wv_{h}", [128, KD, D], F32R) for h in ("hi", "lo")]
        wout = [sb(f"wout_{h}", [128, KD, D], F32R) for h in ("hi", "lo")]
        packs_at = cursor[0]
        pq, pk = [], []
        for par in range(2):
            pq.append(sb(f"pq{par}", [96, 4, 4, 2 * T], F32R))
            pk.append(sb(f"pk{par}", [96, 4, 4, 2 * T], F32R))
        araw = at("araw", [128, 8, 1024], F32, packs_at)
        self_end = cursor[0]

        a_wqk = common_end
        a_wv = a_wqk + 2 * 16384
        a_wout = a_wv + 2 * 8192
        xwk = [at(f"xwk_{i}", [128, 4, KD, 128], F32R, a_wqk + 8192 * i) for i in range(2)]
        xwq = [at(f"xwq_{i}", [128, 4, KD, 128], F32R, a_wqk + 16384 + 8192 * i) for i in range(2)]
        xwv = [at(f"xwv_{i}", [128, KD, D], F32R, a_wv + 8192 * i) for i in range(2)]
        xwo = [at(f"xwo_{i}", [128, KD, D], F32R, a_wout + 8192 * i) for i in range(2)]
        knat = [at(f"knat_{i}", [128, 2, 2, SP], F32R, a_wqk + 16384 + 5792 * i) for i in range(2)]
        cx = [at(f"cx_{i}", [128, 2, KD, SP], F32R, packs_at + 11584 * i) for i in range(2)]
        kp = at("kp", [96, 4, 4, SP], F32R, packs_at + 2 * 11584)
        qp = at("qp", [96, 2, 4, 4, T], F32R, packs_at + 2 * 11584 + 23168)
        assert 2 * 11584 + 23168 + 12800 + packs_at <= nc.sbuf_usable_end

        f_at = [common_end]

        def fb(name, shape, dt=F32):
            t = at(name, shape, dt, f_at[0])
            f_at[0] += size(shape)
            return t
        fx = [fb(f"fx_{h}", [128, KD, B * T], F32R) for h in ("hi", "lo")]
        fw13 = [[fb(f"fw13_{s}{h}", [128, KD, 2, FI], F32R) for h in ("hi", "lo")] for s in range(2)]
        fw2 = [[fb(f"fw2_{s}{h}", [128, 2, D], F32R) for h in ("hi", "lo")] for s in range(2)]
        g_at = [(nc.sbuf_base + 31) // 32 * 32 + size([T, B, D])]

        def gb_(name, shape, dt=F32):
            t = at(name, shape, dt, g_at[0])
            g_at[0] += size(shape)
            assert g_at[0] <= g_end
            return t
        hT = [[gb_(f"hT_{s}{h}", [128, 2, B * T], F32R) for h in ("hi", "lo")] for s in range(2)]
        sg = gb_("silu", [128, 2, 4 * T])
        hf = gb_("hf", [128, 2, 4 * T])
        gw = fb("gw_raw", [128, KD, NE])
        gwr = [fb(f"gw_{h}", [128, KD, NE], F32R) for h in ("hi", "lo")]
        gbias = fb("gate_bias", [T, NE])
        iota = fb("iota", [T, NE])
        lg = fb("logits", [T, B, NE])
        sc = fb("gscores", [T, B, NE])
        bi = fb("biased", [T, B, NE])
        top = fb("top8", [T, B, 8])
        tix = fb("top8ix", [T, B, 8], U32)
        tixf = fb("top8ixf", [T, B, 8])
        m0 = fb("mask0", [T, B, NE])
        m1 = fb("mask1", [T, B, NE])
        dw = fb("dweights", [T, B, NE])
        gmx = fb("gmax", [T, B])
        gsm = fb("gsum", [T, B])
        grc = fb("grec", [T, B])
        fstage = fb("fstage", [128, 2, 3072])

        scores4 = ctx.enter_context(nc.psum_tensor("scores4", [128, 4, 512], F32))
        more = [ctx.enter_context(nc.psum_tensor(f"bank{i}", [128, 512], F32)) for i in range(4, 8)]
        bank = [scores4[:, i, :] for i in range(4)] + [m[:, :] for m in more]
        J3 = [2, 3, 7]

        qs_d = [nc.dram_tensor(f"q_scratch_{h}", [128, B, 4, T], F32, kind="Internal").ap() for h in ("hi", "lo")]

        x_in = sem("x_in")
        const_in = sem("const_in")
        gate_in = sem("gate_in")
        araw_in = [sem(f"araw_in{i}") for i in range(8)]
        stage_in = [sem(f"stage_in{i}") for i in range(2)]
        pool_step = sem("pool_step")
        ident_ok = sem("ident_ok")
        split_hi = sem("split_hi")
        split_lo = sem("split_lo")
        consts_ok = sem("consts_ok")
        var_ok = sem("var_ok")
        sdev_ok = sem("sdev_ok")
        xn_ok = sem("xn_ok")
        dve_step = sem("dve_step")
        bias_added = sem("bias_added")
        unit_mm = sem("unit_mm")
        unit_hi = sem("unit_hi")
        unit_out = sem("unit_out")
        scores_ok = sem("scores_ok")
        negmax_ok = sem("negmax_ok")
        exp_ok = sem("exp_ok")
        probs_ok = sem("probs_ok")
        tp_ok = sem("tp_ok")
        pt_hi = sem("pt_hi")
        pt_lo = sem("pt_lo")
        pv_ok = sem("pv_ok")
        o_out = sem("o_out")
        o_split = sem("o_split")
        packed = [sem(f"packed{i}") for i in range(2)]
        kpacked = [sem(f"kpacked{i}") for i in range(2)]
        q_stored = [sem(f"q_stored{i}") for i in range(2)]
        q_loaded = [sem(f"q_loaded{i}") for i in range(2)]
        late_split = sem("late_split")
        fw_in = [sem(f"fw_in{i}") for i in range(2)]
        fw_split = sem("fw_split")
        router_mm = sem("router_mm")
        gexp = sem("gexp")
        dw_ok = sem("dw_ok")
        up_mm = sem("up_mm")
        silu_ok = sem("silu_ok")
        h_ok = sem("h_ok")
        h_hi = sem("h_hi")
        h_lo = sem("h_lo")
        down_mm = sem("down_mm")
        down_out = sem("down_out")
        stored = sem("stored")

        QP = B // 2
        units, unit_at = [], {}

        def add(*us):
            for u in us:
                unit_at[u] = len(units)
                units.append(u)
            return list(us)

        prologue = add(("X", 0, 0), ("X", 0, 1), *[("QK", 0, m) for m in range(8)], ("V", 0, 0), ("V", 0, 1),
                       ("X", 1, 0), ("X", 1, 1))
        self_slots = []
        for n in range(NSELF + 1):
            p, k = divmod(n, 8)
            q = p + 1
            a, b = [], []
            if q < QP:
                a = {0: [("QK", q, 0)], 1: [("QK", q, 2)], 2: [("QK", q, 3)], 3: [("QK", q, 5)],
                     4: [("QK", q, 7)], 5: [("V", q, 1)]}.get(k, [])
                b = {0: [("QK", q, 1)], 2: [("QK", q, 4)], 3: [("QK", q, 6)], 4: [("V", q, 0)]}.get(k, [])
            if q + 1 < QP:
                a = a + {6: [("X", q + 1, 0)], 7: [("X", q + 1, 1)]}.get(k, [])
            if k == 1 and p > 0:
                b = b + [("O", 2 * p - 1, 0)]
            if k == 5:
                b = b + [("O", 2 * p, 0)]
            self_slots.append((add(*a), add(*b)))
        boundary = add(("O", B - 1, 0))
        for p in range(QP):
            boundary += add(("X2", p, 0), ("X2", p, 1), *[("Q", p, m) for m in range(4)])
        boundary += add(*[("K", 0, g) for g in range(4)], *[("XV", 0, c) for c in range(3)])
        cross_slots = []
        for n in range(NSELF + 1):
            b, g = divmod(n, 4)
            a, bb = [], []
            if b + 1 < B:
                a = [("K", b + 1, g)]
                if g < 3:
                    bb = [("XV", b + 1, g)]
            if g == 3 and b > 0:
                bb = bb + [("XO", b - 1, 0)]
            cross_slots.append((add(*a), add(*bb)))
        last_o = add(("XO", B - 1, 0))
        ffn_x = add(*[("X3", b, 0) for b in range(B)])

        first_cross = unit_at[("K", 1, 0)]
        ubank, prev_user, seen = [], [], {}
        for i, u in enumerate(units):
            if i < first_cross:
                k = J3[i % 3]
            else:
                k = 7
            prev_user.append(seen.get(k))
            seen[k] = i
            ubank.append(k)
        for i in (2, 3):
            assert max(j for j in range(first_cross) if ubank[j] == i) < first_cross
        hi_units = [u for u in units if u[0] not in ("O", "XO")]
        hi_at = {u: i for i, u in enumerate(hi_units)}
        x_units = [u for u in units if u[0] in ("X", "X2", "X3")]
        xn_at = {u: i for i, u in enumerate(x_units)}

        def unit_row(u):
            return u[1] if u[0] == "X3" else 2 * u[1] + u[2]

        pieces, piece_at = [], {}

        def piece(key, src, cols, hi, lo, waits):
            piece_at[key] = len(pieces)
            pieces.append((src, cols, hi, lo, waits))

        def flat(t):
            return t

        qk_free = ("unit", unit_at[("QK", QP - 1, 7)])
        v_free = ("unit", unit_at[("V", QP - 1, 1)])
        for i in range(2):
            piece(("wk", i), xwk_d[:, 1024 * i:1024 * (i + 1)], 1024, xwk[0][:, 2 * i:2 * i + 2, :, :],
                  xwk[1][:, 2 * i:2 * i + 2, :, :], qk_free)
        for i in range(2):
            piece(("wq", i), xwq_d[:, 1024 * i:1024 * (i + 1)], 1024, xwq[0][:, 2 * i:2 * i + 2, :, :],
                  xwq[1][:, 2 * i:2 * i + 2, :, :], qk_free)
        for i in range(2):
            piece(("wv", i), xwv_d[:, 1024 * i:1024 * (i + 1)], 1024, xwv[0][:, 2 * i:2 * i + 2, :],
                  xwv[1][:, 2 * i:2 * i + 2, :], v_free)

        def ctx_piece(b):
            for i in range(2):
                w = ("scores", 24) if b < 2 else ("unit", max(unit_at[("K", b - 2, 3)], unit_at[("XV", b - 2, 2)]))
                piece(("cx", b, i), ctx_d[b, :, 2 * SP * i:2 * SP * (i + 1)], 2 * SP,
                      cx[0][:, b % 2, 2 * i:2 * i + 2, :], cx[1][:, b % 2, 2 * i:2 * i + 2, :], w)
        ctx_piece(0)
        for i in range(2):
            piece(("wo", i), xwo_d[:, 1024 * i:1024 * (i + 1)], 1024, xwo[0][:, 2 * i:2 * i + 2, :],
                  xwo[1][:, 2 * i:2 * i + 2, :], ("unit", unit_at[("O", B - 1, 0)]))
        for b in range(1, B):
            ctx_piece(b)

        def chunk(n, c=0):
            return n if n < NSELF else NSELF + 3 * (n - NSELF) + c

        def nchunks(n):
            return 1 if n < NSELF else 3

        def vslot(n):
            if n < NSELF:
                b = n // NG
                return (b // 2) % 2, b % 2
            return ((n - NSELF) // NG) % 2, 0

        def unit_io(u):
            kind, a, b = u
            bk = bank[ubank[unit_at[u]]]
            if kind in ("X", "X2"):
                return (bk[:, 0:4 * T].rearrange("p (k t) -> p k t", k=KD),
                        [y[:, :, T * b:T * (b + 1)] for y in xnT], None)
            if kind == "X3":
                return (bk[:, 0:4 * T].rearrange("p (k t) -> p k t", k=KD),
                        [y[:, :, T * a:T * (a + 1)] for y in fx], None)
            if kind == "QK":
                return bk[:, 0:2 * T], [y[:, b, :] for y in nat], bqk[:, b:b + 1]
            if kind == "Q":
                return bk[:, 0:2 * T], [y[:, 4 * (a % 2) + b, :] for y in nat], xbq[:, b:b + 1]
            if kind == "K":
                return bk[:, 0:SP], [y[:, b // 2, b % 2, :] for y in knat], xbk[:, b:b + 1]
            if kind == "V":
                return bk[0:T, :], [y[0:T, a % 2, b, :] for y in v], None
            if kind == "XV":
                return bk[0:KEYS[b], :], [y[0:KEYS[b], a % 2, b, :] for y in v], None

        def score_ap(n):
            if n < NSELF:
                return bank[n % 2][0:T, 0:4 * T].rearrange("p (j t) -> p j t", j=4)
            return scores4[0:T, :, 0:S]

        def whole(i):
            raw = araw[:, i, :]
            if i < 4:
                return (raw.rearrange("p (a b c) -> p a b c", a=2, b=KD), [w[:, 2 * i:2 * i + 2, :, :] for w in wqk])
            w = wv if i < 6 else wout
            return raw.rearrange("p (a b) -> p a b", a=2), [y[:, 2 * (i % 2):2 * (i % 2) + 2, :] for y in w]

        block = ctx.enter_context(nc.Block())

        @block.sync
        def _(sp):
            sp.dma_start(x[:, :, :], x_d.rearrange("b t d -> t b d")).then_inc(x_in, 16)
            for i in range(4):
                sp.dma_start(araw[:, i, :], wqk_d[:, 1024 * i:1024 * (i + 1)]).then_inc(araw_in[i], 16)
            for i in range(2):
                sp.dma_start(araw[:, 4 + i, :], wv_d[:, 1024 * i:1024 * (i + 1)]).then_inc(araw_in[4 + i], 16)
            for i in range(2):
                sp.dma_start(araw[:, 6 + i, :], wout_d[:, 1024 * i:1024 * (i + 1)]).then_inc(araw_in[6 + i], 16)

            sp.wait_ge(split_lo, 8)
            for p in range(QP):
                if p >= 2:
                    sp.wait_ge(scores_ok, 8 * (p - 1))
                for dst, half, m0_ in ((pq[p % 2], (0, 1, 0), 0), (pk[p % 2], (0, 0, 1), 4)):
                    sp.wait_ge(unit_out, unit_at[("QK", p, m0_ + 3)] + 1)
                    for r in range(3):
                        for j in range(4):
                            sp.dma_start(dst[32 * r:32 * r + 32, j, :, :].bitcast(F32),
                                         nat[half[r]][32 * j:32 * j + 32, m0_:m0_ + 4, :].bitcast(F32)).then_inc(packed[p % 2], 16)
            for p in range(QP):
                sp.wait_ge(unit_out, unit_at[("Q", p, 3)] + 1)
                for i in range(2):
                    for h in range(2):
                        sp.dma_start(qs_d[h][:, 2 * p + i, :, :],
                                     nat[h][:, 4 * (p % 2):4 * (p % 2) + 4, T * i:T * (i + 1)].bitcast(F32)).then_inc(q_stored[p % 2], 16)

            def load_q(b):
                for r, h in enumerate((0, 1, 0)):
                    sp.dma_start(qp[32 * r:32 * r + 32, b % 2, :, :, :].rearrange("p j m t -> p j (m t)").bitcast(F32),
                                 qs_d[h][:, b, :, :].rearrange("(j d) m t -> d j (m t)", d=32)).then_inc(q_loaded[b % 2], 16)
            for par in range(2):
                sp.wait_ge(q_stored[par], 16 * 4 * QP // 2)
            sp.wait_ge(scores_ok, NSELF)
            load_q(0)
            for b in range(B):
                for h in range(2):
                    sp.wait_ge(unit_out, unit_at[("K", b, 2 * h + 1)] + 1)
                    if b > 0:
                        sp.wait_ge(scores_ok, NSELF + 4 * (b - 1) + 2 * h + 2)
                    for r, half in enumerate((0, 0, 1)):
                        for j in range(4):
                            sp.dma_start(kp[32 * r:32 * r + 32, j, 2 * h:2 * h + 2, :].bitcast(F32),
                                         knat[half][32 * j:32 * j + 32, h, :, :].bitcast(F32)).then_inc(kpacked[h], 16)
                if b + 1 < B:
                    load_q(b + 1) if b == 0 else None
                    if b > 0:
                        sp.wait_ge(scores_ok, NSELF + 4 * b)
                        load_q(b + 1)
            sp.wait_ge(pv_ok, 2 * NSELF)
            sp.wait_ge(unit_out, unit_at[("XO", B - 1, 0)] + 1)
            sp.dma_start(gw[:, :, :], gw_d).then_inc(gate_in, 16)
            sp.dma_start(gbias[:, :], gb_d.broadcast_to([T, NE])).then_inc(gate_in, 16)
            sp.dma_start(iota[:, :], iota_d.broadcast_to([T, NE])).then_inc(gate_in, 16)
            for e in range(NF):
                if e >= 2:
                    sp.wait_ge(fw_split, e - 1)
                sp.dma_start(fstage[:, e % 2, 0:2048], w13_d[e]).then_inc(fw_in[e % 2], 16)
                sp.dma_start(fstage[:, e % 2, 2048:3072], w2_d[e]).then_inc(fw_in[e % 2], 16)
            for b in range(B):
                sp.wait_ge(down_out, B * (NF - 1) + b + 1)
                sp.dma_start(out_d[b, :, :], x[:, b, :]).then_inc(stored, 16)
            sp.wait_ge(stored, 16 * B)

        @block.gpsimd
        def _(pool):
            k = [0]

            def own(ins):
                k[0] += 1
                ins.then_inc(pool_step, 1)
                pool.wait_ge(pool_step, k[0])
            own(nc.gpsimd.memset(ident[:, :], 0.0))
            own(nc.gpsimd.affine_select(out=ident[:, :], in_=ident[:, :], compare_op=ALU.not_equal, fill=1.0,
                                        base=0, pattern=[[-1, 128]], channel_multiplier=1))
            own(nc.gpsimd.memset(maskf[:, :, :], 0.0))
            nc.gpsimd.affine_select(out=maskf[:, :, :], in_=maskf[:, :, :], compare_op=ALU.is_ge, fill=MASKED,
                                    base=0, pattern=[[0, 4], [-1, T]], channel_multiplier=1).then_inc(ident_ok, 1)
            pool.wait_ge(const_in, 16 * 7)
            for b in range(B):
                pool.wait_ge(xn_ok, b + 1)
                nc.gpsimd.tensor_tensor(x[:, b, :], x[:, b, :], bout[:, :], ALU.add).then_inc(bias_added, 1)

            def load(i):
                src, cols, hi, lo, waits = pieces[i]
                pool.dma_start(stage[:, i % 2, 0:cols], src).then_inc(stage_in[i % 2], 16)
            load(0)
            for i, (src, cols, hi, lo, waits) in enumerate(pieces):
                if i == piece_at[("cx", 2, 0)]:
                    for b in range(B):
                        pool.wait_ge(xn_ok, B + b + 1)
                        nc.gpsimd.tensor_tensor(x[:, b, :], x[:, b, :], xbo[:, :], ALU.add).then_inc(bias_added, 1)
                if i + 1 < len(pieces):
                    if i > 0:
                        pool.wait_ge(late_split, i)
                    load(i + 1)
                what, value = waits
                if what == "unit":
                    pool.wait_ge(unit_mm, value + 1)
                else:
                    pool.wait_ge(scores_ok, value)
                pool.wait_ge(stage_in[i % 2], 16 * (i // 2 + 1))
                raw = stage[:, i % 2, 0:cols]
                if len(hi.shape) == 4:
                    raw = raw.rearrange("p (a b c) -> p a b c", a=hi.shape[1], b=hi.shape[2])
                else:
                    raw = raw.rearrange("p (a b) -> p a b", a=hi.shape[1])
                own(nc.gpsimd.tensor_copy(hi, raw))
                nc.gpsimd.tensor_tensor(lo, raw, hi, ALU.subtract).then_inc(late_split, 1)
            for e in range(NF):
                pool.wait_ge(fw_in[e % 2], 32 * (e // 2 + 1))
                if e >= 2:
                    pool.wait_ge(down_mm, B * (e - 1))
                w13 = fstage[:, e % 2, 0:2048].rearrange("p (k i f) -> p k i f", k=KD, i=2)
                w2 = fstage[:, e % 2, 2048:3072].rearrange("p (k n) -> p k n", k=2)
                nc.gpsimd.tensor_copy(fw13[e % 2][0][:, :, :, :], w13)
                own(nc.gpsimd.tensor_copy(fw2[e % 2][0][:, :, :], w2))
                nc.gpsimd.tensor_tensor(fw13[e % 2][1][:, :, :, :], w13, fw13[e % 2][0][:, :, :, :], ALU.subtract)
                nc.gpsimd.tensor_tensor(fw2[e % 2][1][:, :, :], w2, fw2[e % 2][0][:, :, :], ALU.subtract).then_inc(fw_split, 1)

        @block.scalar
        def _(act):
            for dst, src in ((bqk, bqk_d), (bv, bv_d), (xbq, xbq_d), (xbk, xbk_d), (xbv, xbv_d)):
                act.dma_start(dst[:, :], src).then_inc(const_in, 16)
            act.dma_start(bout[:, :], bout_d.broadcast_to([T, D])).then_inc(const_in, 16)
            act.dma_start(xbo[:, :], xbo_d.broadcast_to([T, D])).then_inc(const_in, 16)

            def std():
                act.wait_ge(var_ok, std.n + 1)
                nc.scalar.activation(sd[:, :], ve[:, :], ACT.Sqrt).then_inc(sdev_ok, 1)
                std.n += 1
            std.n = 0

            def unit_high(u):
                kind, a, b = u
                if kind in ("O", "XO"):
                    return
                i = unit_at[u]
                act.wait_ge(unit_mm, i + 1)
                src, dst, bias = unit_io(u)
                if kind == "QK" and a >= 1:
                    act.wait_ge(packed[(a - 1) % 2], 16 * 24 * ((a - 1) // 2 + 1))
                if kind == "V" and a >= 2:
                    act.wait_ge(pv_ok, 8 * (a - 1))
                if kind == "Q" and a >= 2:
                    act.wait_ge(q_stored[a % 2], 64 * (a // 2))
                if kind == "K" and a >= 1:
                    act.wait_ge(kpacked[b // 2], 16 * 12 * a)
                if kind == "XV":
                    act.wait_ge(pv_ok, NSELF + 4 * (a - 1))
                if bias is None:
                    nc.scalar.activation(dst[0], src, ACT.Copy).then_inc(unit_hi, 1)
                else:
                    nc.scalar.activation(dst[0], src, ACT.Identity, bias=bias).then_inc(unit_hi, 1)

            def tail_high(n, chunks):
                for c in chunks:
                    ci = chunk(n, c)
                    kc = T if n < NSELF else KEYS[c]
                    act.wait_ge(tp_ok, ci + 1)
                    if n > 0:
                        act.wait_ge(pv_ok, n)
                    nc.scalar.activation(PT[0][0:kc, c, :], bank[4 + ci % 2][0:kc, 0:4 * T], ACT.Copy).then_inc(pt_hi, 1)

            def exps(n):
                act.wait_ge(negmax_ok, n + 1)
                if n > 0:
                    act.wait_ge(tp_ok, chunk(n - 1) + nchunks(n - 1))
                for j in range(4):
                    src = score_ap(n)[:, j, :]
                    last = nc.scalar.activation(P[:, j, 0:src.shape[-1]], src, ACT.Exp, bias=nb[:, j:j + 1],
                                                scale=SCALE, accum_out=rs[:, n % 2, j:j + 1])
                last.then_inc(exp_ok, 1)

            def heads_out(n):
                bias = bv if n < NSELF else xbv
                g = n % NG
                act.wait_ge(pv_ok, n + 1)
                if g == 0 and n > 0:
                    act.wait_ge(o_split, n // NG)
                for j in range(4):
                    last = nc.scalar.activation(oT[32 * j:32 * j + 32, g, :], bank[6][32 * j:32 * j + 32, T * j:T * (j + 1)],
                                                ACT.Identity, bias=bias[32 * j:32 * j + 32, g:g + 1])
                last.then_inc(o_out, 1)

            std()
            for i in range(8):
                act.wait_ge(araw_in[i], 16)
                raw, halves = whole(i)
                nc.scalar.activation(halves[0], raw, ACT.Copy).then_inc(split_hi, 1)
            act.wait_ge(const_in, 16 * 7)
            for u in prologue:
                unit_high(u)
            for first, slots in ((0, self_slots), (NSELF, cross_slots)):
                for s, (ua, ub) in enumerate(slots):
                    n = first + s
                    if s > 0:
                        tail_high(n - 1, range(nchunks(n - 1))[0:2])
                    for u in ua:
                        unit_high(u)
                    if s > 0 and nchunks(n - 1) > 2:
                        tail_high(n - 1, [2])
                    if s < NSELF:
                        exps(n)
                    if s > 0:
                        heads_out(n - 1)
                    for u in ub:
                        unit_high(u)
                if first == 0:
                    std()
                    for u in boundary:
                        unit_high(u)
            std()
            for u in ffn_x:
                unit_high(u)
            act.wait_ge(negmax_ok, 2 * NSELF + 1)
            nc.scalar.activation(sc[:, :, :], lg[:, :, :], ACT.Exp).then_inc(gexp, 1)
            for e in range(NF):
                for c in range(4):
                    i = 4 * e + c
                    act.wait_ge(up_mm, i + 1)
                    if i >= 2:
                        act.wait_ge(h_ok, i - 1)
                    nc.scalar.activation(sg[:, i % 2, :], bank[2 * (i % 2)][:, 0:4 * T], ACT.Silu).then_inc(silu_ok, 1)
                    act.wait_ge(h_ok, i + 1)
                    if e >= 2:
                        act.wait_ge(down_mm, B * (e - 1))
                    half, it = divmod(c, 2)
                    nc.scalar.activation(hT[e % 2][0][:, it, 4 * T * half:4 * T * (half + 1)], hf[:, i % 2, :],
                                         ACT.Copy).then_inc(h_hi, 1)

        @block.vector
        def _(dve):
            k = [0]

            def own(ins):
                k[0] += 1
                ins.then_inc(dve_step, 1)
                dve.wait_ge(dve_step, k[0])

            def stats():
                for b in range(B):
                    last = nc.vector.bn_stats(st[:, b, :], x[:, b, :])
                own(last)
                for b in range(B):
                    last = nc.vector.bn_aggr(mv[:, b, :], st[:, b, :])
                own(last)
                nc.vector.tensor_scalar(ve[:, :], mv[:, :, 1], EPS, None, ALU.add).then_inc(var_ok, 1)
                stats.n += 1
                dve.wait_ge(sdev_ok, stats.n)
                own(nc.vector.reciprocal(r0[:, :], sd[:, :]))
                own(nc.vector.tensor_tensor(t1[:, :], ve[:, :], r0[:, :], ALU.mult))
                own(nc.vector.tensor_tensor(t2[:, :], t1[:, :], r0[:, :], ALU.mult))
                own(nc.vector.tensor_scalar(t3[:, :], t2[:, :], -0.5, 1.5, ALU.mult, ALU.add))
                own(nc.vector.tensor_tensor(rstd[:, :], t3[:, :], r0[:, :], ALU.mult))
            stats.n = 0

            def normalise(i):
                u = x_units[i]
                b = unit_row(u)
                if i >= 2:
                    dve.wait_ge(unit_mm, unit_at[x_units[i - 2]] + 1)
                nc.vector.tensor_scalar(xn[:, i % 2, :], x[:, b, :], mv[:, b, 0:1], rstd[:, b:b + 1],
                                        ALU.subtract, ALU.mult).then_inc(xn_ok, 1)

            def unit_low(u):
                kind, a, b = u
                i = unit_at[u]
                if kind in ("O", "XO"):
                    dve.wait_ge(unit_mm, i + 1)
                    dve.wait_ge(bias_added, a + 1 + (B if kind == "XO" else 0))
                    nc.vector.tensor_tensor(x[:, a, :], bank[ubank[i]][0:T, :], x[:, a, :], ALU.add).then_inc(unit_out, 1)
                    return
                src, dst, bias = unit_io(u)
                dve.wait_ge(unit_hi, hi_at[u] + 1)
                if bias is None:
                    nc.vector.tensor_tensor(dst[1], src, dst[0], ALU.subtract).then_inc(unit_out, 1)
                else:
                    nc.vector.scalar_tensor_tensor(dst[1], src, bias, dst[0], ALU.add, ALU.subtract).then_inc(unit_out, 1)
                if u in xn_at:
                    nxt = xn_at[u] + 2
                    if nxt < len(x_units) and x_units[nxt][0] == kind:
                        normalise(nxt)

            def rowmax(n):
                dve.wait_ge(scores_ok, n + 1)
                own(nc.vector.tensor_reduce(mx[:, :], score_ap(n), AX.X, ALU.max))
                if n > 0:
                    dve.wait_ge(exp_ok, n)
                nc.vector.tensor_scalar(nb[:, :], mx[:, :], -SCALE, None, ALU.mult).then_inc(negmax_ok, 1)

            def tail_low(n, chunks):
                for c in chunks:
                    ci = chunk(n, c)
                    kc = T if n < NSELF else KEYS[c]
                    dve.wait_ge(pt_hi, ci + 1)
                    nc.vector.tensor_tensor(PT[1][0:kc, c, :], bank[4 + ci % 2][0:kc, 0:4 * T], PT[0][0:kc, c, :],
                                            ALU.subtract).then_inc(pt_lo, 1)

            def norm_probs(n):
                dve.wait_ge(exp_ok, n + 1)
                own(nc.vector.reciprocal(rr[:, :], rs[:, n % 2, :]))
                width = T if n < NSELF else S
                for j in range(4):
                    last = nc.vector.tensor_scalar(P[:, j, 0:width], P[:, j, 0:width], rr[:, j:j + 1], None, ALU.mult)
                last.then_inc(probs_ok, 1)

            def heads_split(n):
                b = n // NG
                dve.wait_ge(o_out, n + 1)
                if b > 0:
                    prev = ("O", b - 1, 0) if b <= B else ("XO", b - 1 - B, 0)
                    dve.wait_ge(unit_mm, unit_at[prev] + 1)
                own(nc.vector.tensor_copy(oTs[0][:, :, :], oT[:, :, :]))
                nc.vector.tensor_tensor(oTs[1][:, :, :], oT[:, :, :], oTs[0][:, :, :], ALU.subtract).then_inc(o_split, 1)

            dve.wait_ge(x_in, 16)
            stats()
            normalise(0)
            normalise(1)
            dve.wait_ge(ident_ok, 1)
            nc.vector.tensor_copy(identr[:, :], ident[0:T, 0:T])
            nc.vector.tensor_copy(maskr[:, :, :], maskf[:, :, :]).then_inc(consts_ok, 1)
            for i in range(8):
                dve.wait_ge(split_hi, i + 1)
                raw, halves = whole(i)
                nc.vector.tensor_tensor(halves[1], raw, halves[0], ALU.subtract).then_inc(split_lo, 1)
            dve.wait_ge(const_in, 16 * 7)
            for u in prologue:
                unit_low(u)
            for first, slots in ((0, self_slots), (NSELF, cross_slots)):
                for s, (ua, ub) in enumerate(slots):
                    n = first + s
                    if s < NSELF:
                        rowmax(n)
                    if s > 0:
                        tail_low(n - 1, range(nchunks(n - 1))[0:2])
                    for u in ua:
                        unit_low(u)
                    if s > 0 and nchunks(n - 1) > 2:
                        tail_low(n - 1, [2])
                    if s < NSELF:
                        norm_probs(n)
                    if s > 0 and (n - 1) % NG == 3:
                        heads_split(n - 1)
                    for u in ub:
                        unit_low(u)
                if first == 0:
                    unit_low(boundary[0])
                    own(nc.vector.tensor_copy(t1[:, :], mv[:, :, 0]))
                    stats()
                    normalise(B)
                    normalise(B + 1)
                    for u in boundary[1:]:
                        unit_low(u)
            unit_low(last_o[0])
            own(nc.vector.tensor_copy(t1[:, :], mv[:, :, 0]))
            stats()
            normalise(2 * B)
            normalise(2 * B + 1)
            dve.wait_ge(gate_in, 48)
            own(nc.vector.tensor_copy(gwr[0][:, :, :], gw[:, :, :]))
            nc.vector.tensor_tensor(gwr[1][:, :, :], gw[:, :, :], gwr[0][:, :, :], ALU.subtract).then_inc(consts_ok, 1)
            for u in ffn_x:
                unit_low(u)
            dve.wait_ge(router_mm, 1)
            lgp = bank[4][0:T, 0:B * NE].rearrange("p (b e) -> p b e", e=NE)
            own(nc.vector.tensor_reduce(gmx[:, :], lgp, AX.X, ALU.max))
            nc.vector.tensor_tensor(lg[:, :, :], lgp, gmx[:, :].unsqueeze(2).to_broadcast([T, B, NE]),
                                    ALU.subtract).then_inc(negmax_ok, 1)
            dve.wait_ge(gexp, 1)
            own(nc.vector.tensor_reduce(gsm[:, :], sc[:, :, :], AX.X, ALU.add))
            own(nc.vector.reciprocal(grc[:, :], gsm[:, :]))
            own(nc.vector.tensor_tensor(lg[:, :, :], sc[:, :, :], grc[:, :].unsqueeze(2).to_broadcast([T, B, NE]), ALU.mult))
            own(nc.vector.tensor_tensor(bi[:, :, :], lg[:, :, :], gbias[:, :].unsqueeze(1).to_broadcast([T, B, NE]), ALU.add))
            for b in range(B):
                own(nc.vector.max(top[:, b, :], bi[:, b, :]))
                own(nc.vector.max_index(tix[:, b, :], top[:, b, :], bi[:, b, :]))
            own(nc.vector.tensor_copy(tixf[:, :, :], tix[:, :, :]))
            iob = iota[:, :].unsqueeze(1).to_broadcast([T, B, NE])
            own(nc.vector.tensor_tensor(m0[:, :, :], iob, tixf[:, :, 0:1].to_broadcast([T, B, NE]), ALU.is_equal))
            own(nc.vector.tensor_tensor(m1[:, :, :], iob, tixf[:, :, 1:2].to_broadcast([T, B, NE]), ALU.is_equal))
            own(nc.vector.tensor_tensor(m0[:, :, :], m0[:, :, :], m1[:, :, :], ALU.add))
            own(nc.vector.tensor_tensor(dw[:, :, :], m0[:, :, :], lg[:, :, :], ALU.mult))

            def up(e):
                for c in range(4):
                    i = 4 * e + c
                    half, it = divmod(c, 2)
                    dve.wait_ge(silu_ok, i + 1)
                    if i >= 2:
                        dve.wait_ge(h_hi, i - 1)
                        dve.wait_ge(h_lo, i - 1)
                    nc.vector.tensor_tensor(hf[:, i % 2, :], bank[2 * (i % 2) + 1][:, 0:4 * T], sg[:, i % 2, :],
                                            ALU.mult).then_inc(h_ok, 1)
                    dve.wait_ge(h_hi, i + 1)
                    span = slice(4 * T * half, 4 * T * (half + 1))
                    nc.vector.tensor_tensor(hT[e % 2][1][:, it, span], hf[:, i % 2, :], hT[e % 2][0][:, it, span],
                                            ALU.subtract).then_inc(h_lo, 1)

            def down(e):
                for b in range(B):
                    i = B * e + b
                    dve.wait_ge(down_mm, i + 1)
                    if e > 0:
                        dve.wait_ge(down_out, i - B + 1)
                    src = bank[4 + i % 3][0:T, :]
                    if e < NE:
                        nc.vector.scalar_tensor_tensor(x[:, b, :], src, dw[:, b, e:e + 1], x[:, b, :],
                                                       ALU.mult, ALU.add).then_inc(down_out, 1)
                    else:
                        nc.vector.tensor_tensor(x[:, b, :], src, x[:, b, :], ALU.add).then_inc(down_out, 1)
            up(0)
            for e in range(NF):
                if e + 1 < NF:
                    up(e + 1)
                down(e)

        @block.tensor
        def _(pe):
            def product(out, lhs, rhs, first=True, last=True):
                for t in range(product.tiles):
                    for i, (s, m) in enumerate(PASSES):
                        ins = nc.tensor.matmul(out, lhs(s, t), rhs(m, t), start=first and t == 0 and i == 0,
                                               stop=last and t == product.tiles - 1 and i == 2)
                return ins
            product.tiles = KD

            def unit(u):
                kind, a, b = u
                i = unit_at[u]
                bk = bank[ubank[i]]
                if prev_user[i] is not None:
                    pe.wait_ge(unit_out, prev_user[i] + 1)
                if kind in ("X", "X2", "X3"):
                    pe.wait_ge(xn_ok, xn_at[u] + 1)
                    if xn_at[u] == 0:
                        pe.wait_ge(ident_ok, 1)
                    for t in range(KD):
                        last = nc.tensor.transpose(bk[:, T * t:T * (t + 1)], xn[:, xn_at[u] % 2, 128 * t:128 * (t + 1)],
                                                   ident[0:T, 0:T])
                elif kind == "QK":
                    pe.wait_ge(unit_out, unit_at[("X", a, 1)] + 1)
                    pe.wait_ge(split_lo, b // 2 + 1)
                    last = product(bk[:, 0:2 * T], lambda h, t: wqk[h][:, b, t, :], lambda h, t: xnT[h][:, t, :])
                elif kind == "V":
                    pe.wait_ge(unit_out, unit_at[("X", a, 1)] + 1)
                    pe.wait_ge(split_lo, 6)
                    last = product(bk[0:T, :], lambda h, t: xnT[h][:, t, T * b:T * (b + 1)], lambda h, t: wv[h][:, t, :])
                elif kind in ("O", "XO"):
                    w = wout if kind == "O" else xwo
                    pe.wait_ge(o_split, a + 1 + (B if kind == "XO" else 0))
                    if kind == "O":
                        pe.wait_ge(split_lo, 8)
                    else:
                        pe.wait_ge(late_split, piece_at[("wo", 1)] + 1)
                    last = product(bk[0:T, :], lambda h, t: oTs[h][:, t, :], lambda h, t: w[h][:, t, :])
                elif kind == "Q":
                    pe.wait_ge(unit_out, unit_at[("X2", a, 1)] + 1)
                    pe.wait_ge(late_split, piece_at[("wq", b // 2)] + 1)
                    last = product(bk[:, 0:2 * T], lambda h, t: xwq[h][:, b, t, :], lambda h, t: xnT[h][:, t, :])
                elif kind == "K":
                    pe.wait_ge(late_split, max(piece_at[("cx", a, 1)], piece_at[("wk", 1)]) + 1)
                    last = product(bk[:, 0:SP], lambda h, t: xwk[h][:, b, t, :], lambda h, t: cx[h][:, a % 2, t, :])
                elif kind == "XV":
                    pe.wait_ge(late_split, max(piece_at[("cx", a, 1)], piece_at[("wv", 1)]) + 1)
                    last = product(bk[0:KEYS[b], :], lambda h, t: cx[h][:, a % 2, t, 128 * b:128 * b + KEYS[b]],
                                   lambda h, t: xwv[h][:, t, :])
                last.then_inc(unit_mm, 1)

            def scores(n):
                if n < NSELF:
                    p, i = divmod(n // NG, 2)
                    g = n % NG
                    pe.wait_ge(packed[p % 2], 16 * 24 * (p // 2 + 1))
                    if n >= 2:
                        pe.wait_ge(exp_ok, n - 1)
                    if n == 0:
                        pe.wait_ge(consts_ok, 1)
                    out = bank[n % 2][0:T, 0:4 * T].rearrange("p (j t) -> p j t", j=4)
                    nc.tensor.matmul(bank[n % 2][0:T, 0:4 * T], identr[:, :], maskr[:, :, :].rearrange("p j t -> p (j t)"),
                                     start=True, stop=False)
                    for j in range(4):
                        last = nc.tensor.matmul(out[:, j, :], pq[p % 2][:, j, g, T * i:T * (i + 1)],
                                                pk[p % 2][:, j, g, T * i:T * (i + 1)], start=False, stop=j == 3)
                else:
                    b, g = divmod(n - NSELF, NG)
                    pe.wait_ge(q_loaded[b % 2], 16 * 3 * (b // 2 + 1))
                    pe.wait_ge(kpacked[g // 2], 16 * 12 * (b + 1))
                    pe.wait_ge(exp_ok, n)
                    if n == NSELF:
                        pe.wait_ge(unit_out, first_cross)
                    for j in range(4):
                        last = nc.tensor.matmul(bank[j][0:T, 0:SP], qp[:, b % 2, j, g, :], kp[:, j, g, :], start=True, stop=True)
                last.then_inc(scores_ok, 1)

            def transposes(n, chunks):
                for c in chunks:
                    ci = chunk(n, c)
                    kc = T if n < NSELF else KEYS[c]
                    pe.wait_ge(probs_ok, n + 1)
                    if ci >= 2:
                        pe.wait_ge(pt_lo, ci - 1)
                    for j in range(4):
                        last = nc.tensor.transpose(bank[4 + ci % 2][0:kc, T * j:T * (j + 1)], P[:, j, 128 * c:128 * c + kc],
                                                   ident[0:T, 0:T])
                    last.then_inc(tp_ok, 1)

            def values(n):
                if n > 0:
                    pe.wait_ge(o_out, n)
                g = n % NG
                buf, c0 = vslot(n)
                steps = [(c, s, m) for c in range(nchunks(n)) for s, m in PASSES]
                for i, (c, s, m) in enumerate(steps):
                    kc = T if n < NSELF else KEYS[c]
                    if i % 3 == 0:
                        pe.wait_ge(pt_lo, chunk(n, c) + 1)
                    last = nc.tensor.matmul(bank[6][:, 0:4 * T], v[s][0:kc, buf, c0 + c, 128 * g:128 * (g + 1)],
                                            PT[m][0:kc, c, :], start=i == 0, stop=i == len(steps) - 1)
                last.then_inc(pv_ok, 1)

            def v_ready(n):
                if n < NSELF:
                    b = n // NG
                    pe.wait_ge(unit_out, unit_at[("V", b // 2, b % 2)] + 1)
                else:
                    pe.wait_ge(unit_out, unit_at[("XV", (n - NSELF) // NG, 2)] + 1)

            for u in prologue:
                unit(u)
            for first, slots in ((0, self_slots), (NSELF, cross_slots)):
                for s, (ua, ub) in enumerate(slots):
                    n = first + s
                    if s < NSELF:
                        scores(n)
                    if s > 0:
                        transposes(n - 1, range(nchunks(n - 1))[0:2])
                    for u in ua:
                        unit(u)
                    if s > 0:
                        if nchunks(n - 1) > 2:
                            transposes(n - 1, [2])
                        if (n - 1) % NG == 0:
                            v_ready(n - 1)
                        values(n - 1)
                    for u in ub:
                        unit(u)
                if first == 0:
                    for u in boundary:
                        unit(u)
            for u in last_o + ffn_x:
                unit(u)
            pe.wait_ge(unit_out, unit_at[("X3", B - 1, 0)] + 1)
            pe.wait_ge(consts_ok, 2)
            for b in range(B):
                last = product(bank[4][0:T, NE * b:NE * (b + 1)], lambda h, t: fx[h][:, t, T * b:T * (b + 1)],
                               lambda h, t: gwr[h][:, t, :])
            last.then_inc(router_mm, 1)

            def up(e):
                pe.wait_ge(fw_split, e + 1)
                for c in range(4):
                    i = 4 * e + c
                    half, it = divmod(c, 2)
                    if i >= 2:
                        pe.wait_ge(h_ok, i - 1)
                    for w in range(2):
                        last = product(bank[2 * (i % 2) + w][:, 0:4 * T],
                                       lambda h, t: fw13[e % 2][h][:, t, w, 128 * it:128 * (it + 1)],
                                       lambda h, t: fx[h][:, t, 4 * T * half:4 * T * (half + 1)])
                    last.then_inc(up_mm, 1)

            def down(e):
                pe.wait_ge(h_lo, 4 * (e + 1))
                product.tiles = 2
                for b in range(B):
                    i = B * e + b
                    if i >= 3:
                        pe.wait_ge(down_out, i - 2)
                    if i == 0:
                        pe.wait_ge(gexp, 1)
                    product(bank[4 + i % 3][0:T, :], lambda h, t: hT[e % 2][h][:, t, T * b:T * (b + 1)],
                            lambda h, t: fw2[e % 2][h][:, t, :]).then_inc(down_mm, 1)
                product.tiles = KD
            up(0)
            for e in range(NF):
                if e + 1 < NF:
                    up(e + 1)
                down(e)


def kernel(**inputs):
    import numpy as np
    import concourse.bacc as bacc
    from concourse.bass_utils import run_bass_kernel_spmd

    g = {k: np.asarray(a) for k, a in inputs.items()}

    def by_tile(w):
        n, m = w.shape
        return w.reshape(n // 128, 128, m // 128, 128).transpose(3, 0, 2, 1).reshape(128, -1)

    def by_row(w):
        n, m = w.shape
        return w.T.reshape(m // 128, 128, n).transpose(1, 0, 2).reshape(128, -1)

    def column(b):
        return b.reshape(-1, 128).T

    wqkv, bqkv = g["L0_attn_w_qkv"], g["L0_attn_b_qkv"]
    c = g["ctx_2048"].transpose(0, 2, 1)
    c = np.concatenate([c, np.zeros(c.shape[:2] + (1,), c.dtype)], axis=2)
    c = c.reshape(8, 4, 128, 362).transpose(0, 2, 1, 3).reshape(8, 128, -1)
    w1 = np.concatenate([g["L0_ffn_W1"], g["L0_ffn_Ws1"][None]])
    w3 = np.concatenate([g["L0_ffn_W3"], g["L0_ffn_Ws3"][None]])
    w2 = np.concatenate([g["L0_ffn_W2"], g["L0_ffn_Ws2"][None]])
    w13 = np.stack([w1, w3], axis=1)
    w13 = w13.reshape(9, 2, 256, 4, 128).transpose(0, 4, 3, 1, 2).reshape(9, 128, -1)
    w2 = np.stack([by_row(w) for w in w2])
    arrays = {
        "x": g["x"], "ctx": c, "wqk": by_tile(wqkv[:1024]), "wv": by_row(wqkv[1024:]),
        "wout": by_row(g["L0_attn_w_out"]), "bqk": column(bqkv[:1024]), "bv": column(bqkv[1024:]),
        "bout": g["L0_attn_b_out"][None], "xwq": by_tile(g["L0_xattn_Wq"]), "xwk": by_tile(g["L0_xattn_Wk"]),
        "xwv": by_row(g["L0_xattn_Wv"]), "xwo": by_row(g["L0_xattn_Wo"]), "xbq": column(g["L0_xattn_bq"]),
        "xbk": column(g["L0_xattn_bk"]), "xbv": column(g["L0_xattn_bv"]), "xbo": g["L0_xattn_bo"][None],
        "gw": by_row(g["L0_ffn_gate_w"]), "gb": g["L0_ffn_gate_b"][None],
        "iota": np.arange(8, dtype=np.float32)[None], "w13": w13, "w2": w2,
    }
    arrays = {f"in_{k}": np.ascontiguousarray(a) for k, a in arrays.items()}
    nc = bacc.Bacc("TRN2", target_bir_lowering=False, num_devices=1, dynamic_dma_scratch_size=4096)
    args = [nc.dram_tensor(k, a.shape, mybir.dt.from_np(a.dtype), kind="ExternalInput").ap() for k, a in arrays.items()]
    out = nc.dram_tensor("out_x", (8, 100, 512), mybir.dt.float32, kind="ExternalOutput").ap()
    decoder_layer(nc, *args, out)
    r = run_bass_kernel_spmd(nc, [arrays], core_ids=[0])
    return r.results[0]["out_x"]
```

```python
import concourse.bass as bass
from concourse import mybir
from contextlib import ExitStack


def decoder_layer(nc, x_d, ctx_d, wqk_d, wv_d, wout_d, bqk_d, bv_d, bout_d,
                  xwq_d, xwk_d, xwv_d, xwo_d, xbq_d, xbk_d, xbv_d, xbo_d,
                  gw_d, gb_d, iota_d, tri_d, w13_d, w2_d, out_d):
    F32 = mybir.dt.float32
    F32R = mybir.dt.float32r
    U32 = mybir.dt.uint32
    I32 = mybir.dt.int32
    ALU = mybir.AluOpType
    ACT = mybir.ActivationFunctionType
    AX = mybir.AxisListType

    B, T, D = 8, 100, 512
    S = 361
    SP = S + 1
    KD = D // 128
    NG = 4
    HD = 32
    NE = 8
    FI = 256
    NR = 128
    NT = (2 * B * T - NE) // NR + NE
    SCALE = float(HD) ** -0.5
    MASKED = -1.0e30
    EPS = 1e-5
    KEYS = [128, 128, S - 256]
    NSELF = B * NG
    PASSES = ((0, 0), (1, 0), (0, 1))

    ctx = ExitStack()
    with ctx:
        cursor = [(nc.sbuf_base + 31) // 32 * 32]

        def at(name, shape, dt, offset):
            return nc.alloc_sbuf_tensor_at(name, shape, dt, offset=offset)

        def size(shape):
            n = 4
            for s in shape[1:]:
                n *= s
            return (n + 31) // 32 * 32

        def sb(name, shape, dt=F32):
            t = at(name, shape, dt, cursor[0])
            cursor[0] += size(shape)
            return t

        def sem(name):
            return ctx.enter_context(nc.semaphore(name))

        x = sb("x_res", [T, B, D])
        x_end = cursor[0]
        v = [sb(f"v_{h}", [128, 2, 3, D], F32R) for h in ("hi", "lo")]
        probs_at = cursor[0]
        P = sb("probs", [T, 4, SP])
        pt_at = cursor[0]
        PT = [sb(f"probsT_{h}", [128, 3, 4 * T], F32R) for h in ("hi", "lo")]
        oT = sb("oT", [128, NG, T])
        oTs = [sb(f"oT_{h}", [128, NG, T], F32R) for h in ("hi", "lo")]
        stage = sb("stage", [128, 2, 1024])
        nat_at = cursor[0]
        nat = [sb(f"nat_{h}", [128, 8, 2 * T], F32R) for h in ("hi", "lo")]
        xnT = [sb(f"xnT_{h}", [128, KD, 2 * T], F32R) for h in ("hi", "lo")]
        xn = sb("xn", [T, 2, D])
        bout = sb("bout_bc", [T, D])
        identr = sb("identr", [T, T], F32R)
        mask_at = cursor[0]
        maskr = sb("maskr", [T, 4, T], F32R)
        mask_end = cursor[0]
        xbo = sb("xbo_bc", [T, D])
        ident = sb("ident", [128, 128])
        maskf = at("maskf", [T, 4, T], F32, probs_at)
        bqk = sb("bqk", [128, 8])
        bv = sb("bv", [128, 4])
        xbq = sb("xbq", [128, 4])
        xbk = sb("xbk", [128, 4])
        xbv = sb("xbv", [128, 4])
        st = sb("bnst", [T, B, 6])
        mv = sb("meanvar", [T, B, 2])
        ve = sb("vareps", [T, B])
        sd = sb("sdev", [T, B])
        r0 = sb("rstd0", [T, B])
        t1 = sb("newt1", [T, B])
        t2 = sb("newt2", [T, B])
        t3 = sb("newt3", [T, B])
        rstd = sb("rstd", [T, B])
        mx = sb("rowmax", [T, 4])
        nb = sb("negmax", [T, 4])
        rs = sb("rowsum", [T, 2, 4])
        rr = sb("rowrec", [T, 4])
        common_end = cursor[0]

        wqk = [sb(f"wqk_{h}", [128, 8, KD, 128], F32R) for h in ("hi", "lo")]
        wv = [sb(f"wv_{h}", [128, KD, D], F32R) for h in ("hi", "lo")]
        wout = [sb(f"wout_{h}", [128, KD, D], F32R) for h in ("hi", "lo")]
        packs_at = cursor[0]
        pq, pk = [], []
        for par in range(2):
            pq.append(sb(f"pq{par}", [96, 4, 4, 2 * T], F32R))
            pk.append(sb(f"pk{par}", [96, 4, 4, 2 * T], F32R))
        araw = at("araw", [128, 8, 1024], F32, packs_at)
        self_end = cursor[0]

        a_wqk = common_end
        a_wv = a_wqk + 2 * 16384
        a_wout = a_wv + 2 * 8192
        xwk = [at(f"xwk_{i}", [128, 4, KD, 128], F32R, a_wqk + 8192 * i) for i in range(2)]
        xwq = [at(f"xwq_{i}", [128, 4, KD, 128], F32R, a_wqk + 16384 + 8192 * i) for i in range(2)]
        xwv = [at(f"xwv_{i}", [128, KD, D], F32R, a_wv + 8192 * i) for i in range(2)]
        xwo = [at(f"xwo_{i}", [128, KD, D], F32R, a_wout + 8192 * i) for i in range(2)]
        knat = [at(f"knat_{i}", [128, 2, 2, SP], F32R, a_wqk + 16384 + 5792 * i) for i in range(2)]
        cx = [at(f"cx_{i}", [128, 2, KD, SP], F32R, packs_at + 11584 * i) for i in range(2)]
        kp = at("kp", [96, 4, 4, SP], F32R, packs_at + 2 * 11584)
        qp = at("qp", [96, 2, 4, 4, T], F32R, packs_at + 2 * 11584 + 23168)
        assert 2 * 11584 + 23168 + 12800 + packs_at <= nc.sbuf_usable_end

        def region(start, end):
            where = [start]

            def put(name, shape, dt=F32):
                t = at(name, shape, dt, where[0])
                where[0] += size(shape)
                assert where[0] <= end, (name, where[0], end)
                return t
            return put
        early = region(a_wqk, a_wout)
        late = region(a_wout, nc.sbuf_usable_end)
        low = region(x_end, nat_at)
        over_mask = region(mask_at, mask_end)
        fx_put = region(nat_at, mask_at)
        fx = [fx_put(f"fx_{h}", [128, KD, B * T], F32R) for h in ("hi", "lo")]
        sw13 = [early(f"sw13_{h}", [128, KD, 2, FI], F32R) for h in ("hi", "lo")]
        sw2 = [early(f"sw2_{h}", [128, 2, D], F32R) for h in ("hi", "lo")]
        raw13 = [None, early("raw13_1", [128, KD, 2, FI])]
        raw13[0] = early("raw13_0", [128, KD, 2, FI])
        raw2 = [early(f"raw2_{i}", [128, 2, D]) for i in range(2)]
        xn_late = at("xn_late", [T, 2, D], F32, a_wqk + 16384 + 2 * 5792)
        hS = [late(f"hS_{h}", [128, 2, B * T], F32R) for h in ("hi", "lo")]
        w13 = [[None, None], [None, None]]
        w2 = [[None, None], [None, None]]
        w13[1] = [late(f"w13_1{h}", [128, KD, 2 * FI], F32R) for h in ("hi", "lo")]
        w2[1] = [late(f"w2_1{h}", [128, 2, D], F32R) for h in ("hi", "lo")]
        xgT = [late(f"xgT_{h}", [128, KD, 128], F32R) for h in ("hi", "lo")]
        hTt = [late(f"hTt_{h}", [128, 2, 128], F32R) for h in ("hi", "lo")]
        sg = late("silu", [128, 2, 4 * T])
        hf = late("hf", [128, 2, 4 * T])
        xg = late("xg", [128, 2, D])
        h_tile = late("h_tile", [128, 2, FI])
        y_tile = late("y_tile", [128, 2, D])
        s_tile = late("s_tile", [128, 2, FI])
        lgT = late("logitsT", [NE, 7 * T])
        xn3 = low("xn3", [T, B, D])
        w13[0] = [low(f"w13_0{h}", [128, KD, 2 * FI], F32R) for h in ("hi", "lo")]
        w2[0] = [low(f"w2_0{h}", [128, 2, D], F32R) for h in ("hi", "lo")]
        gw = over_mask("gw_raw", [128, KD, NE])
        gwr = [over_mask(f"gw_{h}", [128, KD, NE], F32R) for h in ("hi", "lo")]
        gbias = over_mask("gate_bias", [T, NE])
        iota = over_mask("iota", [T, NT])
        tri = over_mask("before", [T, NE, NE])
        tiny = low
        rt = {n: tiny(n, [T, B, NE]) for n in ("lg", "sc", "prob", "bi", "lt", "cand", "m0", "bi2", "lt2", "cand2",
                                               "m1", "slots", "ms0", "ms1", "mw0", "mw1", "below")}
        selr = tiny("selected", [T, B, NE], F32R)
        beforer = tiny("before_r", [T, 128], F32R)
        onesr = tiny("ones_r", [T, 128], F32R)
        trif = tiny("before_f", [T, 128])
        onesf = tiny("ones_f", [T, 128])
        sm = {n: tiny(n, [T, B]) for n in ("gmx", "gsm", "grc", "top0", "ix0", "top1", "ix1", "count", "ntile",
                                           "tstart", "tend", "s0f", "s1f", "wt0", "wt1")}
        over = tiny("over", [T, NE, NE])
        slot_u = tiny("slot_u", [T, 2, B], U32)
        tmap = tiny("tmap", [1, NT, NE])
        tmapf = tiny("tmapf", [1, NT])
        tmapc = tiny("tmapc", [1, NT])
        tmapi = tiny("tmapi", [1, NT], I32)
        gath = [at(f"gath{i}", [T, D], F32, a_wqk + 2048 * i) for i in range(8)]
        zeros = at("zeros", [128, D], F32, pt_at)

        scores4 = ctx.enter_context(nc.psum_tensor("scores4", [128, 4, 512], F32))
        more = [ctx.enter_context(nc.psum_tensor(f"bank{i}", [128, 512], F32)) for i in range(4, 8)]
        bank = [scores4[:, i, :] for i in range(4)] + [m[:, :] for m in more]
        J3 = [2, 3, 7]

        qs_d = [nc.dram_tensor(f"q_scratch_{h}", [128, B, 4, T], F32, kind="Internal").ap() for h in ("hi", "lo")]

        xs_d = nc.dram_tensor("rows_by_expert", [NT * NR, D], F32, kind="Internal").ap()
        ys_d = nc.dram_tensor("results_by_expert", [NT * NR, D], F32, kind="Internal").ap()

        x_in = sem("x_in")
        const_in = sem("const_in")
        gate_in = sem("gate_in")
        araw_in = [sem(f"araw_in{i}") for i in range(8)]
        stage_in = [sem(f"stage_in{i}") for i in range(2)]
        pool_step = sem("pool_step")
        ident_ok = sem("ident_ok")
        split_hi = sem("split_hi")
        split_lo = sem("split_lo")
        consts_ok = sem("consts_ok")
        stats_ok = sem("stats_ok")
        late_var = sem("late_var")
        late_ln = sem("late_ln")
        late_guess = sem("late_guess")
        late_xn = sem("late_xn")
        var_ok = sem("var_ok")
        ln_ok = sem("ln_ok")
        sdev_ok = sem("sdev_ok")
        xn_ok = sem("xn_ok")
        dve_step = sem("dve_step")
        bias_added = sem("bias_added")
        unit_mm = sem("unit_mm")
        unit_hi = sem("unit_hi")
        unit_out = sem("unit_out")
        scores_ok = sem("scores_ok")
        negmax_ok = sem("negmax_ok")
        exp_ok = sem("exp_ok")
        probs_ok = sem("probs_ok")
        tp_ok = sem("tp_ok")
        pt_hi = sem("pt_hi")
        pt_lo = sem("pt_lo")
        pv_ok = sem("pv_ok")
        o_out = sem("o_out")
        o_split = sem("o_split")
        packed = [sem(f"packed{i}") for i in range(2)]
        kpacked = [sem(f"kpacked{i}") for i in range(2)]
        q_stored = [sem(f"q_stored{i}") for i in range(2)]
        q_loaded = [sem(f"q_loaded{i}") for i in range(2)]
        late_split = sem("late_split")
        zero_made = sem("zero_made")
        tri_made = sem("tri_made")
        zero_in = sem("zero_in")
        route_c = sem("route_c")
        gate_mm = sem("gate_mm")
        gate_out = sem("gate_out")
        tri_ok = sem("tri_ok")
        router_mm = sem("router_mm")
        logits_ok = sem("logits_ok")
        gexp = sem("gexp")
        sel_ok = sem("sel_ok")
        cum_mm = sem("cum_mm")
        slots_ok = sem("slots_ok")
        tmap_ok = sem("tmap_ok")
        scattered = sem("scattered")
        sraw_in = sem("sraw_in")
        s_hi = sem("s_hi")
        s_lo = sem("s_lo")
        sup_mm = sem("sup_mm")
        ssilu = sem("ssilu")
        sh_ok = sem("sh_ok")
        sh_hi = sem("sh_hi")
        sh_lo = sem("sh_lo")
        sdn_mm = sem("sdn_mm")
        sdn_out = sem("sdn_out")
        raw13_in = [sem(f"raw13_in{i}") for i in range(2)]
        raw2_in = [sem(f"raw2_in{i}") for i in range(2)]
        w13_hi = sem("w13_hi")
        w13_lo = sem("w13_lo")
        w2_hi = sem("w2_hi")
        w2_lo = sem("w2_lo")
        xg_in = [sem(f"xg_in{i}") for i in range(2)]
        xt_mm = sem("xt_mm")
        xt_hi = sem("xt_hi")
        xt_lo = sem("xt_lo")
        up_mm = sem("up_mm")
        silu_ok = sem("silu_ok")
        h_ok = sem("h_ok")
        ht_mm = sem("ht_mm")
        ht_hi = sem("ht_hi")
        ht_lo = sem("ht_lo")
        down_mm = sem("down_mm")
        y_out = sem("y_out")
        y_stored = [sem(f"y_stored{i}") for i in range(2)]
        gathered = [sem(f"gathered{i}") for i in range(8)]
        added = sem("added")
        stored = sem("stored")

        QP = B // 2
        units, unit_at = [], {}

        def add(*us):
            for u in us:
                unit_at[u] = len(units)
                units.append(u)
            return list(us)

        prologue = add(("X", 0, 0), ("X", 0, 1), *[("QK", 0, m) for m in range(8)], ("V", 0, 0), ("V", 0, 1),
                       ("X", 1, 0), ("X", 1, 1))
        self_slots = []
        for n in range(NSELF + 1):
            p, k = divmod(n, 8)
            q = p + 1
            a, b = [], []
            if q < QP:
                a = {0: [("QK", q, 0)], 1: [("QK", q, 2)], 2: [("QK", q, 3)], 3: [("QK", q, 5)],
                     4: [("QK", q, 7)], 5: [("V", q, 1)]}.get(k, [])
                b = {0: [("QK", q, 1)], 2: [("QK", q, 4)], 3: [("QK", q, 6)], 4: [("V", q, 0)]}.get(k, [])
            if q + 1 < QP:
                a = a + {6: [("X", q + 1, 0)], 7: [("X", q + 1, 1)]}.get(k, [])
            if k == 1 and p > 0:
                b = b + [("O", 2 * p - 1, 0)]
            if k == 5:
                b = b + [("O", 2 * p, 0)]
            self_slots.append((add(*a), add(*b)))
        boundary = add(("O", B - 1, 0))
        for p in range(QP):
            boundary += add(("X2", p, 0), ("X2", p, 1), *[("Q", p, m) for m in range(4)])
        boundary += add(*[("K", 0, g) for g in range(4)], *[("XV", 0, c) for c in range(3)])
        cross_slots = []
        for n in range(NSELF + 1):
            b, g = divmod(n, 4)
            a, bb = [], []
            if b + 1 < B:
                a = [("K", b + 1, g)]
                if g < 3:
                    bb = [("XV", b + 1, g)]
            if g == 3 and b > 0:
                bb = bb + [("XO", b - 1, 0)]
            cross_slots.append((add(*a), add(*bb)))
        last_o = add(("XO", B - 1, 0))

        first_cross = unit_at[("K", 1, 0)]
        ubank, prev_user, seen = [], [], {}
        for i, u in enumerate(units):
            if i < first_cross:
                k = J3[i % 3]
            else:
                k = 7
            prev_user.append(seen.get(k))
            seen[k] = i
            ubank.append(k)
        hi_units = [u for u in units if u[0] not in ("O", "XO")]
        hi_at = {u: i for i, u in enumerate(hi_units)}
        x_units = [u for u in units if u[0] in ("X", "X2")]
        xn_at = {u: i for i, u in enumerate(x_units)}

        pieces, piece_at = [], {}

        def piece(key, src, cols, hi, lo, waits):
            piece_at[key] = len(pieces)
            pieces.append((src, cols, hi, lo, waits))

        def flat(t):
            return t

        qk_free = ("unit", unit_at[("QK", QP - 1, 7)])
        v_free = ("unit", unit_at[("V", QP - 1, 1)])
        for i in range(2):
            piece(("wk", i), xwk_d[:, 1024 * i:1024 * (i + 1)], 1024, xwk[0][:, 2 * i:2 * i + 2, :, :],
                  xwk[1][:, 2 * i:2 * i + 2, :, :], qk_free)
        for i in range(2):
            piece(("wq", i), xwq_d[:, 1024 * i:1024 * (i + 1)], 1024, xwq[0][:, 2 * i:2 * i + 2, :, :],
                  xwq[1][:, 2 * i:2 * i + 2, :, :], qk_free)
        for i in range(2):
            piece(("wv", i), xwv_d[:, 1024 * i:1024 * (i + 1)], 1024, xwv[0][:, 2 * i:2 * i + 2, :],
                  xwv[1][:, 2 * i:2 * i + 2, :], v_free)

        def ctx_piece(b):
            for i in range(2):
                w = ("scores", 24) if b < 2 else ("unit", max(unit_at[("K", b - 2, 3)], unit_at[("XV", b - 2, 2)]))
                piece(("cx", b, i), ctx_d[b, :, 2 * SP * i:2 * SP * (i + 1)], 2 * SP,
                      cx[0][:, b % 2, 2 * i:2 * i + 2, :], cx[1][:, b % 2, 2 * i:2 * i + 2, :], w)
        ctx_piece(0)
        for i in range(2):
            piece(("wo", i), xwo_d[:, 1024 * i:1024 * (i + 1)], 1024, xwo[0][:, 2 * i:2 * i + 2, :],
                  xwo[1][:, 2 * i:2 * i + 2, :], ("unit", unit_at[("O", B - 1, 0)]))
        for b in range(1, B):
            ctx_piece(b)

        def nchunks(n):
            return 1 if n < NSELF else 3

        def x3_row(s):
            return (s - 8) // 4 if s % 4 == 0 and s >= 8 else None

        ring = []
        for n in range(2 * NSELF):
            ring += [("probs", n, c) for c in range(nchunks(n))]
            if n >= NSELF and x3_row(n - NSELF + 1) is not None:
                ring.append(("rows", x3_row(n - NSELF + 1)))
        ring.append(("rows", B - 1))
        ring_at = {r: i for i, r in enumerate(ring)}

        def chunk(n, c=0):
            return ring_at[("probs", n, c)]

        def vslot(n):
            if n < NSELF:
                b = n // NG
                return (b // 2) % 2, b % 2
            return ((n - NSELF) // NG) % 2, 0

        def unit_io(u):
            kind, a, b = u
            bk = bank[ubank[unit_at[u]]]
            if kind in ("X", "X2"):
                return (bk[:, 0:4 * T].rearrange("p (k t) -> p k t", k=KD),
                        [y[:, :, T * b:T * (b + 1)] for y in xnT], None)
            if kind == "QK":
                return bk[:, 0:2 * T], [y[:, b, :] for y in nat], bqk[:, b:b + 1]
            if kind == "Q":
                return bk[:, 0:2 * T], [y[:, 4 * (a % 2) + b, :] for y in nat], xbq[:, b:b + 1]
            if kind == "K":
                return bk[:, 0:SP], [y[:, b // 2, b % 2, :] for y in knat], xbk[:, b:b + 1]
            if kind == "V":
                return bk[0:T, :], [y[0:T, a % 2, b, :] for y in v], None
            if kind == "XV":
                return bk[0:KEYS[b], :], [y[0:KEYS[b], a % 2, b, :] for y in v], None

        def xn_tile(i):
            return xn[:, i % 2, :]

        def rows_io(b):
            src = bank[4 + ring_at[("rows", b)] % 2][:, 0:4 * T].rearrange("p (k t) -> p k t", k=KD)
            return src, [y[:, :, T * b:T * (b + 1)] for y in fx]

        def shared_piece(i, h):
            if i < KD:
                return sw13[h][:, i, :, :], raw13[0][:, i, :, :]
            return sw2[h][:, :, :], raw2[0][:, :, :]

        def score_ap(n):
            if n < NSELF:
                return bank[n % 2][0:T, 0:4 * T].rearrange("p (j t) -> p j t", j=4)
            return scores4[0:T, :, 0:S]

        def whole(i):
            raw = araw[:, i, :]
            if i < 4:
                return (raw.rearrange("p (a b c) -> p a b c", a=2, b=KD), [w[:, 2 * i:2 * i + 2, :, :] for w in wqk])
            w = wv if i < 6 else wout
            return raw.rearrange("p (a b) -> p a b", a=2), [y[:, 2 * (i % 2):2 * (i % 2) + 2, :] for y in w]

        block = ctx.enter_context(nc.Block())

        w13_f = w13_d.rearrange("e p n -> (e p) n")
        w2_f = w2_d.rearrange("e p n -> (e p) n")

        @block.sync
        def _(sp):
            sp.dma_start(x[:, :, :], x_d.rearrange("b t d -> t b d")).then_inc(x_in, 16)
            for i in range(4):
                sp.dma_start(araw[:, i, :], wqk_d[:, 1024 * i:1024 * (i + 1)]).then_inc(araw_in[i], 16)
            for i in range(2):
                sp.dma_start(araw[:, 4 + i, :], wv_d[:, 1024 * i:1024 * (i + 1)]).then_inc(araw_in[4 + i], 16)
            for i in range(2):
                sp.dma_start(araw[:, 6 + i, :], wout_d[:, 1024 * i:1024 * (i + 1)]).then_inc(araw_in[6 + i], 16)

            sp.wait_ge(zero_made, 1)
            sp.dma_start(xs_d.rearrange("(j p) d -> p j d", p=NR),
                         zeros[:, :].unsqueeze(1).to_broadcast([NR, NT, D])).then_inc(zero_in, 16)

            sp.wait_ge(split_lo, 8)
            for p in range(QP):
                if p >= 2:
                    sp.wait_ge(scores_ok, 8 * (p - 1))
                for dst, half, m0_ in ((pq[p % 2], (0, 1, 0), 0), (pk[p % 2], (0, 0, 1), 4)):
                    sp.wait_ge(unit_out, unit_at[("QK", p, m0_ + 3)] + 1)
                    for r in range(3):
                        for j in range(4):
                            sp.dma_start(dst[32 * r:32 * r + 32, j, :, :].bitcast(F32),
                                         nat[half[r]][32 * j:32 * j + 32, m0_:m0_ + 4, :].bitcast(F32)).then_inc(packed[p % 2], 16)
            for p in range(QP):
                sp.wait_ge(unit_out, unit_at[("Q", p, 3)] + 1)
                for i in range(2):
                    for h in range(2):
                        sp.dma_start(qs_d[h][:, 2 * p + i, :, :],
                                     nat[h][:, 4 * (p % 2):4 * (p % 2) + 4, T * i:T * (i + 1)].bitcast(F32)).then_inc(q_stored[p % 2], 16)

            def load_q(b):
                for r, h in enumerate((0, 1, 0)):
                    sp.dma_start(qp[32 * r:32 * r + 32, b % 2, :, :, :].rearrange("p j m t -> p j (m t)").bitcast(F32),
                                 qs_d[h][:, b, :, :].rearrange("(j d) m t -> d j (m t)", d=32)).then_inc(q_loaded[b % 2], 16)
            for par in range(2):
                sp.wait_ge(q_stored[par], 16 * 4 * QP // 2)
            sp.wait_ge(scores_ok, NSELF)
            load_q(0)
            sp.dma_start(gw[:, :, :], gw_d.rearrange("p (k e) -> p k e", k=KD)).then_inc(gate_in, 16)
            sp.dma_start(gbias[:, :], gb_d.broadcast_to([T, NE])).then_inc(gate_in, 16)
            sp.dma_start(iota[:, :], iota_d.broadcast_to([T, NT])).then_inc(gate_in, 16)
            sp.dma_start(tri[:, :, :].rearrange("p a b -> p (a b)"), tri_d.broadcast_to([T, NE * NE])).then_inc(gate_in, 16)
            for b in range(B):
                for h in range(2):
                    sp.wait_ge(unit_out, unit_at[("K", b, 2 * h + 1)] + 1)
                    if b > 0:
                        sp.wait_ge(scores_ok, NSELF + 4 * (b - 1) + 2 * h + 2)
                    for r, half in enumerate((0, 0, 1)):
                        for j in range(4):
                            sp.dma_start(kp[32 * r:32 * r + 32, j, 2 * h:2 * h + 2, :].bitcast(F32),
                                         knat[half][32 * j:32 * j + 32, h, :, :].bitcast(F32)).then_inc(kpacked[h], 16)
                if b + 1 < B:
                    load_q(b + 1) if b == 0 else None
                    if b > 0:
                        sp.wait_ge(scores_ok, NSELF + 4 * b)
                        load_q(b + 1)
            sp.wait_ge(unit_mm, max(unit_at[("K", B - 1, 3)], unit_at[("XV", B - 1, 2)]) + 1)
            sp.dma_start(raw13[0][:, :, :, :], w13_d[NE].rearrange("p (k i f) -> p k i f", k=KD, i=2)).then_inc(sraw_in, 16)
            sp.dma_start(raw2[0][:, :, :], w2_d[NE].rearrange("p (k n) -> p k n", k=2)).then_inc(sraw_in, 16)

            def expert(j):
                return sp.value_load(tmapi[0:1, bass.ds(j, 1)], min_val=0, max_val=NE - 1)

            def load_up(e, i):
                sp.dma_start(raw13[i][:, :, :, :].rearrange("p k i f -> p (k i f)"), w13_f[bass.ds(e * 128, 128), :]).then_inc(raw13_in[i], 16)

            def load_down(e, i):
                sp.dma_start(raw2[i][:, :, :].rearrange("p k n -> p (k n)"), w2_f[bass.ds(e * 128, 128), :]).then_inc(raw2_in[i], 16)

            def load_x(j, i):
                sp.dma_start(xg[:, i, :], xs_d[bass.ds(NR * j, NR), :]).then_inc(xg_in[i], 16)
            sp.wait_ge(tmap_ok, 1)
            sp.wait_ge(s_lo, KD + 1)
            for i in range(2):
                e = expert(i)
                load_up(e, i)
                load_down(e, i)
            sp.wait_ge(scattered, 16 * 2 * B)
            load_x(0, 0)
            load_x(1, 1)

            with sp.Fori(0, NT // 2 - 1) as i:
                for par in range(2):
                    j = 2 * i + par
                    e = expert(j + 2)
                    sp.wait_ge(w13_lo, j + 1)
                    load_up(e, par)
                    sp.wait_ge(xt_mm, j + 1)
                    load_x(j + 2, par)
                    sp.wait_ge(w2_lo, j + 1)
                    load_down(e, par)
            for b in range(B):
                sp.wait_ge(added, b + 1)
                sp.dma_start(out_d[b, :, :], x[:, b, :]).then_inc(stored, 16)
            sp.wait_ge(stored, 16 * B)

        @block.gpsimd
        def _(pool):
            k = [0]

            def own(ins):
                k[0] += 1
                ins.then_inc(pool_step, 1)
                pool.wait_ge(pool_step, k[0])
            own(nc.gpsimd.memset(ident[:, :], 0.0))
            own(nc.gpsimd.affine_select(out=ident[:, :], in_=ident[:, :], compare_op=ALU.not_equal, fill=1.0,
                                        base=0, pattern=[[-1, 128]], channel_multiplier=1))
            own(nc.gpsimd.memset(maskf[:, :, :], 0.0))
            nc.gpsimd.affine_select(out=maskf[:, :, :], in_=maskf[:, :, :], compare_op=ALU.is_ge, fill=MASKED,
                                    base=0, pattern=[[0, 4], [-1, T]], channel_multiplier=1).then_inc(ident_ok, 1)
            pool.wait_ge(const_in, 16 * 7)
            for b in range(B):
                pool.wait_ge(xn_ok, b + 1)
                nc.gpsimd.tensor_tensor(x[:, b, :], x[:, b, :], bout[:, :], ALU.add).then_inc(bias_added, 1)

            def load(i):
                src, cols, hi, lo, waits = pieces[i]
                pool.dma_start(stage[:, i % 2, 0:cols], src).then_inc(stage_in[i % 2], 16)

            def third_norm(b):
                pool.wait_ge(stats_ok, b + 1)
                nc.gpsimd.tensor_scalar(ve[:, b:b + 1], mv[:, b, 1:2], EPS, None, ALU.add).then_inc(late_var, 1)
                pool.wait_ge(late_guess, b + 1)
                c = slice(b, b + 1)
                own(nc.gpsimd.tensor_tensor(t1[:, c], ve[:, c], r0[:, c], ALU.mult))
                own(nc.gpsimd.tensor_tensor(t2[:, c], t1[:, c], r0[:, c], ALU.mult))
                own(nc.gpsimd.tensor_scalar(t3[:, c], t2[:, c], -0.5, 1.5, ALU.mult, ALU.add))
                own(nc.gpsimd.tensor_tensor(rstd[:, c], t3[:, c], r0[:, c], ALU.mult))
                if b >= 2:
                    pool.wait_ge(tp_ok, ring_at[("rows", b - 2)] + 1)
                nc.gpsimd.tensor_scalar(xn_late[:, b % 2, :], x[:, b, :], mv[:, b, 0:1], rstd[:, c],
                                        ALU.subtract, ALU.mult).then_inc(late_xn, 1)

            load(0)
            for i, (src, cols, hi, lo, waits) in enumerate(pieces):
                if i == piece_at[("cx", 2, 0)]:
                    for b in range(B):
                        pool.wait_ge(xn_ok, B + b + 1)
                        nc.gpsimd.tensor_tensor(x[:, b, :], x[:, b, :], xbo[:, :], ALU.add).then_inc(bias_added, 1)
                for b in range(4, B):
                    if i == piece_at[("cx", b, 0)]:
                        third_norm(b - 4)
                if i + 1 < len(pieces):
                    if i > 0:
                        pool.wait_ge(late_split, i)
                    load(i + 1)
                what, value = waits
                if what == "unit":
                    pool.wait_ge(unit_mm, value + 1)
                else:
                    pool.wait_ge(scores_ok, value)
                pool.wait_ge(stage_in[i % 2], 16 * (i // 2 + 1))
                raw = stage[:, i % 2, 0:cols]
                if len(hi.shape) == 4:
                    raw = raw.rearrange("p (a b c) -> p a b c", a=hi.shape[1], b=hi.shape[2])
                else:
                    raw = raw.rearrange("p (a b) -> p a b", a=hi.shape[1])
                own(nc.gpsimd.tensor_copy(hi, raw))
                nc.gpsimd.tensor_tensor(lo, raw, hi, ALU.subtract).then_inc(late_split, 1)
            for b in range(4, B - 1):
                third_norm(b)
            pool.wait_ge(unit_out, unit_at[("XO", B - 1, 0)] + 1)
            own(nc.gpsimd.memset(onesf[:, :], 1.0))
            nc.gpsimd.affine_select(out=trif[:, :], in_=onesf[:, :], compare_op=ALU.is_gt, fill=0.0,
                                    base=0, pattern=[[1, 128]], channel_multiplier=-1).then_inc(tri_made, 1)
            pool.wait_ge(zero_in, 16)
            pool.wait_ge(slots_ok, 1)
            for b in range(B):
                for c in range(2):
                    nc.gpsimd.indirect_dma_start(
                        out=xs_d, out_offset=bass.IndirectOffsetOnAxis(ap=slot_u[:, c, b:b + 1], axis=0),
                        in_=xn3[:, b, :], in_offset=None).then_inc(scattered, 16)

            def w2_low(j, i):
                pool.wait_ge(w2_hi, j + 1)
                nc.gpsimd.tensor_tensor(w2[i][1][:, :, :], raw2[i][:, :, :], w2[i][0][:, :, :], ALU.subtract).then_inc(w2_lo, 1)
            w2_low(0, 0)

            def step(i, last=False):
                for par in range(2):
                    if not (last and par == 1):
                        w2_low(2 * i + par + 1, 1 - par)
            with pool.Fori(0, NT // 2 - 1) as i:
                step(i)
            step(NT // 2 - 1, last=True)
            for i in range(2):
                pool.wait_ge(y_stored[i], 16 * (NT // 2))
            pool.wait_ge(sdn_mm, B)
            for b in range(B):
                for c in range(2):
                    i = (2 * b + c) % 8
                    if b >= 4:
                        pool.wait_ge(added, b - 3)
                    nc.gpsimd.indirect_dma_start(
                        out=gath[i][:, :], out_offset=None, in_=ys_d,
                        in_offset=bass.IndirectOffsetOnAxis(ap=slot_u[:, c, b:b + 1], axis=0)).then_inc(gathered[i], 16)

        @block.scalar
        def _(act):
            nc.scalar.preload_act_table_set("natural_log_exp_and_others")
            for dst, src in ((bqk, bqk_d), (bv, bv_d), (xbq, xbq_d), (xbk, xbk_d), (xbv, xbv_d)):
                act.dma_start(dst[:, :], src).then_inc(const_in, 16)
            act.dma_start(bout[:, :], bout_d.broadcast_to([T, D])).then_inc(const_in, 16)
            act.dma_start(xbo[:, :], xbo_d.broadcast_to([T, D])).then_inc(const_in, 16)

            def std():
                act.wait_ge(var_ok, std.n + 1)
                std.n += 1
                nc.scalar.activation(sd[:, :], ve[:, :], ACT.Ln).then_inc(ln_ok, 1)
                act.wait_ge(ln_ok, std.n)
                nc.scalar.activation(r0[:, :], sd[:, :], ACT.Exp, scale=-0.5).then_inc(sdev_ok, 1)
            std.n = 0

            def late_std(b):
                act.wait_ge(late_var, b + 1)
                nc.scalar.activation(sd[:, b:b + 1], ve[:, b:b + 1], ACT.Ln).then_inc(late_ln, 1)
                act.wait_ge(late_ln, b + 1)
                nc.scalar.activation(r0[:, b:b + 1], sd[:, b:b + 1], ACT.Exp, scale=-0.5).then_inc(late_guess, 1)

            def third_high(b):
                act.wait_ge(tp_ok, ring_at[("rows", b)] + 1)
                src, dst = rows_io(b)
                nc.scalar.activation(dst[0], src, ACT.Copy).then_inc(pt_hi, 1)

            def unit_high(u):
                kind, a, b = u
                if kind in ("O", "XO"):
                    return
                i = unit_at[u]
                act.wait_ge(unit_mm, i + 1)
                src, dst, bias = unit_io(u)
                if kind == "QK" and a >= 1:
                    act.wait_ge(packed[(a - 1) % 2], 16 * 24 * ((a - 1) // 2 + 1))
                if kind == "V" and a >= 2:
                    act.wait_ge(pv_ok, 8 * (a - 1))
                if kind == "Q" and a >= 2:
                    act.wait_ge(q_stored[a % 2], 64 * (a // 2))
                if kind == "K" and a >= 1:
                    act.wait_ge(kpacked[b // 2], 16 * 12 * a)
                if kind == "XV":
                    act.wait_ge(pv_ok, NSELF + 4 * (a - 1))
                if bias is None:
                    nc.scalar.activation(dst[0], src, ACT.Copy).then_inc(unit_hi, 1)
                else:
                    nc.scalar.activation(dst[0], src, ACT.Identity, bias=bias).then_inc(unit_hi, 1)

            def tail_high(n, chunks):
                for c in chunks:
                    ci = chunk(n, c)
                    kc = T if n < NSELF else KEYS[c]
                    act.wait_ge(tp_ok, ci + 1)
                    if n == 0:
                        act.wait_ge(zero_in, 16)
                    if n > 0:
                        act.wait_ge(pv_ok, n)
                    nc.scalar.activation(PT[0][0:kc, c, :], bank[4 + ci % 2][0:kc, 0:4 * T], ACT.Copy).then_inc(pt_hi, 1)

            def exps(n):
                act.wait_ge(negmax_ok, n + 1)
                if n > 0:
                    act.wait_ge(tp_ok, chunk(n - 1) + nchunks(n - 1))
                for j in range(4):
                    src = score_ap(n)[:, j, :]
                    last = nc.scalar.activation(P[:, j, 0:src.shape[-1]], src, ACT.Exp, bias=nb[:, j:j + 1],
                                                scale=SCALE, accum_out=rs[:, n % 2, j:j + 1])
                last.then_inc(exp_ok, 1)

            def heads_out(n):
                bias = bv if n < NSELF else xbv
                g = n % NG
                act.wait_ge(pv_ok, n + 1)
                if g == 0 and n > 0:
                    act.wait_ge(o_split, n // NG)
                for j in range(4):
                    last = nc.scalar.activation(oT[32 * j:32 * j + 32, g, :], bank[6][32 * j:32 * j + 32, T * j:T * (j + 1)],
                                                ACT.Identity, bias=bias[32 * j:32 * j + 32, g:g + 1])
                last.then_inc(o_out, 1)

            def shared_high(k):
                act.wait_ge(sraw_in, 32)
                for i in range(2 * k, min(2 * k + 2, KD + 1)):
                    dst, src = shared_piece(i, 0)
                    if i == KD:
                        act.wait_ge(kpacked[1], 16 * 12 * B)
                    nc.scalar.activation(dst, src, ACT.Copy).then_inc(s_hi, 1)

            std()
            for i in range(8):
                act.wait_ge(araw_in[i], 16)
                raw, halves = whole(i)
                nc.scalar.activation(halves[0], raw, ACT.Copy).then_inc(split_hi, 1)
            act.wait_ge(const_in, 16 * 7)
            for u in prologue:
                unit_high(u)
            for first, slots in ((0, self_slots), (NSELF, cross_slots)):
                for s, (ua, ub) in enumerate(slots):
                    n = first + s
                    if s > 0:
                        tail_high(n - 1, range(nchunks(n - 1))[0:2])
                    if first > 0 and x3_row(s) is not None:
                        late_std(x3_row(s))
                    for u in ua:
                        unit_high(u)
                    if s > 0 and nchunks(n - 1) > 2:
                        tail_high(n - 1, [2])
                    if s < NSELF:
                        exps(n)
                    if s > 0:
                        heads_out(n - 1)
                    if first > 0 and x3_row(s) is not None:
                        third_high(x3_row(s))
                    if first > 0 and s >= NSELF - 3:
                        shared_high(s - (NSELF - 3))
                    for u in ub:
                        unit_high(u)
                if first == 0:
                    std()
                    for u in boundary:
                        unit_high(u)
            std()
            act.wait_ge(gate_mm, 1)
            nc.scalar.activation(lgT[:, 0:4 * T], bank[2][0:NE, 0:4 * T], ACT.Copy)
            nc.scalar.activation(lgT[:, 4 * T:7 * T], bank[3][0:NE, 0:3 * T], ACT.Copy).then_inc(gate_out, 1)
            third_high(B - 1)
            act.wait_ge(logits_ok, 1)
            nc.scalar.activation(rt["sc"][:, :, :], rt["lg"][:, :, :], ACT.Exp).then_inc(gexp, 1)
            for c in range(4):
                half, it = divmod(c, 2)
                act.wait_ge(sup_mm, c + 1)
                if c >= 2:
                    act.wait_ge(sh_ok, c - 1)
                nc.scalar.activation(sg[:, c % 2, :], bank[2 * (c % 2)][:, 0:4 * T], ACT.Silu).then_inc(ssilu, 1)
                act.wait_ge(sh_ok, c + 1)
                nc.scalar.activation(hS[0][:, it, 4 * T * half:4 * T * (half + 1)], hf[:, c % 2, :], ACT.Copy).then_inc(sh_hi, 1)

            def w13_high(i, turn):
                act.wait_ge(raw13_in[i], 16 * turn)
                nc.scalar.activation(w13[i][0][:, :, :], raw13[i][:, :, :, :].rearrange("p k i f -> p k (i f)"),
                                     ACT.Copy).then_inc(w13_hi, 1)

            def rows_high(j):
                act.wait_ge(xt_mm, j + 1)
                nc.scalar.activation(xgT[0][:, :, :], bank[2][:, :].rearrange("p (k t) -> p k t", k=KD), ACT.Copy).then_inc(xt_hi, 1)
            w13_high(0, 1)
            w13_high(1, 1)
            rows_high(0)

            def y_high(j, i, stores=None):
                act.wait_ge(down_mm, j + 1)
                if stores is not None:
                    act.wait_ge(y_stored[i], 16 * stores)
                nc.scalar.activation(y_tile[:, i, :], bank[4 + i][:, :], ACT.Copy).then_inc(y_out, 1)
                act.wait_ge(y_out, j + 1)
                act.dma_start(ys_d[bass.ds(NR * j, NR), :], y_tile[:, i, :]).then_inc(y_stored[i], 16)

            def step(i, first=False, second=False, last=False):
                for par in range(2):
                    j = 2 * i + par
                    act.wait_ge(up_mm, j + 1)
                    if not first:
                        act.wait_ge(h_ok, j - 1)
                    nc.scalar.activation(s_tile[:, par, :], bank[par][:, 0:FI], ACT.Silu).then_inc(silu_ok, 1)
                    if not (last and par == 1):
                        rows_high(j + 1)
                    if not (first and par == 0):
                        y_high(j - 1, 1 - par, None if first or (second and par == 0) else i + par - 1)
                    act.wait_ge(ht_mm, j + 1)
                    if not (first and par == 0):
                        act.wait_ge(down_mm, j)
                    nc.scalar.activation(hTt[0][:, :, :], bank[3][:, 0:FI].rearrange("p (k t) -> p k t", k=2),
                                         ACT.Copy).then_inc(ht_hi, 1)
                    if not last:
                        w13_high(par, i + 2)
            step(0, first=True)
            step(1, second=True)
            with act.Fori(2, NT // 2 - 1) as i:
                step(i)
            step(NT // 2 - 1, last=True)
            y_high(NT - 1, 1, NT // 2 - 1)

        @block.vector
        def _(dve):
            k = [0]

            def own(ins):
                k[0] += 1
                ins.then_inc(dve_step, 1)
                dve.wait_ge(dve_step, k[0])

            def stats(b0, b1):
                for b in range(b0, b1):
                    last = nc.vector.bn_stats(st[:, b, :], x[:, b, :])
                own(last)
                for b in range(b0, b1):
                    last = nc.vector.bn_aggr(mv[:, b, :], st[:, b, :])
                own(last)
                nc.vector.tensor_scalar(ve[:, b0:b1], mv[:, b0:b1, 1], EPS, None, ALU.add).then_inc(var_ok, 1)
                stats.n += 1

            def third_stats(b):
                own(nc.vector.bn_stats(st[:, b, :], x[:, b, :]))
                nc.vector.bn_aggr(mv[:, b, :], st[:, b, :]).then_inc(stats_ok, 1)

            def third_low(b):
                dve.wait_ge(pt_hi, ring_at[("rows", b)] + 1)
                src, dst = rows_io(b)
                nc.vector.tensor_tensor(dst[1], src, dst[0], ALU.subtract).then_inc(pt_lo, 1)

            def newton(b0, b1):
                c = slice(b0, b1)
                dve.wait_ge(sdev_ok, stats.n)
                own(nc.vector.tensor_tensor(t1[:, c], ve[:, c], r0[:, c], ALU.mult))
                own(nc.vector.tensor_tensor(t2[:, c], t1[:, c], r0[:, c], ALU.mult))
                own(nc.vector.tensor_scalar(t3[:, c], t2[:, c], -0.5, 1.5, ALU.mult, ALU.add))
                own(nc.vector.tensor_tensor(rstd[:, c], t3[:, c], r0[:, c], ALU.mult))
            stats.n = 0

            def normalise(i):
                u = x_units[i]
                b = 2 * u[1] + u[2]
                if i >= 2:
                    dve.wait_ge(unit_mm, unit_at[x_units[i - 2]] + 1)
                nc.vector.tensor_scalar(xn_tile(i), x[:, b, :], mv[:, b, 0:1], rstd[:, b:b + 1],
                                        ALU.subtract, ALU.mult).then_inc(xn_ok, 1)

            def unit_low(u):
                kind, a, b = u
                i = unit_at[u]
                if kind in ("O", "XO"):
                    dve.wait_ge(unit_mm, i + 1)
                    dve.wait_ge(bias_added, a + 1 + (B if kind == "XO" else 0))
                    nc.vector.tensor_tensor(x[:, a, :], bank[ubank[i]][0:T, :], x[:, a, :], ALU.add).then_inc(unit_out, 1)
                    return
                src, dst, bias = unit_io(u)
                dve.wait_ge(unit_hi, hi_at[u] + 1)
                if bias is None:
                    nc.vector.tensor_tensor(dst[1], src, dst[0], ALU.subtract).then_inc(unit_out, 1)
                else:
                    nc.vector.scalar_tensor_tensor(dst[1], src, bias, dst[0], ALU.add, ALU.subtract).then_inc(unit_out, 1)
                if u in xn_at:
                    nxt = xn_at[u] + 2
                    if nxt < len(x_units) and x_units[nxt][0] == kind:
                        normalise(nxt)

            def rowmax(n):
                dve.wait_ge(scores_ok, n + 1)
                own(nc.vector.tensor_reduce(mx[:, :], score_ap(n), AX.X, ALU.max))
                if n > 0:
                    dve.wait_ge(exp_ok, n)
                nc.vector.tensor_scalar(nb[:, :], mx[:, :], -SCALE, None, ALU.mult).then_inc(negmax_ok, 1)

            def tail_low(n, chunks):
                for c in chunks:
                    ci = chunk(n, c)
                    kc = T if n < NSELF else KEYS[c]
                    dve.wait_ge(pt_hi, ci + 1)
                    nc.vector.tensor_tensor(PT[1][0:kc, c, :], bank[4 + ci % 2][0:kc, 0:4 * T], PT[0][0:kc, c, :],
                                            ALU.subtract).then_inc(pt_lo, 1)

            def norm_probs(n):
                dve.wait_ge(exp_ok, n + 1)
                own(nc.vector.reciprocal(rr[:, :], rs[:, n % 2, :]))
                width = T if n < NSELF else S
                for j in range(4):
                    last = nc.vector.tensor_scalar(P[:, j, 0:width], P[:, j, 0:width], rr[:, j:j + 1], None, ALU.mult)
                last.then_inc(probs_ok, 1)

            def heads_split(n):
                b = n // NG
                dve.wait_ge(o_out, n + 1)
                if b > 0:
                    prev = ("O", b - 1, 0) if b <= B else ("XO", b - 1 - B, 0)
                    dve.wait_ge(unit_mm, unit_at[prev] + 1)
                own(nc.vector.tensor_copy(oTs[0][:, :, :], oT[:, :, :]))
                nc.vector.tensor_tensor(oTs[1][:, :, :], oT[:, :, :], oTs[0][:, :, :], ALU.subtract).then_inc(o_split, 1)

            def shared_low(k):
                for i in range(2 * k, min(2 * k + 2, KD + 1)):
                    dve.wait_ge(s_hi, i + 1)
                    dst, src = shared_piece(i, 1)
                    nc.vector.tensor_tensor(dst, src, shared_piece(i, 0)[0], ALU.subtract).then_inc(s_lo, 1)

            dve.wait_ge(x_in, 16)
            stats(0, B)
            newton(0, B)
            normalise(0)
            normalise(1)
            dve.wait_ge(ident_ok, 1)
            nc.vector.tensor_copy(identr[:, :], ident[0:T, 0:T])
            nc.vector.tensor_copy(maskr[:, :, :], maskf[:, :, :]).then_inc(consts_ok, 1)
            nc.vector.memset(zeros[:, :], 0.0).then_inc(zero_made, 1)
            for i in range(8):
                dve.wait_ge(split_hi, i + 1)
                raw, halves = whole(i)
                nc.vector.tensor_tensor(halves[1], raw, halves[0], ALU.subtract).then_inc(split_lo, 1)
            dve.wait_ge(const_in, 16 * 7)
            for u in prologue:
                unit_low(u)
            for first, slots in ((0, self_slots), (NSELF, cross_slots)):
                for s, (ua, ub) in enumerate(slots):
                    n = first + s
                    if s < NSELF and first == 0:
                        rowmax(n)
                    if s > 0:
                        tail_low(n - 1, range(nchunks(n - 1))[0:2])
                    if s < NSELF and first > 0:
                        rowmax(n)
                    for u in ua:
                        unit_low(u)
                    if s > 0 and nchunks(n - 1) > 2:
                        tail_low(n - 1, [2])
                    if s < NSELF:
                        norm_probs(n)
                    if s > 0 and (n - 1) % NG == 3:
                        heads_split(n - 1)
                    if first > 0 and x3_row(s) is not None:
                        third_low(x3_row(s))
                    if first > 0 and s >= NSELF - 3:
                        shared_low(s - (NSELF - 3))
                    for u in ub:
                        unit_low(u)
                        if u[0] == "XO":
                            dve.wait_ge(unit_out, unit_at[u] + 1)
                            third_stats(u[1])
                if first == 0:
                    unit_low(boundary[0])
                    dve.wait_ge(unit_out, unit_at[boundary[0]] + 1)
                    stats(0, B)
                    newton(0, B)
                    normalise(B)
                    normalise(B + 1)
                    for u in boundary[1:]:
                        unit_low(u)
                    dve.wait_ge(gate_in, 64)
                    own(nc.vector.tensor_copy(gwr[0][:, :, :], gw[:, :, :]))
                    nc.vector.tensor_tensor(gwr[1][:, :, :], gw[:, :, :], gwr[0][:, :, :], ALU.subtract).then_inc(route_c, 1)
            def keep_rows(b0, b1):
                for b in range(b0, b1):
                    nc.vector.tensor_scalar(xn3[:, b, :], x[:, b, :], mv[:, b, 0:1], rstd[:, b:b + 1],
                                            ALU.subtract, ALU.mult)
            dve.wait_ge(late_xn, B - 1)
            dve.wait_ge(pv_ok, 2 * NSELF)
            keep_rows(0, 2)
            unit_low(last_o[0])
            dve.wait_ge(unit_out, unit_at[last_o[0]] + 1)
            stats(B - 1, B)
            dve.wait_ge(tri_made, 1)
            nc.vector.tensor_copy(beforer[:, :], trif[:, :])
            nc.vector.tensor_copy(onesr[:, :], onesf[:, :]).then_inc(tri_ok, 1)
            newton(B - 1, B)
            nc.vector.tensor_scalar(xn_late[:, (B - 1) % 2, :], x[:, B - 1, :], mv[:, B - 1, 0:1], rstd[:, B - 1:B],
                                    ALU.subtract, ALU.mult).then_inc(xn_ok, 1)
            keep_rows(2, 5)
            third_low(B - 1)
            keep_rows(5, B)

            def wide(ap):
                return ap.unsqueeze(2).to_broadcast([T, B, NE])
            v_ = nc.vector
            iob = iota[:, 0:NE].unsqueeze(1).to_broadcast([T, B, NE])
            dve.wait_ge(router_mm, 1)
            lgp = bank[4][0:T, 0:B * NE].rearrange("p (b e) -> p b e", e=NE)
            own(v_.tensor_reduce(sm["gmx"][:, :], lgp, AX.X, ALU.max))
            v_.tensor_tensor(rt["lg"][:, :, :], lgp, wide(sm["gmx"][:, :]), ALU.subtract).then_inc(logits_ok, 1)
            dve.wait_ge(gexp, 1)
            own(v_.tensor_reduce(sm["gsm"][:, :], rt["sc"][:, :, :], AX.X, ALU.add))
            own(v_.reciprocal(sm["grc"][:, :], sm["gsm"][:, :]))
            own(v_.tensor_tensor(rt["prob"][:, :, :], rt["sc"][:, :, :], wide(sm["grc"][:, :]), ALU.mult))
            own(v_.tensor_tensor(rt["bi"][:, :, :], rt["prob"][:, :, :],
                                 gbias[:, :].unsqueeze(1).to_broadcast([T, B, NE]), ALU.add))
            for src, top, lt, cand, ix, m in (("bi", "top0", "lt", "cand", "ix0", "m0"),
                                              ("bi2", "top1", "lt2", "cand2", "ix1", "m1")):
                if src == "bi2":
                    own(v_.scalar_tensor_tensor(rt["bi2"][:, :, :], rt["m0"][:, :, :], MASKED, rt["bi"][:, :, :],
                                                ALU.mult, ALU.add))
                own(v_.tensor_reduce(sm[top][:, :], rt[src][:, :, :], AX.X, ALU.max))
                own(v_.tensor_tensor(rt[lt][:, :, :], rt[src][:, :, :], wide(sm[top][:, :]), ALU.is_lt))
                own(v_.scalar_tensor_tensor(rt[cand][:, :, :], rt[lt][:, :, :], float(NE), iob, ALU.mult, ALU.add))
                own(v_.tensor_reduce(sm[ix][:, :], rt[cand][:, :, :], AX.X, ALU.min))
                own(v_.tensor_tensor(rt[m][:, :, :], iob, wide(sm[ix][:, :]), ALU.is_equal))
            v_.tensor_tensor(selr[:, :, :], rt["m0"][:, :, :], rt["m1"][:, :, :], ALU.add).then_inc(sel_ok, 1)
            dve.wait_ge(cum_mm, 1)
            rank = bank[6][0:T, 0:B * NE].rearrange("p (b e) -> p b e", e=NE)
            count = bank[6][0:T, B * NE:(B + 1) * NE]
            own(v_.scalar_tensor_tensor(over[:, :, :], iob, float(NR), wide(count), ALU.mult, ALU.is_lt))
            own(v_.tensor_reduce(sm["ntile"][:, :], over[:, :, :], AX.X, ALU.add))
            own(v_.tensor_tensor(rt["below"][:, :, :], tri[:, :, :], sm["ntile"][:, :].unsqueeze(1).to_broadcast([T, NE, NE]),
                                 ALU.mult))
            own(v_.tensor_reduce(sm["tstart"][:, :], rt["below"][:, :, :], AX.X, ALU.add))
            own(v_.scalar_tensor_tensor(rt["slots"][:, :, :], sm["tstart"][:, :].unsqueeze(1).to_broadcast([T, B, NE]),
                                        float(NR), rank, ALU.mult, ALU.add))
            v_.tensor_tensor(rt["ms0"][:, :, :], rt["m0"][:, :, :], rt["slots"][:, :, :], ALU.mult)
            own(v_.tensor_tensor(rt["ms1"][:, :, :], rt["m1"][:, :, :], rt["slots"][:, :, :], ALU.mult))
            v_.tensor_reduce(sm["s0f"][:, :], rt["ms0"][:, :, :], AX.X, ALU.add)
            own(v_.tensor_reduce(sm["s1f"][:, :], rt["ms1"][:, :, :], AX.X, ALU.add))
            v_.tensor_copy(slot_u[:, 0, :], sm["s0f"][:, :])
            v_.tensor_copy(slot_u[:, 1, :], sm["s1f"][:, :]).then_inc(slots_ok, 1)
            own(v_.tensor_tensor(sm["tend"][:, :], sm["tstart"][:, :], sm["ntile"][:, :], ALU.add))
            own(v_.tensor_tensor(tmap[:, :, :], sm["tend"][0:1, :].unsqueeze(1).to_broadcast([1, NT, NE]),
                                 iota[0:1, :].unsqueeze(2).to_broadcast([1, NT, NE]), ALU.is_le))
            own(v_.tensor_reduce(tmapf[:, :], tmap[:, :, :], AX.X, ALU.add))
            own(v_.tensor_scalar(tmapc[:, :], tmapf[:, :], float(NE - 1), None, ALU.min))
            v_.tensor_copy(tmapi[:, :], tmapc[:, :]).then_inc(tmap_ok, 1)
            v_.tensor_tensor(rt["mw0"][:, :, :], rt["m0"][:, :, :], rt["prob"][:, :, :], ALU.mult)
            own(v_.tensor_tensor(rt["mw1"][:, :, :], rt["m1"][:, :, :], rt["prob"][:, :, :], ALU.mult))
            v_.tensor_reduce(sm["wt0"][:, :], rt["mw0"][:, :, :], AX.X, ALU.add)
            own(v_.tensor_reduce(sm["wt1"][:, :], rt["mw1"][:, :, :], AX.X, ALU.add))

            for c in range(4):
                half, it = divmod(c, 2)
                dve.wait_ge(ssilu, c + 1)
                if c >= 2:
                    dve.wait_ge(sh_hi, c - 1)
                nc.vector.tensor_tensor(hf[:, c % 2, :], bank[2 * (c % 2) + 1][:, 0:4 * T], sg[:, c % 2, :],
                                        ALU.mult).then_inc(sh_ok, 1)
                dve.wait_ge(sh_hi, c + 1)
                span = slice(4 * T * half, 4 * T * (half + 1))
                nc.vector.tensor_tensor(hS[1][:, it, span], hf[:, c % 2, :], hS[0][:, it, span], ALU.subtract).then_inc(sh_lo, 1)
            def w13_low(j, i):
                dve.wait_ge(w13_hi, j + 1)
                nc.vector.tensor_tensor(w13[i][1][:, :, :], raw13[i][:, :, :, :].rearrange("p k i f -> p k (i f)"),
                                        w13[i][0][:, :, :], ALU.subtract).then_inc(w13_lo, 1)

            def w2_high(i, turn):
                dve.wait_ge(raw2_in[i], 16 * turn)
                nc.vector.tensor_copy(w2[i][0][:, :, :], raw2[i][:, :, :]).then_inc(w2_hi, 1)

            def rows_low(j):
                dve.wait_ge(xt_hi, j + 1)
                nc.vector.tensor_tensor(xgT[1][:, :, :], bank[2][:, :].rearrange("p (k t) -> p k t", k=KD), xgT[0][:, :, :],
                                        ALU.subtract).then_inc(xt_lo, 1)
            w13_low(0, 0)
            w2_high(0, 1)
            for b in range(B):
                dve.wait_ge(sdn_mm, b + 1)
                nc.vector.tensor_tensor(x[:, b, :], bank[4 + b % 3][0:T, :], x[:, b, :], ALU.add).then_inc(sdn_out, 1)
            rows_low(0)

            def step(i, first=False, last=False):
                for par in range(2):
                    j = 2 * i + par
                    if not (last and par == 1):
                        w13_low(j + 1, 1 - par)
                    dve.wait_ge(silu_ok, j + 1)
                    if not first:
                        dve.wait_ge(ht_mm, j - 1)
                    nc.vector.tensor_tensor(h_tile[:, par, :], bank[par][:, FI:2 * FI], s_tile[:, par, :], ALU.mult).then_inc(h_ok, 1)
                    if not (last and par == 1):
                        rows_low(j + 1)
                        if not (first and par == 0):
                            dve.wait_ge(down_mm, j)
                        w2_high(1 - par, i + 1 + par)
                    dve.wait_ge(ht_hi, j + 1)
                    nc.vector.tensor_tensor(hTt[1][:, :, :], bank[3][:, 0:FI].rearrange("p (k t) -> p k t", k=2),
                                            hTt[0][:, :, :], ALU.subtract).then_inc(ht_lo, 1)
            step(0, first=True)
            with dve.Fori(1, NT // 2 - 1) as i:
                step(i)
            step(NT // 2 - 1, last=True)
            for b in range(B):
                i = (2 * b) % 8
                dve.wait_ge(gathered[i], 16 * (b // 4 + 1))
                own(nc.vector.scalar_tensor_tensor(x[:, b, :], gath[i][:, :], sm["wt0"][:, b:b + 1], x[:, b, :], ALU.mult, ALU.add))
                dve.wait_ge(gathered[i + 1], 16 * (b // 4 + 1))
                nc.vector.scalar_tensor_tensor(x[:, b, :], gath[i + 1][:, :], sm["wt1"][:, b:b + 1], x[:, b, :],
                                               ALU.mult, ALU.add).then_inc(added, 1)

        @block.tensor
        def _(pe):
            def product(out, lhs, rhs, first=True, last=True):
                for t in range(product.tiles):
                    for i, (s, m) in enumerate(PASSES):
                        ins = nc.tensor.matmul(out, lhs(s, t), rhs(m, t), start=first and t == 0 and i == 0,
                                               stop=last and t == product.tiles - 1 and i == 2)
                return ins
            product.tiles = KD

            def unit(u):
                kind, a, b = u
                i = unit_at[u]
                bk = bank[ubank[i]]
                if prev_user[i] is not None:
                    pe.wait_ge(unit_out, prev_user[i] + 1)
                if kind in ("X", "X2"):
                    pe.wait_ge(xn_ok, xn_at[u] + 1)
                    if xn_at[u] == 0:
                        pe.wait_ge(ident_ok, 1)
                    for t in range(KD):
                        last = nc.tensor.transpose(bk[:, T * t:T * (t + 1)],
                                                   xn_tile(xn_at[u])[:, 128 * t:128 * (t + 1)],
                                                   ident[0:T, 0:T])
                elif kind == "QK":
                    pe.wait_ge(unit_out, unit_at[("X", a, 1)] + 1)
                    pe.wait_ge(split_lo, b // 2 + 1)
                    last = product(bk[:, 0:2 * T], lambda h, t: wqk[h][:, b, t, :], lambda h, t: xnT[h][:, t, :])
                elif kind == "V":
                    pe.wait_ge(unit_out, unit_at[("X", a, 1)] + 1)
                    pe.wait_ge(split_lo, 6)
                    last = product(bk[0:T, :], lambda h, t: xnT[h][:, t, T * b:T * (b + 1)], lambda h, t: wv[h][:, t, :])
                elif kind in ("O", "XO"):
                    w = wout if kind == "O" else xwo
                    pe.wait_ge(o_split, a + 1 + (B if kind == "XO" else 0))
                    if kind == "O":
                        pe.wait_ge(split_lo, 8)
                    else:
                        pe.wait_ge(late_split, piece_at[("wo", 1)] + 1)
                    last = product(bk[0:T, :], lambda h, t: oTs[h][:, t, :], lambda h, t: w[h][:, t, :])
                elif kind == "Q":
                    pe.wait_ge(unit_out, unit_at[("X2", a, 1)] + 1)
                    pe.wait_ge(late_split, piece_at[("wq", b // 2)] + 1)
                    last = product(bk[:, 0:2 * T], lambda h, t: xwq[h][:, b, t, :], lambda h, t: xnT[h][:, t, :])
                elif kind == "K":
                    pe.wait_ge(late_split, max(piece_at[("cx", a, 1)], piece_at[("wk", 1)]) + 1)
                    last = product(bk[:, 0:SP], lambda h, t: xwk[h][:, b, t, :], lambda h, t: cx[h][:, a % 2, t, :])
                elif kind == "XV":
                    pe.wait_ge(late_split, max(piece_at[("cx", a, 1)], piece_at[("wv", 1)]) + 1)
                    last = product(bk[0:KEYS[b], :], lambda h, t: cx[h][:, a % 2, t, 128 * b:128 * b + KEYS[b]],
                                   lambda h, t: xwv[h][:, t, :])
                last.then_inc(unit_mm, 1)

            def scores(n):
                if n < NSELF:
                    p, i = divmod(n // NG, 2)
                    g = n % NG
                    pe.wait_ge(packed[p % 2], 16 * 24 * (p // 2 + 1))
                    if n >= 2:
                        pe.wait_ge(exp_ok, n - 1)
                    if n == 0:
                        pe.wait_ge(consts_ok, 1)
                    out = bank[n % 2][0:T, 0:4 * T].rearrange("p (j t) -> p j t", j=4)
                    nc.tensor.matmul(bank[n % 2][0:T, 0:4 * T], identr[:, :], maskr[:, :, :].rearrange("p j t -> p (j t)"),
                                     start=True, stop=False)
                    for j in range(4):
                        last = nc.tensor.matmul(out[:, j, :], pq[p % 2][:, j, g, T * i:T * (i + 1)],
                                                pk[p % 2][:, j, g, T * i:T * (i + 1)], start=False, stop=j == 3)
                else:
                    b, g = divmod(n - NSELF, NG)
                    pe.wait_ge(q_loaded[b % 2], 16 * 3 * (b // 2 + 1))
                    pe.wait_ge(kpacked[g // 2], 16 * 12 * (b + 1))
                    pe.wait_ge(exp_ok, n)
                    if n == NSELF:
                        pe.wait_ge(unit_out, first_cross)
                    for j in range(4):
                        last = nc.tensor.matmul(bank[j][0:T, 0:SP], qp[:, b % 2, j, g, :], kp[:, j, g, :], start=True, stop=True)
                last.then_inc(scores_ok, 1)

            def transposes(n, chunks):
                for c in chunks:
                    ci = chunk(n, c)
                    kc = T if n < NSELF else KEYS[c]
                    pe.wait_ge(probs_ok, n + 1)
                    if ci >= 2:
                        pe.wait_ge(pt_lo, ci - 1)
                    for j in range(4):
                        last = nc.tensor.transpose(bank[4 + ci % 2][0:kc, T * j:T * (j + 1)], P[:, j, 128 * c:128 * c + kc],
                                                   ident[0:T, 0:T])
                    last.then_inc(tp_ok, 1)

            def third_rows(b):
                i = ring_at[("rows", b)]
                if b < B - 1:
                    pe.wait_ge(late_xn, b + 1)
                else:
                    pe.wait_ge(xn_ok, 2 * B + 1)
                pe.wait_ge(pt_lo, i - 1)
                for t in range(KD):
                    last = nc.tensor.transpose(bank[4 + i % 2][:, T * t:T * (t + 1)],
                                               xn_late[:, b % 2, 128 * t:128 * (t + 1)], ident[0:T, 0:T])
                last.then_inc(tp_ok, 1)

            def values(n):
                if n > 0:
                    pe.wait_ge(o_out, n)
                g = n % NG
                buf, c0 = vslot(n)
                steps = [(c, s, m) for c in range(nchunks(n)) for s, m in PASSES]
                for i, (c, s, m) in enumerate(steps):
                    kc = T if n < NSELF else KEYS[c]
                    if i % 3 == 0:
                        pe.wait_ge(pt_lo, chunk(n, c) + 1)
                    last = nc.tensor.matmul(bank[6][:, 0:4 * T], v[s][0:kc, buf, c0 + c, 128 * g:128 * (g + 1)],
                                            PT[m][0:kc, c, :], start=i == 0, stop=i == len(steps) - 1)
                last.then_inc(pv_ok, 1)

            def v_ready(n):
                if n < NSELF:
                    b = n // NG
                    pe.wait_ge(unit_out, unit_at[("V", b // 2, b % 2)] + 1)
                else:
                    pe.wait_ge(unit_out, unit_at[("XV", (n - NSELF) // NG, 2)] + 1)

            for u in prologue:
                unit(u)
            for first, slots in ((0, self_slots), (NSELF, cross_slots)):
                for s, (ua, ub) in enumerate(slots):
                    n = first + s
                    if s < NSELF:
                        scores(n)
                    if s > 0:
                        transposes(n - 1, range(nchunks(n - 1))[0:2])
                    for u in ua:
                        unit(u)
                    if s > 0:
                        if nchunks(n - 1) > 2:
                            transposes(n - 1, [2])
                        if (n - 1) % NG == 0:
                            v_ready(n - 1)
                        values(n - 1)
                    if first > 0 and x3_row(s) is not None:
                        third_rows(x3_row(s))
                    for u in ub:
                        unit(u)
                if first == 0:
                    for u in boundary:
                        unit(u)
            for u in last_o:
                unit(u)

            pe.wait_ge(route_c, 1)
            pe.wait_ge(pt_lo, ring_at[("rows", B - 2)] + 1)
            pe.wait_ge(exp_ok, 2 * NSELF)
            for out, c0, c1 in ((bank[2], 0, 4), (bank[3], 4, 7)):
                last = product(out[0:NE, 0:T * (c1 - c0)], lambda h, t: gwr[h][:, t, :],
                               lambda h, t: fx[h][:, t, T * c0:T * c1])
            last.then_inc(gate_mm, 1)

            def shared_up(c):
                half, it = divmod(c, 2)
                if c >= 2:
                    pe.wait_ge(sh_ok, c - 1)
                for w in range(2):
                    last = product(bank[2 * (c % 2) + w][:, 0:4 * T], lambda h, t: sw13[h][:, t, w, 128 * it:128 * (it + 1)],
                                   lambda h, t: fx[h][:, t, 4 * T * half:4 * T * (half + 1)])
                last.then_inc(sup_mm, 1)

            third_rows(B - 1)
            pe.wait_ge(gate_out, 1)
            for b in range(B - 1):
                nc.tensor.transpose(bank[4][0:T, NE * b:NE * (b + 1)], lgT[:, T * b:T * (b + 1)], ident[0:NE, 0:NE])
            pe.wait_ge(pt_lo, len(ring))
            product(bank[4][0:T, NE * (B - 1):NE * B], lambda h, t: fx[h][:, t, T * (B - 1):T * B],
                    lambda h, t: gwr[h][:, t, :]).then_inc(router_mm, 1)

            pe.wait_ge(s_lo, KD + 1)
            shared_up(0)
            pe.wait_ge(sel_ok, 1)
            pe.wait_ge(tri_ok, 1)
            nc.tensor.matmul(bank[6][:, 0:B * NE], beforer[:, :], selr[:, :, :].rearrange("p b e -> p (b e)"),
                             start=True, stop=False)
            for d in range(1, B):
                nc.tensor.matmul(bank[6][:, NE * d:NE * B], onesr[:, :], selr[:, 0:B - d, :].rearrange("p b e -> p (b e)"),
                                 start=False, stop=d == B - 1)
            for b in range(B):
                last = nc.tensor.matmul(bank[6][:, NE * B:NE * (B + 1)], onesr[:, :], selr[:, b, :],
                                        start=b == 0, stop=b == B - 1)
            last.then_inc(cum_mm, 1)
            for c in range(1, 4):
                shared_up(c)
            pe.wait_ge(sh_lo, 4)
            pe.wait_ge(slots_ok, 1)
            product.tiles = 2
            for b in range(B):
                if b >= 3:
                    pe.wait_ge(sdn_out, b - 2)
                product(bank[4 + b % 3][0:T, :], lambda h, t: hS[h][:, t, T * b:T * (b + 1)],
                        lambda h, t: sw2[h][:, t, :]).then_inc(sdn_mm, 1)
            product.tiles = KD
            pe.wait_ge(sdn_out, B)

            def rows(j, i, turn, first=False):
                pe.wait_ge(xg_in[i], 16 * turn)
                if not first:
                    pe.wait_ge(xt_lo, j)
                for t in range(KD):
                    last = nc.tensor.transpose(bank[2][:, 128 * t:128 * (t + 1)], xg[:, i, 128 * t:128 * (t + 1)], ident[:, :])
                last.then_inc(xt_mm, 1)
            rows(0, 0, 1, first=True)

            def down(j, i):
                pe.wait_ge(ht_lo, j + 1)
                pe.wait_ge(w2_lo, j + 1)
                product.tiles = 2
                product(bank[4 + i][:, :], lambda h, t: hTt[h][:, t, :], lambda h, t: w2[i][h][:, t, :]).then_inc(down_mm, 1)
                product.tiles = KD

            def step(i, first=False, second=False, last=False):
                for par in range(2):
                    j = 2 * i + par
                    pe.wait_ge(w13_lo, j + 1)
                    pe.wait_ge(xt_lo, j + 1)
                    if not first:
                        pe.wait_ge(h_ok, j - 1)
                    product(bank[par][:, :], lambda h, t: xgT[h][:, t, :], lambda h, t: w13[par][h][:, t, :]).then_inc(up_mm, 1)
                    if not (last and par == 1):
                        rows(j + 1, 1 - par, i + 1 + par)
                    if not (first and par == 0):
                        if not (first or (second and par == 0)):
                            pe.wait_ge(y_out, j - 2)
                        down(j - 1, 1 - par)
                    pe.wait_ge(h_ok, j + 1)
                    if not (first and par == 0):
                        pe.wait_ge(ht_lo, j)
                    for t in range(2):
                        last_t = nc.tensor.transpose(bank[3][:, 128 * t:128 * (t + 1)], h_tile[:, par, 128 * t:128 * (t + 1)], ident[:, :])
                    last_t.then_inc(ht_mm, 1)
            step(0, first=True)
            step(1, second=True)
            with pe.Fori(2, NT // 2 - 1) as i:
                step(i)
            step(NT // 2 - 1, last=True)
            down(NT - 1, 1)


def kernel(**inputs):
    import numpy as np
    import concourse.bacc as bacc
    from concourse.bass_utils import run_bass_kernel_spmd

    g = {k: np.asarray(a) for k, a in inputs.items()}

    def by_tile(w):
        n, m = w.shape
        return w.reshape(n // 128, 128, m // 128, 128).transpose(3, 0, 2, 1).reshape(128, -1)

    def by_row(w):
        n, m = w.shape
        return w.T.reshape(m // 128, 128, n).transpose(1, 0, 2).reshape(128, -1)

    def column(b):
        return b.reshape(-1, 128).T

    wqkv, bqkv = g["L0_attn_w_qkv"], g["L0_attn_b_qkv"]
    c = g["ctx_2048"].transpose(0, 2, 1)
    c = np.concatenate([c, np.zeros(c.shape[:2] + (1,), c.dtype)], axis=2)
    c = c.reshape(8, 4, 128, 362).transpose(0, 2, 1, 3).reshape(8, 128, -1)
    w1 = np.concatenate([g["L0_ffn_W1"], g["L0_ffn_Ws1"][None]])
    w3 = np.concatenate([g["L0_ffn_W3"], g["L0_ffn_Ws3"][None]])
    w2 = np.concatenate([g["L0_ffn_W2"], g["L0_ffn_Ws2"][None]])
    w13 = np.stack([w1, w3], axis=1)
    w13 = w13.reshape(9, 2, 256, 4, 128).transpose(0, 4, 3, 1, 2).reshape(9, 128, -1)
    w2 = np.stack([by_row(w) for w in w2])
    arrays = {
        "x": g["x"], "ctx": c, "wqk": by_tile(wqkv[:1024]), "wv": by_row(wqkv[1024:]),
        "wout": by_row(g["L0_attn_w_out"]), "bqk": column(bqkv[:1024]), "bv": column(bqkv[1024:]),
        "bout": g["L0_attn_b_out"][None], "xwq": by_tile(g["L0_xattn_Wq"]), "xwk": by_tile(g["L0_xattn_Wk"]),
        "xwv": by_row(g["L0_xattn_Wv"]), "xwo": by_row(g["L0_xattn_Wo"]), "xbq": column(g["L0_xattn_bq"]),
        "xbk": column(g["L0_xattn_bk"]), "xbv": column(g["L0_xattn_bv"]), "xbo": g["L0_xattn_bo"][None],
        "gw": by_row(g["L0_ffn_gate_w"]), "gb": g["L0_ffn_gate_b"][None],
        "iota": np.arange(20, dtype=np.float32)[None],
        "tri": np.tril(np.ones((8, 8), np.float32), -1).reshape(1, -1), "w13": w13, "w2": w2,
    }
    arrays = {f"in_{k}": np.ascontiguousarray(a) for k, a in arrays.items()}
    nc = bacc.Bacc("TRN2", target_bir_lowering=False, num_devices=1, dynamic_dma_scratch_size=4096)
    args = [nc.dram_tensor(k, a.shape, mybir.dt.from_np(a.dtype), kind="ExternalInput").ap() for k, a in arrays.items()]
    out = nc.dram_tensor("out_x", (8, 100, 512), mybir.dt.float32, kind="ExternalOutput").ap()
    decoder_layer(nc, *args, out)
    r = run_bass_kernel_spmd(nc, [arrays], core_ids=[0])
    return r.results[0]["out_x"]
```

```python
import concourse.bass as bass
from concourse import mybir
from contextlib import ExitStack


def decoder_layer(nc, x_d, ctx_d, wqk_d, wv_d, wout_d, bqk_d, bv_d, bout_d,
                  xwq_d, xwk_d, xwv_d, xwo_d, xbq_d, xbk_d, xbv_d, xbo_d,
                  gw_d, gb_d, iota_d, tri_d, w13_d, w2_d, out_d):
    F32 = mybir.dt.float32
    F32R = mybir.dt.float32r
    U32 = mybir.dt.uint32
    I32 = mybir.dt.int32
    ALU = mybir.AluOpType
    ACT = mybir.ActivationFunctionType
    AX = mybir.AxisListType

    B, T, D = 8, 100, 512
    S = 361
    SP = S + 1
    KD = D // 128
    NG = 4
    HD = 32
    NE = 8
    FI = 256
    NR = 128
    NT = (2 * B * T - NE) // NR + NE
    SCALE = float(HD) ** -0.5
    MASKED = -1.0e30
    EPS = 1e-5
    KEYS = [128, 128, S - 256]
    NSELF = B * NG
    PASSES = ((0, 0), (1, 0), (0, 1))

    ctx = ExitStack()
    with ctx:
        cursor = [(nc.sbuf_base + 31) // 32 * 32]

        def at(name, shape, dt, offset):
            return nc.alloc_sbuf_tensor_at(name, shape, dt, offset=offset)

        def size(shape):
            n = 4
            for s in shape[1:]:
                n *= s
            return (n + 31) // 32 * 32

        def sb(name, shape, dt=F32):
            t = at(name, shape, dt, cursor[0])
            cursor[0] += size(shape)
            return t

        def sem(name):
            return ctx.enter_context(nc.semaphore(name))

        x = sb("x_res", [T, B, D])
        x_end = cursor[0]
        v = [sb(f"v_{h}", [128, 2, 3, D], F32R) for h in ("hi", "lo")]
        probs_at = cursor[0]
        P = sb("probs", [T, 4, SP])
        pt_at = cursor[0]
        PT = [sb(f"probsT_{h}", [128, 3, 4 * T], F32R) for h in ("hi", "lo")]
        oT = sb("oT", [128, NG, T])
        oTs = [sb(f"oT_{h}", [128, NG, T], F32R) for h in ("hi", "lo")]
        stage = sb("stage", [128, 2, 1024])
        nat_at = cursor[0]
        nat = [sb(f"nat_{h}", [128, 8, 2 * T], F32R) for h in ("hi", "lo")]
        xnT = [sb(f"xnT_{h}", [128, KD, 2 * T], F32R) for h in ("hi", "lo")]
        xn = sb("xn", [T, 2, D])
        bout = sb("bout_bc", [T, D])
        identr = sb("identr", [T, T], F32R)
        mask_at = cursor[0]
        maskr = sb("maskr", [T, 4, T], F32R)
        mask_end = cursor[0]
        xbo = sb("xbo_bc", [T, D])
        ident = sb("ident", [128, 128])
        maskf = at("maskf", [T, 4, T], F32, probs_at)
        bqk = sb("bqk", [128, 8])
        bv = sb("bv", [128, 4])
        xbq = sb("xbq", [128, 4])
        xbk = sb("xbk", [128, 4])
        xbv = sb("xbv", [128, 4])
        st = sb("bnst", [T, B, 6])
        mv = sb("meanvar", [T, B, 2])
        ve = sb("vareps", [T, B])
        sd = sb("sdev", [T, B])
        r0 = sb("rstd0", [T, B])
        t1 = sb("newt1", [T, B])
        t2 = sb("newt2", [T, B])
        t3 = sb("newt3", [T, B])
        rstd = sb("rstd", [T, B])
        mx = sb("rowmax", [T, 4])
        nb = sb("negmax", [T, 4])
        rs = sb("rowsum", [T, 2, 4])
        rr = sb("rowrec", [T, 4])
        common_end = cursor[0]

        wqk = [sb(f"wqk_{h}", [128, 8, KD, 128], F32R) for h in ("hi", "lo")]
        wv = [sb(f"wv_{h}", [128, KD, D], F32R) for h in ("hi", "lo")]
        wout = [sb(f"wout_{h}", [128, KD, D], F32R) for h in ("hi", "lo")]
        packs_at = cursor[0]
        pq, pk = [], []
        for par in range(2):
            pq.append(sb(f"pq{par}", [96, 4, 4, 2 * T], F32R))
            pk.append(sb(f"pk{par}", [96, 4, 4, 2 * T], F32R))
        araw = at("araw", [128, 6, 1024], F32, packs_at)
        araw_out = at("araw_out", [128, 2, 1024], F32, packs_at + 2 * 4 * 4 * 2 * T * 4)
        self_end = cursor[0]

        a_wqk = common_end
        a_wv = a_wqk + 2 * 16384
        a_wout = a_wv + 2 * 8192
        xwk = [at(f"xwk_{i}", [128, 4, KD, 128], F32R, a_wqk + 8192 * i) for i in range(2)]
        xwq = [at(f"xwq_{i}", [128, 4, KD, 128], F32R, a_wqk + 16384 + 8192 * i) for i in range(2)]
        xwv = [at(f"xwv_{i}", [128, KD, D], F32R, a_wv + 8192 * i) for i in range(2)]
        xwo = [at(f"xwo_{i}", [128, KD, D], F32R, a_wout + 8192 * i) for i in range(2)]
        knat = [at(f"knat_{i}", [128, 2, 2, SP], F32R, a_wqk + 16384 + 5792 * i) for i in range(2)]
        cx = [[at(f"cx_{i}{h}", [128, KD, SP], F32R, packs_at + 11584 * i + 5792 * h) for h in range(2)] for i in range(2)]
        knat0 = [at(f"knat0_{h}", [128, 2, 2, SP], F32R, packs_at + 11584 + 5792 * h) for h in range(2)]
        kp = at("kp", [96, 4, 4, SP], F32R, packs_at + 2 * 11584)
        qp = at("qp", [96, 2, 4, 4, T], F32R, packs_at + 2 * 11584 + 23168)
        assert 2 * 11584 + 23168 + 12800 + packs_at <= nc.sbuf_usable_end

        def region(start, end):
            where = [start]

            def put(name, shape, dt=F32):
                t = at(name, shape, dt, where[0])
                where[0] += size(shape)
                assert where[0] <= end, (name, where[0], end)
                return t
            return put
        W13, W2 = KD * 2 * FI, 2 * D
        over_mask = region(mask_at, mask_end)
        fx_put = region(nat_at, mask_at)
        fx = [fx_put(f"fx_{h}", [128, KD, B * T], F32R) for h in ("hi", "lo")]
        xn_late = at("xn_late", [T, 2, D], F32, a_wqk + 16384 + 2 * 5792)
        early = region(a_wqk, a_wout)
        sw13 = [early(f"sw13_{h}", [128, KD, 2, FI], F32R) for h in ("hi", "lo")]
        sw2 = [early(f"sw2_{h}", [128, 2, D], F32R) for h in ("hi", "lo")]
        hS = [early(f"hS_{h}", [128, 2, B * T], F32R) for h in ("hi", "lo")]
        w2_at = hS_end = a_wqk + 3 * 8192 + 2 * size([128, 2, B * T])
        sg = early("silu", [128, 2, 4 * T])
        hf = early("hf", [128, 2, 4 * T])
        w2 = [[at(f"w2_0{h}", [128, 2, D], F32R, w2_at + 4096 * i) for i, h in enumerate(("hi", "lo"))], None]
        lgT = at("logitsT", [NE, 7 * T], F32, w2_at + 8192)
        assert w2_at + 8192 + 2816 <= a_wout
        w13 = [[at(f"w13_0{h}", [128, KD, 2 * FI], F32R, a_wqk + 8192 * i) for i, h in enumerate(("hi", "lo"))], None]
        over_fx = region(nat_at, mask_at)
        w13[1] = [over_fx(f"w13_1{h}", [128, KD, 2 * FI], F32R) for h in ("hi", "lo")]
        w2[1] = [over_fx(f"w2_1{h}", [128, 2, D], F32R) for h in ("hi", "lo")]
        low = region(x_end, nat_at)
        raw2 = low("raw2", [128, NE * W2])
        xn3_at = x_end + size([128, NE * W2])
        xn3 = low("xn3", [T, B, D])
        over_xn3 = region(xn3_at, nat_at)
        xgT = [over_xn3(f"xgT_{h}", [128, KD, 128], F32R) for h in ("hi", "lo")]
        hTt = [over_xn3(f"hTt_{h}", [128, 2, 128], F32R) for h in ("hi", "lo")]
        xg = over_xn3("xg", [128, 2, D])
        h_tile = over_xn3("h_tile", [128, 2, FI])
        y_tile = over_xn3("y_tile", [128, 2, D])
        s_tile = over_xn3("s_tile", [128, 2, FI])
        raw13_at = (nc.sbuf_usable_end - 4 * NE * W13) // 32 * 32
        raw13 = at("raw13", [128, NE * W13], F32, raw13_at)
        sraw13 = at("sraw13", [128, KD, 2, FI], F32, raw13_at + 4 * W13)
        sraw2 = at("sraw2", [128, 2, D], F32, raw13_at + 2 * 4 * W13)
        late = region(a_wout, raw13_at)
        gw = over_mask("gw_raw", [128, KD, NE])
        gwr = [over_mask(f"gw_{h}", [128, KD, NE], F32R) for h in ("hi", "lo")]
        gbias = over_mask("gate_bias", [T, NE])
        iota = over_mask("iota", [T, NT])
        tri = over_mask("before", [T, NE, NE])
        tiny = late
        rt = {n: tiny(n, [T, B, NE]) for n in ("lg", "sc", "prob", "bi", "lt", "cand", "m0", "bi2", "lt2", "cand2",
                                               "m1", "slots", "ms0", "ms1", "mw0", "mw1", "below")}
        selr = tiny("selected", [T, B, NE], F32R)
        beforer = tiny("before_r", [T, 128], F32R)
        onesr = tiny("ones_r", [T, 128], F32R)
        trif = tiny("before_f", [T, 128])
        onesf = tiny("ones_f", [T, 128])
        sm = {n: tiny(n, [T, B]) for n in ("gmx", "gsm", "grc", "top0", "ix0", "top1", "ix1", "count", "ntile",
                                           "tstart", "tend", "s0f", "s1f", "wt0", "wt1")}
        over = tiny("over", [T, NE, NE])
        slot_u = tiny("slot_u", [T, 2, B], U32)
        tmap = tiny("tmap", [1, NT, NE])
        tmapf = tiny("tmapf", [1, NT])
        tmapc = tiny("tmapc", [1, NT])
        tmapi = tiny("tmapi", [1, NT], I32)
        gath = [at(f"gath{i}", [T, D], F32, a_wqk + 2048 * i) for i in range(8)]
        zeros = at("zeros", [128, D], F32, self_end)

        scores4 = ctx.enter_context(nc.psum_tensor("scores4", [128, 4, 512], F32))
        more = [ctx.enter_context(nc.psum_tensor(f"bank{i}", [128, 512], F32)) for i in range(4, 8)]
        bank = [scores4[:, i, :] for i in range(4)] + [m[:, :] for m in more]
        J3 = [2, 3, 7]

        qs_d = [nc.dram_tensor(f"q_scratch_{h}", [128, B, 4, T], F32, kind="Internal").ap() for h in ("hi", "lo")]

        qk_d = [nc.dram_tensor(f"qk_scratch_{h}", [B // 2, 2, 128, 4, 2 * T], F32, kind="Internal").ap() for h in ("hi", "lo")]
        ks_d = [nc.dram_tensor(f"k_scratch_{h}", [B, 2, 128, 2, SP], F32, kind="Internal").ap() for h in ("hi", "lo")]
        xs_d = nc.dram_tensor("rows_by_expert", [NT * NR, D], F32, kind="Internal").ap()
        ys_d = nc.dram_tensor("results_by_expert", [NT * NR, D], F32, kind="Internal").ap()

        x_in = [sem(f"x_in{i}") for i in range(2)]
        bqk_in = sem("bqk_in")
        const_in = sem("const_in")
        gate_in = sem("gate_in")
        araw_in = [sem(f"araw_in{i}") for i in range(8)]
        stage_in = [sem(f"stage_in{i}") for i in range(2)]
        pool_step = sem("pool_step")
        ident_ok = sem("ident_ok")
        split_hi = sem("split_hi")
        split_lo = sem("split_lo")
        consts_ok = sem("consts_ok")
        stats_ok = sem("stats_ok")
        late_var = sem("late_var")
        late_ln = sem("late_ln")
        late_guess = sem("late_guess")
        late_xn = sem("late_xn")
        var_ok = sem("var_ok")
        ln_ok = sem("ln_ok")
        sdev_ok = sem("sdev_ok")
        xn_ok = sem("xn_ok")
        dve_step = sem("dve_step")
        bias_added = sem("bias_added")
        unit_mm = sem("unit_mm")
        unit_hi = sem("unit_hi")
        unit_out = sem("unit_out")
        scores_ok = sem("scores_ok")
        negmax_ok = sem("negmax_ok")
        exp_ok = sem("exp_ok")
        probs_ok = sem("probs_ok")
        tp_ok = sem("tp_ok")
        pt_hi = sem("pt_hi")
        pt_lo = sem("pt_lo")
        pv_ok = sem("pv_ok")
        o_out = sem("o_out")
        o_split = sem("o_split")
        qk_stored = [sem(f"qk_stored{i}") for i in range(2)]
        packed = [sem(f"packed{i}") for i in range(2)]
        k_stored = [sem(f"k_stored{i}") for i in range(2)]
        kpacked = [sem(f"kpacked{i}") for i in range(2)]
        q_stored = [sem(f"q_stored{i}") for i in range(2)]
        q_loaded = [sem(f"q_loaded{i}") for i in range(2)]
        late_hi = sem("late_hi")
        late_split = sem("late_split")
        zero_made = sem("zero_made")
        tri_made = sem("tri_made")
        zero_in = sem("zero_in")
        route_c = sem("route_c")
        gate_mm = sem("gate_mm")
        gate_out = sem("gate_out")
        tri_ok = sem("tri_ok")
        router_mm = sem("router_mm")
        logits_ok = sem("logits_ok")
        gexp = sem("gexp")
        sel_ok = sem("sel_ok")
        cum_mm = sem("cum_mm")
        slots_ok = sem("slots_ok")
        tmap_ok = sem("tmap_ok")
        scattered = sem("scattered")
        sraw_in = sem("sraw_in")
        s_lo = sem("s_lo")
        sup_mm = sem("sup_mm")
        ssilu = sem("ssilu")
        sh_ok = sem("sh_ok")
        sh_hi = sem("sh_hi")
        sh_lo = sem("sh_lo")
        sdn_mm = sem("sdn_mm")
        sdn_out = sem("sdn_out")
        raw13_in = sem("raw13_in")
        raw2_in = sem("raw2_in")
        w13_hi = sem("w13_hi")
        w13_lo = sem("w13_lo")
        w2_hi = sem("w2_hi")
        w2_lo = sem("w2_lo")
        xg_in = [sem(f"xg_in{i}") for i in range(2)]
        xt_mm = sem("xt_mm")
        xt_hi = sem("xt_hi")
        xt_lo = sem("xt_lo")
        up_mm = sem("up_mm")
        silu_ok = sem("silu_ok")
        h_ok = sem("h_ok")
        ht_mm = sem("ht_mm")
        ht_hi = sem("ht_hi")
        ht_lo = sem("ht_lo")
        down_mm = sem("down_mm")
        y_out = sem("y_out")
        y_stored = [sem(f"y_stored{i}") for i in range(2)]
        gathered = [sem(f"gathered{i}") for i in range(8)]
        added = sem("added")
        stored = sem("stored")

        QP = B // 2
        units, unit_at = [], {}

        def add(*us):
            for u in us:
                unit_at[u] = len(units)
                units.append(u)
            return list(us)

        prologue = add(("X", 0, 0), ("X", 0, 1), *[("QK", 0, m) for m in range(8)], ("V", 0, 0), ("V", 0, 1),
                       ("X", 1, 0), ("X", 1, 1))
        self_slots = []
        for n in range(NSELF + 1):
            p, k = divmod(n, 8)
            a, b = [], []
            if p + 1 < QP:
                q = p + 1
                a = {0: [("QK", q, 4)], 1: [("QK", q, 5)], 2: [("QK", q, 6)], 3: [("V", q, 0)], 4: [("V", q, 1)]}.get(k, [])
                b = {2: [("QK", q, 7)]}.get(k, [])
            if p + 2 < QP:
                q = p + 2
                a = a + {5: [("X", q, 0), ("X", q, 1)], 6: [("QK", q, 0)], 7: [("QK", q, 2)]}.get(k, [])
                b = b + {6: [("QK", q, 1)], 7: [("QK", q, 3)]}.get(k, [])
            if n < 3:
                a = [[("QK", 1, 0)], [("QK", 1, 3), ("QK", 1, 4)], [("QK", 1, 6)]][n]
                b = [[("QK", 1, 1), ("QK", 1, 2)], [("QK", 1, 5)], [("QK", 1, 7)]][n]
            if k == 1 and p > 0:
                b = b + [("O", 2 * p - 1, 0)]
            if k == 5:
                b = b + [("O", 2 * p, 0)]
            a = a + {22: [("Q", 0, 0)], 23: [("Q", 0, 2)], 24: [("X2", 1, 0), ("X2", 1, 1)], 25: [("Q", 1, 0)],
                     26: [("Q", 1, 2)], 27: [("X2", 2, 0), ("X2", 2, 1)], 28: [("Q", 2, 0)],
                     29: [("Q", 2, 2)], 30: [("K", 0, 2)], 31: [("XV", 0, 0)],
                     32: [("XV", 0, 1)]}.get(n, [])
            b = b + {21: [("X2", 0, 0), ("X2", 0, 1)], 22: [("Q", 0, 1)], 23: [("Q", 0, 3)], 25: [("Q", 1, 1)],
                     26: [("Q", 1, 3)], 27: [("K", 0, 0)], 28: [("Q", 2, 1), ("K", 0, 1)],
                     29: [("Q", 2, 3)], 30: [("K", 0, 3)]}.get(n, [])
            self_slots.append((add(*a), add(*b)))
        boundary = add(("XV", 0, 2), ("O", B - 1, 0))
        cross_slots = []
        for n in range(NSELF + 1):
            b, g = divmod(n, 4)
            a, bb = [], []
            if b + 1 < B:
                a = [("K", b + 1, g)]
                if g < 3:
                    bb = [("XV", b + 1, g)]
            if n == 0:
                a = []
                bb = [("XV", 1, 0), ("X2", QP - 1, 0), ("X2", QP - 1, 1), ("XV", 1, 1),
                      *[("Q", QP - 1, m) for m in range(4)], ("K", 1, 0)]
            if n in (1, 2):
                bb = [[("XV", 1, 2)], []][n - 1]
            if g == 3 and b > 0:
                bb = bb + [("XO", b - 1, 0)]
            cross_slots.append((add(*a), add(*bb)))
        last_o = add(("XO", B - 1, 0))

        first_cross = unit_at[boundary[-1]] + 1
        second_slot = unit_at[("K", 1, 1)]
        ubank, prev_user, seen = [], [], {}
        for i, u in enumerate(units):
            if i < first_cross:
                k = J3[i % 3]
            elif i < second_slot:
                k = 4 + i % 4
            else:
                k = 7 if u[0] == "K" else 6
            prev_user.append(seen.get(k))
            seen[k] = i
            ubank.append(k)
        hi_units = [u for u in units if u[0] not in ("O", "XO")]
        hi_at = {u: i for i, u in enumerate(hi_units)}
        x_units = [u for u in units if u[0] in ("X", "X2")]
        xn_at = {u: i for i, u in enumerate(x_units)}

        SHARED_FIRST = 5

        pieces, piece_at = [], {}

        def piece(key, src, cols, hi, lo, waits):
            piece_at[key] = len(pieces)
            pieces.append((src, cols, hi, lo, waits))

        qk_free = ("unit", unit_at[("QK", QP - 1, 7)])
        v_free = ("unit", unit_at[("V", QP - 1, 1)])

        def weight_pieces(key, src, dst, waits):
            for i in range(2):
                piece((key, i), src[:, 1024 * i:1024 * (i + 1)], 1024, dst[0][:, 2 * i:2 * i + 2],
                      dst[1][:, 2 * i:2 * i + 2], waits)

        def ctx_pieces(b):
            if b == 0:
                w = ("scores", 24)
            elif b == 1:
                w = ("stored", 16 * 2)
            else:
                w = ("unit", max(unit_at[("K", b - 2, 3)], unit_at[("XV", b - 2, 2)]))
            for i in range(2):
                piece(("cx", b, i), ctx_d[b, :, 2 * SP * i:2 * SP * (i + 1)], 2 * SP,
                      cx[b % 2][0][:, 2 * i:2 * i + 2, :], cx[b % 2][1][:, 2 * i:2 * i + 2, :], w)
        weight_pieces("wq", xwq_d, xwq, qk_free)
        weight_pieces("wk", xwk_d, xwk, qk_free)
        weight_pieces("wv", xwv_d, xwv, v_free)
        ctx_pieces(0)
        ctx_pieces(1)
        act_pieces = len(pieces)
        weight_pieces("wo", xwo_d, xwo, ("unit", unit_at[("O", B - 1, 0)]))
        for b in range(2, B):
            ctx_pieces(b)
        SECOND = {21: (0, 4), 26: (4, 6)}
        SPLIT_BEFORE = {("QK", 0, 0): (1,), ("QK", 0, 1): (2,), ("QK", 0, 2): (3,), ("QK", 0, 4): (4,),
                        ("QK", 0, 6): (5,)}
        PIECE_SLOT = 19

        def nchunks(n):
            return 1 if n < NSELF else 3

        def x3_row(s):
            if s == NSELF:
                return B - 2
            return s // NG - 2 if s % NG == 1 and s > 2 * NG else None

        ring = []
        for n in range(2 * NSELF):
            ring += [("probs", n, c) for c in range(nchunks(n))]
            if n >= NSELF and x3_row(n - NSELF + 1) is not None:
                ring.append(("rows", x3_row(n - NSELF + 1)))
        ring.append(("rows", B - 1))
        ring_at = {r: i for i, r in enumerate(ring)}

        def chunk(n, c=0):
            return ring_at[("probs", n, c)]

        def probs_col(n):
            return 128 * (n % 2) if n < NSELF else 0

        def vslot(n):
            if n < NSELF:
                b = n // NG
                return (b // 2) % 2, b % 2
            return ((n - NSELF) // NG) % 2, 0

        def heads_bank(n):
            return bank[6] if n < NSELF else bank[7]

        def ub_first(n):
            return n > NSELF and n % NG != 0

        def k_place(b):
            return knat if b > 0 else knat0

        def piece_free(eng, i):
            what, value = pieces[i][4]
            if what == "unit":
                eng.wait_ge(unit_mm, value + 1)
            elif what == "scores":
                eng.wait_ge(scores_ok, value)
            else:
                for h in range(2):
                    eng.wait_ge(k_stored[h], value)

        def piece_raw(i):
            src, cols, hi, lo, waits = pieces[i]
            raw = stage[:, i % 2, 0:cols]
            if len(hi.shape) == 4:
                return raw.rearrange("p (a b c) -> p a b c", a=hi.shape[1], b=hi.shape[2])
            return raw.rearrange("p (a b) -> p a b", a=hi.shape[1])

        def unit_io(u):
            kind, a, b = u
            bk = bank[ubank[unit_at[u]]]
            if kind in ("X", "X2"):
                return (bk[:, 0:4 * T].rearrange("p (k t) -> p k t", k=KD),
                        [y[:, :, T * b:T * (b + 1)] for y in xnT], None)
            if kind == "QK":
                return bk[:, 0:2 * T], [y[:, b, :] for y in nat], bqk[:, b:b + 1]
            if kind == "Q":
                return bk[:, 0:2 * T], [y[:, 4 * (a % 2) + b, :] for y in nat], xbq[:, b:b + 1]
            if kind == "K":
                return bk[:, 0:SP], [y[:, b // 2, b % 2, :] for y in k_place(a)], xbk[:, b:b + 1]
            if kind == "V":
                return bk[0:T, :], [y[0:T, a % 2, b, :] for y in v], None
            if kind == "XV":
                return bk[0:KEYS[b], :], [y[0:KEYS[b], a % 2, b, :] for y in v], None

        def xn_tile(i):
            return xn[:, i % 2, :]

        def rows_io(b):
            src = bank[4 + ring_at[("rows", b)] % 2][:, 0:4 * T].rearrange("p (k t) -> p k t", k=KD)
            return src, [y[:, :, T * b:T * (b + 1)] for y in fx]

        def shared_piece(i, h):
            if i < KD:
                return sw13[h][:, i, :, :], sraw13[:, i, :, :]
            return sw2[h][:, :, :], sraw2[:, :, :]

        def score_ap(n):
            if n < NSELF:
                return bank[n % 2][0:T, 0:4 * T].rearrange("p (j t) -> p j t", j=4)
            return scores4[0:T, :, 0:S]

        def whole(i):
            raw = araw[:, i, :] if i < 6 else araw_out[:, i - 6, :]
            if i < 4:
                return (raw.rearrange("p (a b c) -> p a b c", a=2, b=KD), [w[:, 2 * i:2 * i + 2, :, :] for w in wqk])
            w = wv if i < 6 else wout
            return raw.rearrange("p (a b) -> p a b", a=2), [y[:, 2 * (i % 2):2 * (i % 2) + 2, :] for y in w]

        block = ctx.enter_context(nc.Block())

        def raw13_of(e):
            return raw13[:, bass.ds(e * W13, W13)].rearrange("p (k n) -> p k n", k=KD)

        def raw2_of(e):
            return raw2[:, bass.ds(e * W2, W2)].rearrange("p (k n) -> p k n", k=2)

        def expert(eng, j):
            return eng.value_load(tmapi[0:1, bass.ds(j, 1)], min_val=0, max_val=NE - 1)

        @block.sync
        def _(sp):
            xs = x_d.rearrange("b t d -> t b d")
            sp.dma_start(x[:, 0:2, :], xs[:, 0:2, :]).then_inc(x_in[0], 16)
            for i in range(4):
                sp.dma_start(araw[:, i, :], wqk_d[:, 1024 * i:1024 * (i + 1)]).then_inc(araw_in[i], 16)
            for i in range(2):
                sp.dma_start(araw[:, 4 + i, :], wv_d[:, 1024 * i:1024 * (i + 1)]).then_inc(araw_in[4 + i], 16)
            sp.dma_start(x[:, 2:B, :], xs[:, 2:B, :]).then_inc(x_in[1], 16)
            for i in range(2):
                sp.dma_start(araw_out[:, i, :], wout_d[:, 1024 * i:1024 * (i + 1)]).then_inc(araw_in[6 + i], 16)
            for dst, src in ((bv, bv_d), (xbq, xbq_d), (xbk, xbk_d), (xbv, xbv_d)):
                sp.dma_start(dst[:, :], src).then_inc(const_in, 16)
            sp.dma_start(bout[:, :], bout_d.broadcast_to([T, D])).then_inc(const_in, 16)
            sp.dma_start(xbo[:, :], xbo_d.broadcast_to([T, D])).then_inc(const_in, 16)

            for p in range(QP):
                for w in range(2):
                    sp.wait_ge(unit_out, unit_at[("QK", p, 4 * w + 3)] + 1)
                    for h in range(2):
                        sp.dma_start(qk_d[h][p, w], nat[h][:, 4 * w:4 * w + 4, :].bitcast(F32)).then_inc(qk_stored[w], 16)
                if p < 2:
                    sp.wait_ge(split_lo, 6 if p == 0 else 8)
                else:
                    sp.wait_ge(scores_ok, 8 * (p - 1))
                for w, (dst, halves) in enumerate(((pq[p % 2], (0, 1, 0)), (pk[p % 2], (0, 0, 1)))):
                    sp.wait_ge(qk_stored[w], 16 * 2 * (p + 1))
                    for r, h in enumerate(halves):
                        sp.dma_start(dst[32 * r:32 * r + 32, :, :, :].rearrange("p j m t -> p j (m t)").bitcast(F32),
                                     qk_d[h][p, w].rearrange("(j d) m t -> d j (m t)", d=32)).then_inc(packed[p % 2], 16)
                if p == 0:
                    sp.wait_ge(zero_made, 1)
                    xz = xs_d.rearrange("(j p) d -> p j d", p=NR)
                    for i in range(4):
                        sp.dma_start(xz[:, 5 * i:5 * i + 5, :],
                                     zeros[:, :].unsqueeze(1).to_broadcast([NR, 5, D])).then_inc(zero_in, 16)
            def store_q(p):
                sp.wait_ge(unit_out, unit_at[("Q", p, 3)] + 1)
                for i in range(2):
                    for h in range(2):
                        sp.dma_start(qs_d[h][:, 2 * p + i, :, :],
                                     nat[h][:, 4 * (p % 2):4 * (p % 2) + 4, T * i:T * (i + 1)].bitcast(F32)).then_inc(q_stored[p % 2], 16)
            def store_k(b, w):
                sp.wait_ge(unit_out, unit_at[("K", b, 2 * w + 1)] + 1)
                for h in range(2):
                    sp.dma_start(ks_d[h][b, w], k_place(b)[h][:, w, :, :].bitcast(F32)).then_inc(k_stored[w], 16)

            def load_k(b, w):
                sp.wait_ge(k_stored[w], 16 * 2 * (b + 1))
                if b > 0:
                    sp.wait_ge(scores_ok, NSELF + 4 * (b - 1) + 2 * w + 2)
                for r, h in enumerate((0, 0, 1)):
                    sp.dma_start(kp[32 * r:32 * r + 32, :, 2 * w:2 * w + 2, :].rearrange("p j m t -> p j (m t)").bitcast(F32),
                                 ks_d[h][b, w].rearrange("(j d) m t -> d j (m t)", d=32)).then_inc(kpacked[w], 16)

            store_q(0)
            store_q(1)
            store_k(0, 0)
            store_q(2)
            store_k(0, 1)

            def load_q(b):
                for r, h in enumerate((0, 1, 0)):
                    sp.dma_start(qp[32 * r:32 * r + 32, b % 2, :, :, :].rearrange("p j m t -> p j (m t)").bitcast(F32),
                                 qs_d[h][:, b, :, :].rearrange("(j d) m t -> d j (m t)", d=32)).then_inc(q_loaded[b % 2], 16)
            sp.wait_ge(zero_in, 64)
            sp.wait_ge(scores_ok, NSELF)
            sp.wait_ge(q_stored[0], 16 * 4 * QP // 2)
            load_k(0, 0)
            load_q(0)
            load_k(0, 1)
            sp.dma_start(gw[:, :, :], gw_d.rearrange("p (k e) -> p k e", k=KD)).then_inc(gate_in, 16)
            sp.dma_start(gbias[:, :], gb_d.broadcast_to([T, NE])).then_inc(gate_in, 16)
            sp.dma_start(iota[:, :], iota_d.broadcast_to([T, NT])).then_inc(gate_in, 16)
            sp.dma_start(tri[:, :, :].rearrange("p a b -> p (a b)"), tri_d.broadcast_to([T, NE * NE])).then_inc(gate_in, 16)
            store_q(QP - 1)
            sp.wait_ge(q_stored[1], 16 * 4 * QP // 2)
            for b in range(B):
                if b > 0:
                    for w in range(2):
                        store_k(b, w)
                        load_k(b, w)
                if b + 1 < B:
                    if b > 0:
                        sp.wait_ge(scores_ok, NSELF + 4 * b)
                    load_q(b + 1)
            sp.wait_ge(unit_mm, max(unit_at[("K", B - 1, 3)], unit_at[("XV", B - 1, 2)]) + 1)
            sp.dma_start(sraw13[:, :, :, :], w13_d[NE].rearrange("p (k i f) -> p k i f", k=KD, i=2)).then_inc(sraw_in, 16)
            sp.dma_start(sraw2[:, :, :], w2_d[NE].rearrange("p (k n) -> p k n", k=2)).then_inc(sraw_in, 16)
            sp.wait_ge(scores_ok, 2 * NSELF)
            for e in (3, 4, 5, 6, 7):
                sp.dma_start(raw13[:, e * W13:(e + 1) * W13], w13_d[e]).then_inc(raw13_in, 16)
            sp.wait_ge(s_lo, KD)
            sp.dma_start(raw13[:, W13:2 * W13], w13_d[1]).then_inc(raw13_in, 16)
            sp.wait_ge(unit_out, unit_at[("XO", B - 1, 0)] + 1)
            sp.dma_start(raw13[:, 0:W13], w13_d[0]).then_inc(raw13_in, 16)
            for e in range(NE):
                sp.dma_start(raw2[:, e * W2:(e + 1) * W2], w2_d[e]).then_inc(raw2_in, 16)
            sp.wait_ge(s_lo, KD + 1)
            sp.dma_start(raw13[:, 2 * W13:3 * W13], w13_d[2]).then_inc(raw13_in, 16)

            def load_x(j, i):
                sp.dma_start(xg[:, i, :], xs_d[bass.ds(NR * j, NR), :]).then_inc(xg_in[i], 16)
            sp.wait_ge(scattered, 16 * 2 * B)
            load_x(0, 0)
            load_x(1, 1)

            with sp.Fori(0, NT // 2 - 1) as i:
                for par in range(2):
                    j = 2 * i + par
                    sp.wait_ge(xt_mm, j + 1)
                    load_x(j + 2, par)
            for b in range(B):
                sp.wait_ge(added, b + 1)
                sp.dma_start(out_d[b, :, :], x[:, b, :]).then_inc(stored, 16)
            sp.wait_ge(stored, 16 * B)

        @block.gpsimd
        def _(pool):
            k = [0]

            def own(ins):
                k[0] += 1
                ins.then_inc(pool_step, 1)
                pool.wait_ge(pool_step, k[0])
            own(nc.gpsimd.memset(ident[:, :], 0.0))
            own(nc.gpsimd.affine_select(out=ident[:, :], in_=ident[:, :], compare_op=ALU.not_equal, fill=1.0,
                                        base=0, pattern=[[-1, 128]], channel_multiplier=1))
            own(nc.gpsimd.memset(maskf[:, :, :], 0.0))
            nc.gpsimd.affine_select(out=maskf[:, :, :], in_=maskf[:, :, :], compare_op=ALU.is_ge, fill=MASKED,
                                    base=0, pattern=[[0, 4], [-1, T]], channel_multiplier=1).then_inc(ident_ok, 1)
            pool.wait_ge(const_in, 16 * 6)
            for b in range(B):
                pool.wait_ge(xn_ok, b + 1)
                nc.gpsimd.tensor_tensor(x[:, b, :], x[:, b, :], bout[:, :], ALU.add).then_inc(bias_added, 1)

            def load(i):
                src, cols, hi, lo, waits = pieces[i]
                pool.dma_start(stage[:, i % 2, 0:cols], src).then_inc(stage_in[i % 2], 16)

            def third_norm(b):
                pool.wait_ge(stats_ok, b + 1)
                nc.gpsimd.tensor_scalar(ve[:, b:b + 1], mv[:, b, 1:2], EPS, None, ALU.add).then_inc(late_var, 1)
                pool.wait_ge(late_guess, b + 1)
                c = slice(b, b + 1)
                own(nc.gpsimd.tensor_tensor(t1[:, c], ve[:, c], r0[:, c], ALU.mult))
                own(nc.gpsimd.tensor_tensor(t2[:, c], t1[:, c], r0[:, c], ALU.mult))
                own(nc.gpsimd.tensor_scalar(t3[:, c], t2[:, c], -0.5, 1.5, ALU.mult, ALU.add))
                own(nc.gpsimd.tensor_tensor(rstd[:, c], t3[:, c], r0[:, c], ALU.mult))
                if b >= 2:
                    pool.wait_ge(tp_ok, ring_at[("rows", b - 2)] + 1)
                nc.gpsimd.tensor_scalar(xn_late[:, b % 2, :], x[:, b, :], mv[:, b, 0:1], rstd[:, c],
                                        ALU.subtract, ALU.mult).then_inc(late_xn, 1)

            load(0)
            for i, (src, cols, hi, lo, waits) in enumerate(pieces):
                if i == piece_at[("cx", 2, 0)]:
                    for b in range(B):
                        pool.wait_ge(xn_ok, B + b + 1)
                        nc.gpsimd.tensor_tensor(x[:, b, :], x[:, b, :], xbo[:, :], ALU.add).then_inc(bias_added, 1)
                for b in range(4, B):
                    if i == piece_at[("cx", b, 0)]:
                        third_norm(b - 4)
                if i + 1 < len(pieces):
                    if i > 0:
                        pool.wait_ge(late_split, i)
                    load(i + 1)
                raw = piece_raw(i)
                if i < act_pieces:
                    pool.wait_ge(late_hi, i + 1)
                else:
                    piece_free(pool, i)
                    pool.wait_ge(stage_in[i % 2], 16 * (i // 2 + 1))
                    own(nc.gpsimd.tensor_copy(hi, raw))
                nc.gpsimd.tensor_tensor(lo, raw, hi, ALU.subtract).then_inc(late_split, 1)

            def shared_split(i):
                hi, raw = shared_piece(i, 0)
                own(nc.gpsimd.tensor_copy(hi, raw))
                nc.gpsimd.tensor_tensor(shared_piece(i, 1)[0], raw, hi, ALU.subtract).then_inc(s_lo, 1)

            for b in range(4, B - 2):
                third_norm(b)
            pool.wait_ge(sraw_in, 32)
            for i in range(KD):
                shared_split(i)
            third_norm(B - 2)
            pool.wait_ge(k_stored[1], 16 * 2 * B)
            shared_split(KD)
            pool.wait_ge(unit_out, unit_at[("XO", B - 1, 0)] + 1)
            own(nc.gpsimd.memset(onesf[:, :], 1.0))
            nc.gpsimd.affine_select(out=trif[:, :], in_=onesf[:, :], compare_op=ALU.is_gt, fill=0.0,
                                    base=0, pattern=[[1, 128]], channel_multiplier=-1).then_inc(tri_made, 1)
            pool.wait_ge(zero_in, 64)
            pool.wait_ge(slots_ok, 1)
            for b in range(B):
                for c in range(2):
                    nc.gpsimd.indirect_dma_start(
                        out=xs_d, out_offset=bass.IndirectOffsetOnAxis(ap=slot_u[:, c, b:b + 1], axis=0),
                        in_=xn3[:, b, :], in_offset=None).then_inc(scattered, 16)

            def w2_low(j, i):
                e = expert(pool, j)
                pool.wait_ge(w2_hi, j + 1)
                pool.wait_ge(raw2_in, 16 * NE)
                nc.gpsimd.tensor_tensor(w2[i][1][:, :, :], raw2_of(e), w2[i][0][:, :, :], ALU.subtract).then_inc(w2_lo, 1)
            pool.wait_ge(tmap_ok, 1)
            with pool.Fori(0, NT // 2) as i:
                for par in range(2):
                    w2_low(2 * i + par, par)
            for i in range(2):
                pool.wait_ge(y_stored[i], 16 * (NT // 2))
            pool.wait_ge(down_mm, NT)
            for b in range(B):
                for c in range(2):
                    i = (2 * b + c) % 8
                    if b >= 4:
                        pool.wait_ge(added, b - 3)
                    nc.gpsimd.indirect_dma_start(
                        out=gath[i][:, :], out_offset=None, in_=ys_d,
                        in_offset=bass.IndirectOffsetOnAxis(ap=slot_u[:, c, b:b + 1], axis=0)).then_inc(gathered[i], 16)

        @block.scalar
        def _(act):
            nc.scalar.preload_act_table_set("natural_log_exp_and_others")
            act.dma_start(bqk[:, :], bqk_d).then_inc(bqk_in, 16)

            def std(b0, b1):
                act.wait_ge(var_ok, std.n + 1)
                std.n += 1
                nc.scalar.activation(sd[:, b0:b1], ve[:, b0:b1], ACT.Ln).then_inc(ln_ok, 1)
                act.wait_ge(ln_ok, std.n)
                nc.scalar.activation(r0[:, b0:b1], sd[:, b0:b1], ACT.Exp, scale=-0.5).then_inc(sdev_ok, 1)
            std.n = 0

            def late_std(b):
                act.wait_ge(late_var, b + 1)
                nc.scalar.activation(sd[:, b:b + 1], ve[:, b:b + 1], ACT.Ln).then_inc(late_ln, 1)
                act.wait_ge(late_ln, b + 1)
                nc.scalar.activation(r0[:, b:b + 1], sd[:, b:b + 1], ACT.Exp, scale=-0.5).then_inc(late_guess, 1)

            def third_high(b):
                act.wait_ge(tp_ok, ring_at[("rows", b)] + 1)
                src, dst = rows_io(b)
                nc.scalar.activation(dst[0], src, ACT.Copy).then_inc(pt_hi, 1)

            def unit_high(u):
                kind, a, b = u
                if kind in ("O", "XO"):
                    return
                i = unit_at[u]
                act.wait_ge(unit_mm, i + 1)
                src, dst, bias = unit_io(u)
                if kind == "QK" and a >= 1:
                    act.wait_ge(qk_stored[b // 4], 16 * 2 * a)
                if kind == "V" and a >= 2:
                    act.wait_ge(pv_ok, 8 * (a - 1))
                if kind == "Q" and a < 2:
                    for i in range(2):
                        act.wait_ge(qk_stored[i], 16 * 2 * QP)
                if kind == "Q" and a >= 2:
                    act.wait_ge(q_stored[a % 2], 64 * (a // 2))
                if kind == "K" and a >= 1:
                    act.wait_ge(k_stored[b // 2], 16 * 2 * a)
                if kind == "XV":
                    act.wait_ge(pv_ok, NSELF + 4 * (a - 1) if a > 0 else 24)
                if bias is None:
                    nc.scalar.activation(dst[0], src, ACT.Copy).then_inc(unit_hi, 1)
                else:
                    nc.scalar.activation(dst[0], src, ACT.Identity, bias=bias).then_inc(unit_hi, 1)

            def tail_high(n, chunks):
                for c in chunks:
                    ci = chunk(n, c)
                    kc = T if n < NSELF else KEYS[c]
                    act.wait_ge(tp_ok, ci + 1)
                    if n > 0:
                        act.wait_ge(pv_ok, n)
                    nc.scalar.activation(PT[0][0:kc, c, :], bank[4 + ci % 2][0:kc, 0:4 * T], ACT.Copy).then_inc(pt_hi, 1)

            def exps(n):
                act.wait_ge(negmax_ok, n + 1)
                if n >= NSELF:
                    act.wait_ge(tp_ok, chunk(n - 1) + nchunks(n - 1))
                elif n >= 2:
                    act.wait_ge(tp_ok, n - 1)
                for j in range(4):
                    src = score_ap(n)[:, j, :]
                    last = nc.scalar.activation(P[:, j, probs_col(n):probs_col(n) + src.shape[-1]], src, ACT.Exp, bias=nb[:, j:j + 1],
                                                scale=SCALE, accum_out=rs[:, n % 2, j:j + 1])
                last.then_inc(exp_ok, 1)

            def heads_out(n):
                bias = bv if n < NSELF else xbv
                g = n % NG
                act.wait_ge(pv_ok, n + 1)
                if g == 0 and n > 0:
                    act.wait_ge(o_split, n // NG)
                for j in range(4):
                    last = nc.scalar.activation(oT[32 * j:32 * j + 32, g, :], heads_bank(n)[32 * j:32 * j + 32, T * j:T * (j + 1)],
                                                ACT.Identity, bias=bias[32 * j:32 * j + 32, g:g + 1])
                last.then_inc(o_out, 1)

            def piece_high(i):
                piece_free(act, i)
                act.wait_ge(stage_in[i % 2], 16 * (i // 2 + 1))
                nc.scalar.activation(pieces[i][2], piece_raw(i), ACT.Copy).then_inc(late_hi, 1)

            def self_high(i):
                act.wait_ge(araw_in[i], 16)
                raw, halves = whole(i)
                nc.scalar.activation(halves[0], raw, ACT.Copy).then_inc(split_hi, 1)

            std(0, 2)
            self_high(0)
            for u in prologue:
                if u == ("QK", 0, 0):
                    act.wait_ge(bqk_in, 16)
                if u in SPLIT_BEFORE:
                    for i in SPLIT_BEFORE[u]:
                        self_high(i)
                if u == ("X", 1, 0):
                    std(2, B)
                unit_high(u)
            for i in (6, 7):
                self_high(i)
            act.wait_ge(const_in, 16 * 6)
            for first, slots in ((0, self_slots), (NSELF, cross_slots)):
                if first > 0:
                    for u in boundary:
                        unit_high(u)
                    for i in range(8, act_pieces):
                        piece_high(i)
                    std(6, 8)
                for s, (ua, ub) in enumerate(slots):
                    n = first + s
                    if s > 0:
                        tail_high(n - 1, range(nchunks(n - 1))[0:2])
                    if first > 0 and s % NG == 0 and s >= 2 * NG:
                        late_std(s // NG - 2)
                    if first == 0 and s in SECOND:
                        std(*SECOND[s])
                    if s < NSELF and (first == 0):
                        exps(n)
                    if first == 0 and 0 <= s - PIECE_SLOT < 8:
                        piece_high(s - PIECE_SLOT)
                    for u in ua:
                        unit_high(u)
                    if s > 0 and nchunks(n - 1) > 2:
                        tail_high(n - 1, [2])
                    if s < NSELF and not (first == 0):
                        exps(n)
                    if first > 0 and x3_row(s) is not None and s < NSELF:
                        third_high(x3_row(s))
                    if ub_first(n):
                        for u in ub:
                            unit_high(u)
                    if s > 0:
                        heads_out(n - 1)
                    if first > 0 and x3_row(s) is not None and s == NSELF:
                        third_high(x3_row(s))
                    if not ub_first(n):
                        for u in ub:
                            unit_high(u)
            std(B - 1, B)
            act.wait_ge(gate_mm, 1)
            nc.scalar.activation(lgT[:, 0:4 * T], bank[2][0:NE, 0:4 * T], ACT.Copy)
            nc.scalar.activation(lgT[:, 4 * T:7 * T], bank[3][0:NE, 0:3 * T], ACT.Copy).then_inc(gate_out, 1)
            third_high(B - 1)
            act.wait_ge(logits_ok, 1)
            nc.scalar.activation(rt["sc"][:, :, :], rt["lg"][:, :, :], ACT.Exp).then_inc(gexp, 1)
            for c in range(4):
                half, it = divmod(c, 2)
                act.wait_ge(sup_mm, c + 1)
                if c >= 2:
                    act.wait_ge(sh_ok, c - 1)
                nc.scalar.activation(sg[:, c % 2, :], bank[2 * (c % 2)][:, 0:4 * T], ACT.Silu).then_inc(ssilu, 1)
                act.wait_ge(sh_ok, c + 1)
                nc.scalar.activation(hS[0][:, it, 4 * T * half:4 * T * (half + 1)], hf[:, c % 2, :], ACT.Copy).then_inc(sh_hi, 1)

            def w13_high(j, i, h):
                e = expert(act, j)
                act.wait_ge(raw13_in, 16 * NE)
                nc.scalar.activation(w13[i][0][:, 2 * h:2 * h + 2, :], raw13_of(e)[:, 2 * h:2 * h + 2, :], ACT.Copy).then_inc(w13_hi, 1)

            def rows_high(j):
                act.wait_ge(xt_mm, j + 1)
                nc.scalar.activation(xgT[0][:, :, :], bank[2][:, :].rearrange("p (k t) -> p k t", k=KD), ACT.Copy).then_inc(xt_hi, 1)
            act.wait_ge(tmap_ok, 1)
            w13_high(0, 0, 0)
            w13_high(0, 0, 1)
            w13_high(1, 1, 0)
            rows_high(0)

            def y_high(j, i, stores=None):
                act.wait_ge(down_mm, j + 1)
                if stores is not None:
                    act.wait_ge(y_stored[i], 16 * stores)
                nc.scalar.activation(y_tile[:, i, :], bank[4 + i][:, :], ACT.Copy).then_inc(y_out, 1)
                act.wait_ge(y_out, j + 1)
                act.dma_start(ys_d[bass.ds(NR * j, NR), :], y_tile[:, i, :]).then_inc(y_stored[i], 16)

            def h_high(j):
                act.wait_ge(ht_mm, j + 1)
                nc.scalar.activation(hTt[0][:, :, :], bank[3][:, 0:FI].rearrange("p (k t) -> p k t", k=2),
                                     ACT.Copy).then_inc(ht_hi, 1)

            def step(i, done=2 * NR, last=False):
                for par in range(2):
                    j = 2 * i + par
                    if not (last and par == 1):
                        w13_high(j + 1, 1 - par, 1)
                    if done + par >= 2:
                        act.wait_ge(down_mm, j - 1)
                    if done + par >= 1:
                        h_high(j - 1)
                    if done + par >= 2:
                        y_high(j - 2, par, i - 1 if done + par >= 4 else None)
                    act.wait_ge(up_mm, j + 1)
                    if done + par >= 2:
                        act.wait_ge(h_ok, j - 1)
                    nc.scalar.activation(s_tile[:, par, :], bank[par][:, 0:FI], ACT.Silu).then_inc(silu_ok, 1)
                    if not (last and par == 1):
                        rows_high(j + 1)
                    if not last:
                        w13_high(j + 2, par, 0)
            step(0, done=0)
            step(1, done=2)
            with act.Fori(2, NT // 2 - 1) as i:
                step(i)
            step(NT // 2 - 1, last=True)
            act.wait_ge(down_mm, NT - 1)
            h_high(NT - 1)
            y_high(NT - 2, 0, NT // 2 - 1)
            y_high(NT - 1, 1, NT // 2 - 1)

        @block.vector
        def _(dve):
            k = [0]

            def own(ins):
                k[0] += 1
                ins.then_inc(dve_step, 1)
                dve.wait_ge(dve_step, k[0])

            def stats(b0, b1):
                for b in range(b0, b1):
                    last = nc.vector.bn_stats(st[:, b, :], x[:, b, :])
                own(last)
                variance(b0, b1)

            def variance(b0, b1):
                for b in range(b0, b1):
                    last = nc.vector.bn_aggr(mv[:, b, :], st[:, b, :])
                own(last)
                nc.vector.tensor_scalar(ve[:, b0:b1], mv[:, b0:b1, 1], EPS, None, ALU.add).then_inc(var_ok, 1)
                stats.n += 1

            def third_stats(b):
                own(nc.vector.bn_stats(st[:, b, :], x[:, b, :]))
                nc.vector.bn_aggr(mv[:, b, :], st[:, b, :]).then_inc(stats_ok, 1)

            def third_low(b):
                dve.wait_ge(pt_hi, ring_at[("rows", b)] + 1)
                src, dst = rows_io(b)
                nc.vector.tensor_tensor(dst[1], src, dst[0], ALU.subtract).then_inc(pt_lo, 1)

            def newton(b0, b1):
                c = slice(b0, b1)
                dve.wait_ge(sdev_ok, stats.n)
                own(nc.vector.tensor_tensor(t1[:, c], ve[:, c], r0[:, c], ALU.mult))
                own(nc.vector.tensor_tensor(t2[:, c], t1[:, c], r0[:, c], ALU.mult))
                own(nc.vector.tensor_scalar(t3[:, c], t2[:, c], -0.5, 1.5, ALU.mult, ALU.add))
                own(nc.vector.tensor_tensor(rstd[:, c], t3[:, c], r0[:, c], ALU.mult))
            stats.n = 0

            def normalise(i):
                u = x_units[i]
                b = 2 * u[1] + u[2]
                if i >= 2:
                    dve.wait_ge(unit_mm, unit_at[x_units[i - 2]] + 1)
                nc.vector.tensor_scalar(xn_tile(i), x[:, b, :], mv[:, b, 0:1], rstd[:, b:b + 1],
                                        ALU.subtract, ALU.mult).then_inc(xn_ok, 1)

            def unit_low(u):
                kind, a, b = u
                i = unit_at[u]
                if kind in ("O", "XO"):
                    dve.wait_ge(unit_mm, i + 1)
                    dve.wait_ge(bias_added, a + 1 + (B if kind == "XO" else 0))
                    nc.vector.tensor_tensor(x[:, a, :], bank[ubank[i]][0:T, :], x[:, a, :], ALU.add).then_inc(unit_out, 1)
                    return
                src, dst, bias = unit_io(u)
                dve.wait_ge(unit_hi, hi_at[u] + 1)
                if bias is None:
                    nc.vector.tensor_tensor(dst[1], src, dst[0], ALU.subtract).then_inc(unit_out, 1)
                else:
                    nc.vector.scalar_tensor_tensor(dst[1], src, bias, dst[0], ALU.add, ALU.subtract).then_inc(unit_out, 1)
                if u in xn_at:
                    nxt = xn_at[u] + 2
                    if nxt < len(x_units) and x_units[nxt][0] == kind and (a == 0) == (kind == "X2"):
                        normalise(nxt)

            def later_units(us):
                for u in us:
                    unit_low(u)
                    if u[0] in ("O", "XO"):
                        dve.wait_ge(unit_out, unit_at[u] + 1)
                    if u[0] == "O":
                        own(nc.vector.bn_stats(st[:, u[1], :], x[:, u[1], :]))
                    if u[0] == "XO":
                        third_stats(u[1])

            def rowmax(n):
                dve.wait_ge(scores_ok, n + 1)
                own(nc.vector.tensor_reduce(mx[:, :], score_ap(n), AX.X, ALU.max))
                if n > 0:
                    dve.wait_ge(exp_ok, n)
                nc.vector.tensor_scalar(nb[:, :], mx[:, :], -SCALE, None, ALU.mult).then_inc(negmax_ok, 1)

            def tail_low(n, chunks):
                for c in chunks:
                    ci = chunk(n, c)
                    kc = T if n < NSELF else KEYS[c]
                    dve.wait_ge(pt_hi, ci + 1)
                    nc.vector.tensor_tensor(PT[1][0:kc, c, :], bank[4 + ci % 2][0:kc, 0:4 * T], PT[0][0:kc, c, :],
                                            ALU.subtract).then_inc(pt_lo, 1)

            def norm_probs(n):
                dve.wait_ge(exp_ok, n + 1)
                own(nc.vector.reciprocal(rr[:, :], rs[:, n % 2, :]))
                width = T if n < NSELF else S
                c0 = probs_col(n)
                for j in range(4):
                    last = nc.vector.tensor_scalar(P[:, j, c0:c0 + width], P[:, j, c0:c0 + width], rr[:, j:j + 1], None, ALU.mult)
                last.then_inc(probs_ok, 1)

            def heads_split(n):
                b = n // NG
                dve.wait_ge(o_out, n + 1)
                if b > 0:
                    prev = ("O", b - 1, 0) if b <= B else ("XO", b - 1 - B, 0)
                    dve.wait_ge(unit_mm, unit_at[prev] + 1)
                own(nc.vector.tensor_copy(oTs[0][:, :, :], oT[:, :, :]))
                nc.vector.tensor_tensor(oTs[1][:, :, :], oT[:, :, :], oTs[0][:, :, :], ALU.subtract).then_inc(o_split, 1)

            def self_low(i):
                dve.wait_ge(split_hi, i + 1)
                raw, halves = whole(i)
                nc.vector.tensor_tensor(halves[1], raw, halves[0], ALU.subtract).then_inc(split_lo, 1)

            dve.wait_ge(x_in[0], 16)
            stats(0, 2)
            newton(0, 2)
            normalise(0)
            normalise(1)
            self_low(0)
            for u in prologue:
                if u == ("QK", 0, 0):
                    dve.wait_ge(bqk_in, 16)
                if u in SPLIT_BEFORE:
                    for i in SPLIT_BEFORE[u]:
                        self_low(i)
                if u == ("V", 0, 0):
                    dve.wait_ge(x_in[1], 16)
                    stats(2, B)
                if u == ("X", 1, 0):
                    newton(2, B)
                    normalise(2)
                    normalise(3)
                    dve.wait_ge(ident_ok, 1)
                    nc.vector.tensor_copy(identr[:, :], ident[0:T, 0:T])
                    nc.vector.tensor_copy(maskr[:, :, :], maskf[:, :, :]).then_inc(consts_ok, 1)
                unit_low(u)
            for i in (6, 7):
                self_low(i)
            nc.vector.memset(zeros[:, :], 0.0).then_inc(zero_made, 1)
            dve.wait_ge(const_in, 16 * 6)
            for first, slots in ((0, self_slots), (NSELF, cross_slots)):
                for s, (ua, ub) in enumerate(slots):
                    n = first + s
                    if s == 0 and first == 0:
                        rowmax(n)
                    if s > 0:
                        tail_low(n - 1, range(nchunks(n - 1))[0:2])
                    if first == 0 and s in SECOND:
                        newton(*SECOND[s])
                        for i in range(2):
                            normalise(B + SECOND[s][0] + i)
                    if s < NSELF and first > 0:
                        rowmax(n)
                    if first > 0 and s == 0:
                        newton(6, 8)
                        normalise(2 * B - 2)
                        normalise(2 * B - 1)
                    if s < NSELF and (first == 0):
                        norm_probs(n)
                        if s + 1 < NSELF:
                            rowmax(n + 1)
                    if s > 0 and nchunks(n - 1) > 2:
                        tail_low(n - 1, [2])
                    for u in ua:
                        unit_low(u)
                    if s < NSELF and not (first == 0):
                        norm_probs(n)
                    if first > 0 and x3_row(s) is not None and s < NSELF:
                        third_low(x3_row(s))
                    if ub_first(n):
                        later_units(ub)
                    if s > 0 and (n - 1) % NG == 3:
                        heads_split(n - 1)
                    if first > 0 and x3_row(s) is not None and s == NSELF:
                        third_low(x3_row(s))
                    if first > 0 and s == 4:
                        dve.wait_ge(gate_in, 64)
                        own(nc.vector.tensor_copy(gwr[0][:, :, :], gw[:, :, :]))
                        nc.vector.tensor_tensor(gwr[1][:, :, :], gw[:, :, :], gwr[0][:, :, :], ALU.subtract).then_inc(route_c, 1)
                    if not ub_first(n):
                        later_units(ub)
                    if first == 0 and s + 1 in SECOND:
                        variance(*SECOND[s + 1])
                if first == 0:
                    for u in boundary:
                        unit_low(u)
                    dve.wait_ge(unit_out, unit_at[boundary[-1]] + 1)
                    own(nc.vector.bn_stats(st[:, B - 1, :], x[:, B - 1, :]))
                    variance(6, 8)
            def keep_rows(b0, b1):
                for b in range(b0, b1):
                    nc.vector.tensor_scalar(xn3[:, b, :], x[:, b, :], mv[:, b, 0:1], rstd[:, b:b + 1],
                                            ALU.subtract, ALU.mult)
            dve.wait_ge(late_xn, B - 1)
            dve.wait_ge(pv_ok, 2 * NSELF)
            unit_low(last_o[0])
            dve.wait_ge(unit_out, unit_at[last_o[0]] + 1)
            stats(B - 1, B)
            newton(B - 1, B)
            nc.vector.tensor_scalar(xn_late[:, (B - 1) % 2, :], x[:, B - 1, :], mv[:, B - 1, 0:1], rstd[:, B - 1:B],
                                    ALU.subtract, ALU.mult).then_inc(xn_ok, 1)
            keep_rows(0, 2)
            third_low(B - 1)
            dve.wait_ge(tri_made, 1)
            nc.vector.tensor_copy(beforer[:, :], trif[:, :])
            nc.vector.tensor_copy(onesr[:, :], onesf[:, :]).then_inc(tri_ok, 1)
            keep_rows(2, 3)

            def wide(ap):
                return ap.unsqueeze(2).to_broadcast([T, B, NE])
            v_ = nc.vector
            iob = iota[:, 0:NE].unsqueeze(1).to_broadcast([T, B, NE])
            dve.wait_ge(router_mm, 1)
            lgp = bank[4][0:T, 0:B * NE].rearrange("p (b e) -> p b e", e=NE)
            own(v_.tensor_reduce(sm["gmx"][:, :], lgp, AX.X, ALU.max))
            v_.tensor_tensor(rt["lg"][:, :, :], lgp, wide(sm["gmx"][:, :]), ALU.subtract).then_inc(logits_ok, 1)
            keep_rows(3, 4)
            dve.wait_ge(gexp, 1)
            own(v_.tensor_reduce(sm["gsm"][:, :], rt["sc"][:, :, :], AX.X, ALU.add))
            own(v_.reciprocal(sm["grc"][:, :], sm["gsm"][:, :]))
            own(v_.tensor_tensor(rt["prob"][:, :, :], rt["sc"][:, :, :], wide(sm["grc"][:, :]), ALU.mult))
            own(v_.tensor_tensor(rt["bi"][:, :, :], rt["prob"][:, :, :],
                                 gbias[:, :].unsqueeze(1).to_broadcast([T, B, NE]), ALU.add))
            for src, top, lt, cand, ix, m in (("bi", "top0", "lt", "cand", "ix0", "m0"),
                                              ("bi2", "top1", "lt2", "cand2", "ix1", "m1")):
                if src == "bi2":
                    own(v_.scalar_tensor_tensor(rt["bi2"][:, :, :], rt["m0"][:, :, :], MASKED, rt["bi"][:, :, :],
                                                ALU.mult, ALU.add))
                own(v_.tensor_reduce(sm[top][:, :], rt[src][:, :, :], AX.X, ALU.max))
                own(v_.tensor_tensor(rt[lt][:, :, :], rt[src][:, :, :], wide(sm[top][:, :]), ALU.is_lt))
                own(v_.scalar_tensor_tensor(rt[cand][:, :, :], rt[lt][:, :, :], float(NE), iob, ALU.mult, ALU.add))
                own(v_.tensor_reduce(sm[ix][:, :], rt[cand][:, :, :], AX.X, ALU.min))
                own(v_.tensor_tensor(rt[m][:, :, :], iob, wide(sm[ix][:, :]), ALU.is_equal))
            v_.tensor_tensor(selr[:, :, :], rt["m0"][:, :, :], rt["m1"][:, :, :], ALU.add).then_inc(sel_ok, 1)
            keep_rows(4, B)
            dve.wait_ge(cum_mm, 1)
            rank = bank[6][0:T, 0:B * NE].rearrange("p (b e) -> p b e", e=NE)
            count = bank[6][0:T, B * NE:(B + 1) * NE]
            own(v_.scalar_tensor_tensor(over[:, :, :], iob, float(NR), wide(count), ALU.mult, ALU.is_lt))
            own(v_.tensor_reduce(sm["ntile"][:, :], over[:, :, :], AX.X, ALU.add))
            own(v_.tensor_tensor(rt["below"][:, :, :], tri[:, :, :], sm["ntile"][:, :].unsqueeze(1).to_broadcast([T, NE, NE]),
                                 ALU.mult))
            own(v_.tensor_reduce(sm["tstart"][:, :], rt["below"][:, :, :], AX.X, ALU.add))
            own(v_.scalar_tensor_tensor(rt["slots"][:, :, :], sm["tstart"][:, :].unsqueeze(1).to_broadcast([T, B, NE]),
                                        float(NR), rank, ALU.mult, ALU.add))
            v_.tensor_tensor(rt["ms0"][:, :, :], rt["m0"][:, :, :], rt["slots"][:, :, :], ALU.mult)
            own(v_.tensor_tensor(rt["ms1"][:, :, :], rt["m1"][:, :, :], rt["slots"][:, :, :], ALU.mult))
            v_.tensor_reduce(sm["s0f"][:, :], rt["ms0"][:, :, :], AX.X, ALU.add)
            own(v_.tensor_reduce(sm["s1f"][:, :], rt["ms1"][:, :, :], AX.X, ALU.add))
            v_.tensor_copy(slot_u[:, 0, :], sm["s0f"][:, :])
            v_.tensor_copy(slot_u[:, 1, :], sm["s1f"][:, :]).then_inc(slots_ok, 1)
            own(v_.tensor_tensor(sm["tend"][:, :], sm["tstart"][:, :], sm["ntile"][:, :], ALU.add))
            own(v_.tensor_tensor(tmap[:, :, :], sm["tend"][0:1, :].unsqueeze(1).to_broadcast([1, NT, NE]),
                                 iota[0:1, :].unsqueeze(2).to_broadcast([1, NT, NE]), ALU.is_le))
            own(v_.tensor_reduce(tmapf[:, :], tmap[:, :, :], AX.X, ALU.add))
            own(v_.tensor_scalar(tmapc[:, :], tmapf[:, :], float(NE - 1), None, ALU.min))
            v_.tensor_copy(tmapi[:, :], tmapc[:, :]).then_inc(tmap_ok, 1)
            v_.tensor_tensor(rt["mw0"][:, :, :], rt["m0"][:, :, :], rt["prob"][:, :, :], ALU.mult)
            own(v_.tensor_tensor(rt["mw1"][:, :, :], rt["m1"][:, :, :], rt["prob"][:, :, :], ALU.mult))
            v_.tensor_reduce(sm["wt0"][:, :], rt["mw0"][:, :, :], AX.X, ALU.add)
            own(v_.tensor_reduce(sm["wt1"][:, :], rt["mw1"][:, :, :], AX.X, ALU.add))

            for c in range(4):
                half, it = divmod(c, 2)
                dve.wait_ge(ssilu, c + 1)
                if c >= 2:
                    dve.wait_ge(sh_hi, c - 1)
                nc.vector.tensor_tensor(hf[:, c % 2, :], bank[2 * (c % 2) + 1][:, 0:4 * T], sg[:, c % 2, :],
                                        ALU.mult).then_inc(sh_ok, 1)
                dve.wait_ge(sh_hi, c + 1)
                span = slice(4 * T * half, 4 * T * (half + 1))
                nc.vector.tensor_tensor(hS[1][:, it, span], hf[:, c % 2, :], hS[0][:, it, span], ALU.subtract).then_inc(sh_lo, 1)
            def w13_low(j, i):
                e = expert(dve, j)
                for h in range(2):
                    k = slice(2 * h, 2 * h + 2)
                    dve.wait_ge(w13_hi, 2 * j + h + 1)
                    nc.vector.tensor_tensor(w13[i][1][:, k, :], raw13_of(e)[:, k, :], w13[i][0][:, k, :],
                                            ALU.subtract).then_inc(w13_lo, 1)

            def w2_high(i, e):
                nc.vector.tensor_scalar(w2[i][0][:, :, :], raw2_of(e), 1.0, None, ALU.mult).then_inc(w2_hi, 1)

            def rows_low(j):
                dve.wait_ge(xt_hi, j + 1)
                nc.vector.tensor_tensor(xgT[1][:, :, :], bank[2][:, :].rearrange("p (k t) -> p k t", k=KD), xgT[0][:, :, :],
                                        ALU.subtract).then_inc(xt_lo, 1)
            dve.wait_ge(tmap_ok, 1)
            dve.wait_ge(raw2_in, 16 * NE)
            w13_low(0, 0)
            def add_shared(b):
                dve.wait_ge(sdn_mm, b + 1)
                nc.vector.tensor_tensor(x[:, b, :], bank[4 + b % 3][0:T, :], x[:, b, :], ALU.add).then_inc(sdn_out, 1)
            for b in range(SHARED_FIRST - 1):
                add_shared(b)
            rows_low(0)
            add_shared(SHARED_FIRST - 1)

            def h_low(j):
                dve.wait_ge(ht_hi, j + 1)
                nc.vector.tensor_tensor(hTt[1][:, :, :], bank[3][:, 0:FI].rearrange("p (k t) -> p k t", k=2),
                                        hTt[0][:, :, :], ALU.subtract).then_inc(ht_lo, 1)

            def step(i, done=2 * NR, last=False):
                for par in range(2):
                    j = 2 * i + par
                    if not (last and par == 1):
                        w13_low(j + 1, 1 - par)
                    if done + par >= 1:
                        h_low(j - 1)
                    e = expert(dve, j)
                    if done + par >= 2:
                        dve.wait_ge(down_mm, j - 1)
                    w2_high(par, e)
                    dve.wait_ge(silu_ok, j + 1)
                    if done + par >= 2:
                        dve.wait_ge(ht_mm, j - 1)
                    nc.vector.tensor_tensor(h_tile[:, par, :], bank[par][:, FI:2 * FI], s_tile[:, par, :], ALU.mult).then_inc(h_ok, 1)
                    if not (last and par == 1):
                        rows_low(j + 1)
            step(0, done=0)
            with dve.Fori(1, NT // 2 - 1) as i:
                step(i)
            step(NT // 2 - 1, last=True)
            h_low(NT - 1)
            for b in range(SHARED_FIRST, B):
                add_shared(b)
            for b in range(B):
                dve.wait_ge(sdn_out, b + 1)
                i = (2 * b) % 8
                dve.wait_ge(gathered[i], 16 * (b // 4 + 1))
                own(nc.vector.scalar_tensor_tensor(x[:, b, :], gath[i][:, :], sm["wt0"][:, b:b + 1], x[:, b, :], ALU.mult, ALU.add))
                dve.wait_ge(gathered[i + 1], 16 * (b // 4 + 1))
                nc.vector.scalar_tensor_tensor(x[:, b, :], gath[i + 1][:, :], sm["wt1"][:, b:b + 1], x[:, b, :],
                                               ALU.mult, ALU.add).then_inc(added, 1)

        @block.tensor
        def _(pe):
            def product(out, lhs, rhs, first=True, last=True):
                for t in range(product.tiles):
                    for i, (s, m) in enumerate(PASSES):
                        ins = nc.tensor.matmul(out, lhs(s, t), rhs(m, t), start=first and t == 0 and i == 0,
                                               stop=last and t == product.tiles - 1 and i == 2)
                return ins
            product.tiles = KD

            def unit(u):
                kind, a, b = u
                i = unit_at[u]
                bk = bank[ubank[i]]
                if prev_user[i] is not None:
                    pe.wait_ge(unit_out, prev_user[i] + 1)
                if kind == "K" and i > second_slot:
                    pe.wait_ge(o_out, NSELF + NG * (a - 1) + b - 1)
                if kind in ("X", "X2"):
                    pe.wait_ge(xn_ok, xn_at[u] + 1)
                    if xn_at[u] == 0:
                        pe.wait_ge(ident_ok, 1)
                    for t in range(KD):
                        last = nc.tensor.transpose(bk[:, T * t:T * (t + 1)],
                                                   xn_tile(xn_at[u])[:, 128 * t:128 * (t + 1)],
                                                   ident[0:T, 0:T])
                elif kind == "QK":
                    pe.wait_ge(unit_out, unit_at[("X", a, 1)] + 1)
                    pe.wait_ge(split_lo, b // 2 + 1)
                    last = product(bk[:, 0:2 * T], lambda h, t: wqk[h][:, b, t, :], lambda h, t: xnT[h][:, t, :])
                elif kind == "V":
                    pe.wait_ge(unit_out, unit_at[("X", a, 1)] + 1)
                    pe.wait_ge(split_lo, 6)
                    last = product(bk[0:T, :], lambda h, t: xnT[h][:, t, T * b:T * (b + 1)], lambda h, t: wv[h][:, t, :])
                elif kind in ("O", "XO"):
                    w = wout if kind == "O" else xwo
                    pe.wait_ge(o_split, a + 1 + (B if kind == "XO" else 0))
                    if kind == "O":
                        pe.wait_ge(split_lo, 8)
                    else:
                        pe.wait_ge(late_split, piece_at[("wo", 1)] + 1)
                    last = product(bk[0:T, :], lambda h, t: oTs[h][:, t, :], lambda h, t: w[h][:, t, :])
                elif kind == "Q":
                    pe.wait_ge(unit_out, unit_at[("X2", a, 1)] + 1)
                    pe.wait_ge(late_split, piece_at[("wq", b // 2)] + 1)
                    last = product(bk[:, 0:2 * T], lambda h, t: xwq[h][:, b, t, :], lambda h, t: xnT[h][:, t, :])
                elif kind == "K":
                    pe.wait_ge(late_split, max(piece_at[("cx", a, 1)], piece_at[("wk", 1)]) + 1)
                    last = product(bk[:, 0:SP], lambda h, t: xwk[h][:, b, t, :], lambda h, t: cx[a % 2][h][:, t, :])
                elif kind == "XV":
                    pe.wait_ge(late_split, max(piece_at[("cx", a, 1)], piece_at[("wv", 1)]) + 1)
                    last = product(bk[0:KEYS[b], :], lambda h, t: cx[a % 2][h][:, t, 128 * b:128 * b + KEYS[b]],
                                   lambda h, t: xwv[h][:, t, :])
                last.then_inc(unit_mm, 1)

            def scores(n):
                if n < NSELF:
                    p, i = divmod(n // NG, 2)
                    g = n % NG
                    pe.wait_ge(packed[p % 2], 16 * 6 * (p // 2 + 1))
                    if n >= 2:
                        pe.wait_ge(exp_ok, n - 1)
                    if n == 0:
                        pe.wait_ge(consts_ok, 1)
                    out = bank[n % 2][0:T, 0:4 * T].rearrange("p (j t) -> p j t", j=4)
                    nc.tensor.matmul(bank[n % 2][0:T, 0:4 * T], identr[:, :], maskr[:, :, :].rearrange("p j t -> p (j t)"),
                                     start=True, stop=False)
                    for j in range(4):
                        last = nc.tensor.matmul(out[:, j, :], pq[p % 2][:, j, g, T * i:T * (i + 1)],
                                                pk[p % 2][:, j, g, T * i:T * (i + 1)], start=False, stop=j == 3)
                else:
                    b, g = divmod(n - NSELF, NG)
                    pe.wait_ge(q_loaded[b % 2], 16 * 3 * (b // 2 + 1))
                    pe.wait_ge(kpacked[g // 2], 16 * 3 * (b + 1))
                    pe.wait_ge(exp_ok, n)
                    if n == NSELF:
                        pe.wait_ge(unit_out, first_cross)
                    for j in range(4):
                        last = nc.tensor.matmul(bank[j][0:T, 0:SP], qp[:, b % 2, j, g, :], kp[:, j, g, :], start=True, stop=True)
                last.then_inc(scores_ok, 1)

            def transposes(n, chunks):
                for c in chunks:
                    ci = chunk(n, c)
                    kc = T if n < NSELF else KEYS[c]
                    pe.wait_ge(probs_ok, n + 1)
                    if n == NSELF:
                        pe.wait_ge(unit_out, second_slot)
                    if ci >= 2:
                        pe.wait_ge(pt_lo, ci - 1)
                    for j in range(4):
                        last = nc.tensor.transpose(bank[4 + ci % 2][0:kc, T * j:T * (j + 1)], P[:, j, probs_col(n) + 128 * c:probs_col(n) + 128 * c + kc],
                                                   ident[0:T, 0:T])
                    last.then_inc(tp_ok, 1)

            def third_rows(b):
                i = ring_at[("rows", b)]
                if b < B - 1:
                    pe.wait_ge(late_xn, b + 1)
                else:
                    pe.wait_ge(xn_ok, 2 * B + 1)
                pe.wait_ge(pt_lo, i - 1)
                for t in range(KD):
                    last = nc.tensor.transpose(bank[4 + i % 2][:, T * t:T * (t + 1)],
                                               xn_late[:, b % 2, 128 * t:128 * (t + 1)], ident[0:T, 0:T])
                last.then_inc(tp_ok, 1)

            def values(n):
                if n >= NSELF:
                    k = min(n + 1 - NSELF + NG, NG * B - 1)
                    if k != NG:
                        pe.wait_ge(unit_out, unit_at[("K", k // NG, k % NG)] + 1)
                if n > 0:
                    pe.wait_ge(o_out, n)
                g = n % NG
                buf, c0 = vslot(n)
                steps = [(c, s, m) for c in range(nchunks(n)) for s, m in PASSES]
                for i, (c, s, m) in enumerate(steps):
                    kc = T if n < NSELF else KEYS[c]
                    if i % 3 == 0:
                        pe.wait_ge(pt_lo, chunk(n, c) + 1)
                    last = nc.tensor.matmul(heads_bank(n)[:, 0:4 * T], v[s][0:kc, buf, c0 + c, 128 * g:128 * (g + 1)],
                                            PT[m][0:kc, c, :], start=i == 0, stop=i == len(steps) - 1)
                last.then_inc(pv_ok, 1)

            def v_ready(n):
                if n < NSELF:
                    b = n // NG
                    pe.wait_ge(unit_out, unit_at[("V", b // 2, b % 2)] + 1)
                else:
                    pe.wait_ge(unit_out, unit_at[("XV", (n - NSELF) // NG, 2)] + 1)

            def shared_up_half(c, w):
                half, it = divmod(c, 2)
                return product(bank[2 * (c % 2) + w][:, 0:4 * T],
                               lambda h, t: sw13[h][:, t, w, 128 * it:128 * (it + 1)],
                               lambda h, t: fx[h][:, t, 4 * T * half:4 * T * (half + 1)])

            for u in prologue:
                unit(u)
            for first, slots in ((0, self_slots), (NSELF, cross_slots)):
                for s, (ua, ub) in enumerate(slots):
                    n = first + s
                    if s < NSELF and (first > 0 or s == 0):
                        scores(n)
                    if s > 0:
                        transposes(n - 1, range(nchunks(n - 1))[0:2])
                    if n == 2 * NSELF:
                        pe.wait_ge(exp_ok, 2 * NSELF)
                        pe.wait_ge(s_lo, KD)
                        pe.wait_ge(pt_lo, ring_at[("rows", 3)] + 1)
                        shared_up_half(0, 0)
                    if first == 0 and s + 1 < NSELF:
                        scores(n + 1)
                    for u in ua:
                        unit(u)
                    if s > 0 and nchunks(n - 1) > 2:
                        transposes(n - 1, [2])
                    if first > 0 and x3_row(s) is not None and s < NSELF:
                        third_rows(x3_row(s))
                    if first > 0 and s > 0:
                        for u in ub:
                            unit(u)
                    if s > 0:
                        if (n - 1) % NG == 0:
                            v_ready(n - 1)
                        values(n - 1)
                    if n == 2 * NSELF:
                        shared_up_half(0, 1).then_inc(sup_mm, 1)
                    if first > 0 and x3_row(s) is not None and s == NSELF:
                        third_rows(x3_row(s))
                    if first == 0 or s == 0:
                        for u in ub:
                            unit(u)
                if first == 0:
                    for u in boundary:
                        unit(u)

            for u in last_o:
                unit(u)

            pe.wait_ge(route_c, 1)
            pe.wait_ge(pt_lo, ring_at[("rows", B - 2)] + 1)
            for out, c0, c1 in ((bank[2], 0, 4), (bank[3], 4, 7)):
                last = product(out[0:NE, 0:T * (c1 - c0)], lambda h, t: gwr[h][:, t, :],
                               lambda h, t: fx[h][:, t, T * c0:T * c1])
            last.then_inc(gate_mm, 1)

            def shared_up(c):
                pe.wait_ge(sh_ok, c - 1)
                for w in range(2):
                    last = shared_up_half(c, w)
                last.then_inc(sup_mm, 1)

            third_rows(B - 1)
            pe.wait_ge(gate_out, 1)
            for b in range(B - 1):
                nc.tensor.transpose(bank[4][0:T, NE * b:NE * (b + 1)], lgT[:, T * b:T * (b + 1)], ident[0:NE, 0:NE])
            pe.wait_ge(pt_lo, len(ring))
            product(bank[4][0:T, NE * (B - 1):NE * B], lambda h, t: fx[h][:, t, T * (B - 1):T * B],
                    lambda h, t: gwr[h][:, t, :]).then_inc(router_mm, 1)

            shared_up_half(1, 0)
            pe.wait_ge(sel_ok, 1)
            pe.wait_ge(tri_ok, 1)
            nc.tensor.matmul(bank[6][:, 0:B * NE], beforer[:, :], selr[:, :, :].rearrange("p b e -> p (b e)"),
                             start=True, stop=False)
            for d in range(1, B):
                nc.tensor.matmul(bank[6][:, NE * d:NE * B], onesr[:, :], selr[:, 0:B - d, :].rearrange("p b e -> p (b e)"),
                                 start=False, stop=d == B - 1)
            for b in range(B):
                last = nc.tensor.matmul(bank[6][:, NE * B:NE * (B + 1)], onesr[:, :], selr[:, b, :],
                                        start=b == 0, stop=b == B - 1)
            last.then_inc(cum_mm, 1)
            shared_up_half(1, 1).then_inc(sup_mm, 1)
            for c in range(2, 4):
                shared_up(c)
            pe.wait_ge(s_lo, KD + 1)
            pe.wait_ge(sh_lo, 4)
            pe.wait_ge(slots_ok, 1)

            def shared_down(b):
                if b >= 3:
                    pe.wait_ge(sdn_out, b - 2)
                product.tiles = 2
                product(bank[4 + b % 3][0:T, :], lambda h, t: hS[h][:, t, T * b:T * (b + 1)],
                        lambda h, t: sw2[h][:, t, :]).then_inc(sdn_mm, 1)
                product.tiles = KD
            for b in range(SHARED_FIRST - 1):
                shared_down(b)

            def rows(j, i, turn, first=False):
                pe.wait_ge(xg_in[i], 16 * turn)
                if not first:
                    pe.wait_ge(xt_lo, j)
                for t in range(KD):
                    last = nc.tensor.transpose(bank[2][:, 128 * t:128 * (t + 1)], xg[:, i, 128 * t:128 * (t + 1)], ident[:, :])
                last.then_inc(xt_mm, 1)
            rows(0, 0, 1, first=True)
            shared_down(SHARED_FIRST - 1)

            def down(j, i):
                pe.wait_ge(ht_lo, j + 1)
                pe.wait_ge(w2_lo, j + 1)
                product.tiles = 2
                product(bank[4 + i][:, :], lambda h, t: hTt[h][:, t, :], lambda h, t: w2[i][h][:, t, :]).then_inc(down_mm, 1)
                product.tiles = KD

            def step(i, first=False, second=False, last=False):
                for par in range(2):
                    j = 2 * i + par
                    pe.wait_ge(xt_lo, j + 1)
                    if not first:
                        pe.wait_ge(h_ok, j - 1)
                    product.tiles = 2
                    for k in range(2):
                        pe.wait_ge(w13_lo, 2 * j + k + 1)
                        up = product(bank[par][:, :], lambda h, t: xgT[h][:, 2 * k + t, :],
                                     lambda h, t: w13[par][h][:, 2 * k + t, :], first=k == 0, last=k == 1)
                    up.then_inc(up_mm, 1)
                    product.tiles = KD
                    if not (last and par == 1):
                        rows(j + 1, 1 - par, i + 1 + par)
                    if not (first and par == 0):
                        if not (first or (second and par == 0)):
                            pe.wait_ge(y_out, j - 2)
                        if first:
                            pe.wait_ge(sdn_out, SHARED_FIRST)
                        down(j - 1, 1 - par)
                    pe.wait_ge(h_ok, j + 1)
                    if not (first and par == 0):
                        pe.wait_ge(ht_lo, j)
                    for t in range(2):
                        last_t = nc.tensor.transpose(bank[3][:, 128 * t:128 * (t + 1)], h_tile[:, par, 128 * t:128 * (t + 1)], ident[:, :])
                    last_t.then_inc(ht_mm, 1)
            step(0, first=True)
            step(1, second=True)
            with pe.Fori(2, NT // 2 - 1) as i:
                step(i)
            step(NT // 2 - 1, last=True)
            down(NT - 1, 1)
            pe.wait_ge(y_out, NT)
            for b in range(SHARED_FIRST, B):
                shared_down(b)


def kernel(**inputs):
    import numpy as np
    import concourse.bacc as bacc
    from concourse.bass_utils import run_bass_kernel_spmd

    g = {k: np.asarray(a) for k, a in inputs.items()}

    def by_tile(w):
        n, m = w.shape
        return w.reshape(n // 128, 128, m // 128, 128).transpose(3, 0, 2, 1).reshape(128, -1)

    def by_row(w):
        n, m = w.shape
        return w.T.reshape(m // 128, 128, n).transpose(1, 0, 2).reshape(128, -1)

    def column(b):
        return b.reshape(-1, 128).T

    wqkv, bqkv = g["L0_attn_w_qkv"], g["L0_attn_b_qkv"]
    c = g["ctx_2048"].transpose(0, 2, 1)
    c = np.concatenate([c, np.zeros(c.shape[:2] + (1,), c.dtype)], axis=2)
    c = c.reshape(8, 4, 128, 362).transpose(0, 2, 1, 3).reshape(8, 128, -1)
    w1 = np.concatenate([g["L0_ffn_W1"], g["L0_ffn_Ws1"][None]])
    w3 = np.concatenate([g["L0_ffn_W3"], g["L0_ffn_Ws3"][None]])
    w2 = np.concatenate([g["L0_ffn_W2"], g["L0_ffn_Ws2"][None]])
    w13 = np.stack([w1, w3], axis=1)
    w13 = w13.reshape(9, 2, 256, 4, 128).transpose(0, 4, 3, 1, 2).reshape(9, 128, -1)
    w2 = np.stack([by_row(w) for w in w2])
    arrays = {
        "x": g["x"], "ctx": c, "wqk": by_tile(wqkv[:1024]), "wv": by_row(wqkv[1024:]),
        "wout": by_row(g["L0_attn_w_out"]), "bqk": column(bqkv[:1024]), "bv": column(bqkv[1024:]),
        "bout": g["L0_attn_b_out"][None], "xwq": by_tile(g["L0_xattn_Wq"]), "xwk": by_tile(g["L0_xattn_Wk"]),
        "xwv": by_row(g["L0_xattn_Wv"]), "xwo": by_row(g["L0_xattn_Wo"]), "xbq": column(g["L0_xattn_bq"]),
        "xbk": column(g["L0_xattn_bk"]), "xbv": column(g["L0_xattn_bv"]), "xbo": g["L0_xattn_bo"][None],
        "gw": by_row(g["L0_ffn_gate_w"]), "gb": g["L0_ffn_gate_b"][None],
        "iota": np.arange(20, dtype=np.float32)[None],
        "tri": np.tril(np.ones((8, 8), np.float32), -1).reshape(1, -1), "w13": w13, "w2": w2,
    }
    arrays = {f"in_{k}": np.ascontiguousarray(a) for k, a in arrays.items()}
    nc = bacc.Bacc("TRN2", target_bir_lowering=False, num_devices=1, dynamic_dma_scratch_size=4096)
    args = [nc.dram_tensor(k, a.shape, mybir.dt.from_np(a.dtype), kind="ExternalInput").ap() for k, a in arrays.items()]
    out = nc.dram_tensor("out_x", (8, 100, 512), mybir.dt.float32, kind="ExternalOutput").ap()
    decoder_layer(nc, *args, out)
    r = run_bass_kernel_spmd(nc, [arrays], core_ids=[0])
    return r.results[0]["out_x"]
```
